# Optimizing a Trainium2 kernel written in Bass

```python
import numpy as np
import jax
import jax.numpy as jnp

def _softmax(x, axis=-1):
    return jax.nn.softmax(x, axis=axis)

def _gelu(x):
    return jax.nn.gelu(x, approximate=True)

def _silu(x):
    return jax.nn.silu(x)

def _sigmoid(x):
    return jax.nn.sigmoid(x)

def _layernorm(x, axis=-1, eps=1e-05):
    m = jnp.mean(x, axis=axis, keepdims=True)
    v = jnp.var(x, axis=axis, keepdims=True)
    return (x - m) / jnp.sqrt(v + eps)

def _scatter_add(tgt, idx, src, axis=0):
    return tgt.at[idx].add(src)

def _segment_sum(src, seg, n):
    return jax.ops.segment_sum(src, seg, n)
kernel_name = 'mk_prb_d2_jaxref_r8_e4f409'

def setup_inputs(seed: int=0):
    np.random.seed(seed)
    _w = jnp.asarray

    def _L0_attn_setup():
        import jax, jax.numpy as jnp
        import numpy as np
        D_MODEL = 128
        N_HEADS = 16
        HEAD_DIM = D_MODEL // N_HEADS
        D_LATENT = 32
        LAMBDA_DECAY = 0.01
        TIME_STEP = 0.01
        CLAMP = 10000.0

        def _reference_tuple_inner(x, Wq, Wk, Wv, Wo, W_down_kv, W_up_k, W_up_v):
            B, S, _ = x.shape
            q = x @ Wq
            k = x @ Wk
            v = x @ Wv
            latent_kv = (k + v) @ W_down_kv
            k_rec = latent_kv @ W_up_k
            v_rec = latent_kv @ W_up_v

            def heads(t):
                return t.reshape(B, S, N_HEADS, HEAD_DIM).transpose(0, 2, 1, 3)
            qh, kh, vh = (heads(q), heads(k_rec), heads(v_rec))
            scale = 1.0 / (jnp.sqrt(jnp.float32(D_MODEL)) + 1e-08)
            scores = jnp.einsum('bhqd,bhkd->bhqk', qh, kh) * scale
            scores = jnp.clip(jnp.nan_to_num(scores, nan=-1000000000.0), -CLAMP, CLAMP)
            idx = jnp.arange(S, dtype=jnp.float32)
            decay = jnp.exp(-LAMBDA_DECAY * TIME_STEP * jnp.abs(idx[:, None] - idx[None, :]))
            scores = scores * decay[None, None, :, :]
            scores = jnp.clip(jnp.nan_to_num(scores, nan=-1000000000.0), -CLAMP, CLAMP)
            attn = jax.nn.softmax(scores, axis=-1)
            out = jnp.einsum('bhqk,bhkd->bhqd', attn, vh)
            out = out.transpose(0, 2, 1, 3).reshape(B, S, D_MODEL)
            return (out @ Wo, latent_kv)
        key = jax.random.key(seed)
        ks = jax.random.split(key, 8)
        B, S = (2, 256)

        def w(k, i, o):
            return jax.random.normal(k, (i, o), dtype=jnp.float32) * 0.02
        return {'x': jax.random.normal(ks[0], (B, S, D_MODEL), dtype=jnp.float32), 'Wq': w(ks[1], D_MODEL, D_MODEL), 'Wk': w(ks[2], D_MODEL, D_MODEL), 'Wv': w(ks[3], D_MODEL, D_MODEL), 'Wo': w(ks[4], D_MODEL, D_MODEL), 'W_down_kv': w(ks[5], D_MODEL, D_LATENT), 'W_up_k': w(ks[6], D_LATENT, D_MODEL), 'W_up_v': w(ks[7], D_LATENT, D_MODEL)}
    _L0_attn_in = _L0_attn_setup()

    def _L0_ffn_setup():
        import jax, jax.numpy as jnp
        import numpy as np
        import math
        B, S, D = (2, 256, 128)
        H = 16
        HD = D // H
        FFN = 256
        E = 8
        TOP_K = 2
        CAP_FACTOR = 1.25
        EPS = 1e-06
        BASE = 10000.0
        CAP = max(math.ceil(B * S * TOP_K * CAP_FACTOR / E), 1)

        def _rmsnorm(x, w):
            rms = jax.lax.rsqrt(jnp.mean(x * x, axis=-1, keepdims=True) + EPS)
            return w * x * rms

        def _rope(x, cos, sin):
            xr = x[..., 0::2]
            xi = x[..., 1::2]
            c = cos[None, None]
            s_ = sin[None, None]
            out_r = xr * c - xi * s_
            out_i = xr * s_ + xi * c
            return jnp.stack([out_r, out_i], axis=-1).reshape(x.shape)

        def _mha(x, w_qkv, w_o):
            b, s, d = x.shape
            qkv = x @ w_qkv
            q, k, v = jnp.split(qkv, 3, axis=-1)
            to_heads = lambda z: z.reshape(b, s, H, HD).transpose(0, 2, 1, 3)
            q, k, v = (to_heads(q), to_heads(k), to_heads(v))
            theta = BASE ** (-2.0 * (jnp.arange(HD // 2, dtype=jnp.float32) / HD))
            freqs = jnp.arange(s, dtype=jnp.float32)[:, None] * theta[None, :]
            cos, sin = (jnp.cos(freqs), jnp.sin(freqs))
            q = _rope(q, cos, sin)
            k = _rope(k, cos, sin)
            scores = jnp.einsum('bhqd,bhkd->bhqk', q, k) / jnp.sqrt(jnp.float32(HD))
            causal = jnp.tril(jnp.ones((s, s), dtype=bool))
            scores = jnp.where(causal, scores, -jnp.inf)
            attn = jax.nn.softmax(scores, axis=-1)
            y = jnp.einsum('bhqk,bhkd->bhqd', attn, v)
            y = y.transpose(0, 2, 1, 3).reshape(b, s, d)
            return y @ w_o

        def _moe(x, w_router, w1, w2):
            b, s, d = x.shape
            t = b * s
            xf = x.reshape(t, d)
            logits = xf.astype(jnp.float32) @ w_router.astype(jnp.float32)
            probs = jax.nn.softmax(logits, axis=-1)
            g, eidx = jax.lax.top_k(probs, TOP_K)
            fg = g.reshape(t * TOP_K)
            fe = eidx.reshape(t * TOP_K)
            tok_of = jnp.arange(t * TOP_K) // TOP_K
            masked = jnp.where(fe[None, :] == jnp.arange(E)[:, None], fg[None, :], -jnp.inf)
            vals, idx = jax.lax.top_k(masked, CAP)
            valid = jnp.isfinite(vals)
            gates = jnp.where(valid, vals, 0.0)
            tok = tok_of[idx]
            xe = xf[tok]
            h = jax.nn.relu(jnp.einsum('ecd,edf->ecf', xe, w1))
            ye = jnp.einsum('ecf,efd->ecd', h, w2) * gates[..., None]
            y = jnp.zeros_like(xf).at[tok.reshape(-1)].add(ye.reshape(-1, d))
            return y.reshape(b, s, d)
        key = jax.random.key(seed)
        ks = jax.random.split(key, 6)
        sd = 0.02
        return {'x': jax.random.normal(ks[0], (B, S, D), jnp.float32), 'g1': jnp.ones((D,), jnp.float32), 'w_qkv': jax.random.normal(ks[1], (D, 3 * D), jnp.float32) * sd, 'w_o': jax.random.normal(ks[2], (D, D), jnp.float32) * sd, 'g2': jnp.ones((D,), jnp.float32), 'w_router': jax.random.normal(ks[3], (D, E), jnp.float32) * sd, 'w1': jax.random.normal(ks[4], (E, D, FFN), jnp.float32) * sd, 'w2': jax.random.normal(ks[5], (E, FFN, D), jnp.float32) * sd}
    _L0_ffn_in = _L0_ffn_setup()

    def _L1_attn_setup():
        import jax, jax.numpy as jnp
        import numpy as np
        HEADS = 16
        DIM_HEAD = 64
        SEG = 32
        SCALE = DIM_HEAD ** (-0.5)
        INNER = HEADS * DIM_HEAD

        def elu1(x):
            return jax.nn.elu(x) + 1.0

        def rope(t, pos):
            d = t.shape[-1]
            freqs = 10000.0 ** (-jnp.arange(0, d, 2, dtype=jnp.float32) / d)
            ang = pos[:, None] * freqs
            cos = jnp.repeat(jnp.cos(ang), 2, axis=-1)
            sin = jnp.repeat(jnp.sin(ang), 2, axis=-1)
            t2 = t.reshape(t.shape[:-1] + (d // 2, 2))
            rot = jnp.stack((-t2[..., 1], t2[..., 0]), axis=-1).reshape(t.shape)
            return t * cos + rot * sin

        def _reference_tuple_inner(x, w_qkv, w_out, ln_g, ln_b, mem_beta):
            B, N, D = x.shape
            mu = x.mean(-1, keepdims=True)
            var = x.var(-1, keepdims=True)
            xn = (x - mu) / jnp.sqrt(var + 1e-05) * ln_g + ln_b
            qkv = xn @ w_qkv
            q, k, v = jnp.split(qkv, 3, axis=-1)

            def to_heads(t):
                return t.reshape(B, N, HEADS, DIM_HEAD).transpose(0, 2, 1, 3)
            q, k, v = map(to_heads, (q, k, v))
            next_k, next_v = (k, v)
            pos = jnp.arange(N, dtype=jnp.float32)
            qr, kr = (rope(q, pos), rope(k, pos))
            W = N // SEG

            def to_segs(t):
                return t.reshape(B, HEADS, W, SEG, DIM_HEAD).transpose(2, 0, 1, 3, 4)
            qs, ks, vs, qnope, knope = map(to_segs, (qr, kr, v, q, k))
            mask = jnp.tril(jnp.ones((SEG, SEG), bool))
            beta = jax.nn.sigmoid(mem_beta)
            mem0 = jnp.zeros((B, HEADS, DIM_HEAD, DIM_HEAD), x.dtype)
            z0 = jnp.full((B, HEADS, DIM_HEAD), 1e-06, x.dtype)

            def step(carry, inp):
                mem, z = carry
                q_s, k_s, v_s, qn_s, kn_s = inp
                scores = jnp.einsum('bhnd,bhmd->bhnm', q_s, k_s) * SCALE
                scores = jnp.where(mask, scores, -jnp.inf)
                sdpa = jnp.einsum('bhnm,bhmd->bhnd', jax.nn.softmax(scores, axis=-1), v_s)
                sq = elu1(qn_s)
                num = jnp.einsum('bhnk,bhkv->bhnv', sq, mem)
                den = jnp.einsum('bhnk,bhk->bhn', sq, z)[..., None]
                mem_out = num / (den + 1e-06)
                out = beta * mem_out + (1.0 - beta) * sdpa
                sk = elu1(kn_s)
                prev_v = jnp.einsum('bhnk,bhkv->bhnv', sk, mem) / jnp.einsum('bhnk,bhk->bhn', sk, z)[..., None]
                mem = mem + jnp.einsum('bhnk,bhnv->bhkv', sk, v_s - prev_v)
                z = z + sk.sum(axis=2)
                return ((mem, z), out)
            _, outs = jax.lax.scan(step, (mem0, z0), (qs, ks, vs, qnope, knope))
            o = outs.transpose(1, 0, 3, 2, 4).reshape(B, N, INNER)
            out = o @ w_out
            return (out, next_k, next_v)
        key = jax.random.key(seed)
        k1, k2, k3 = jax.random.split(key, 3)
        B, N, D = (4, 512, 128)
        x = jax.random.normal(k1, (B, N, D), dtype=jnp.float32)
        w_qkv = jax.random.normal(k2, (D, 3 * INNER), dtype=jnp.float32) * 0.02
        w_out = jax.random.normal(k3, (INNER, D), dtype=jnp.float32) * 0.02
        ln_g = jnp.ones((D,), jnp.float32)
        ln_b = jnp.zeros((D,), jnp.float32)
        mem_beta = jnp.zeros((1, HEADS, 1, 1), jnp.float32)
        return {'x': x, 'w_qkv': w_qkv, 'w_out': w_out, 'ln_g': ln_g, 'ln_b': ln_b, 'mem_beta': mem_beta}
    _L1_attn_in = _L1_attn_setup()

    def _L1_ffn_setup():
        import jax, jax.numpy as jnp
        import numpy as np
        FP8_E4M3_MAX = 448.0

        def fake_quant_fp8(t):
            amax = jnp.max(jnp.abs(t))
            scale = FP8_E4M3_MAX / jnp.maximum(amax, 1e-12)
            q = (t * scale).astype(jnp.float8_e4m3fn).astype(jnp.float32)
            return q / scale
        key = jax.random.key(seed)
        k1, k2, k3 = jax.random.split(key, 3)
        d_in, d_out = (128, 128)
        x = jax.random.normal(k1, (4, 1024, d_in), dtype=jnp.float32)
        weight = jax.random.normal(k2, (d_out, d_in), dtype=jnp.float32) * (1.0 / np.sqrt(d_in))
        bias = jax.random.normal(k3, (d_out,), dtype=jnp.float32) * 0.01
        return {'x': x, 'weight': weight, 'bias': bias}
    _L1_ffn_in = _L1_ffn_setup()
    _d = {'L0_attn_x': _L0_attn_in['x'], 'L0_attn_Wq': _L0_attn_in['Wq'], 'L0_attn_Wk': _L0_attn_in['Wk'], 'L0_attn_Wv': _L0_attn_in['Wv'], 'L0_attn_Wo': _L0_attn_in['Wo'], 'L0_attn_W_down_kv': _L0_attn_in['W_down_kv'], 'L0_attn_W_up_k': _L0_attn_in['W_up_k'], 'L0_attn_W_up_v': _L0_attn_in['W_up_v'], 'L0_ffn_g1': _L0_ffn_in['g1'], 'L0_ffn_w_qkv': _L0_ffn_in['w_qkv'], 'L0_ffn_w_o': _L0_ffn_in['w_o'], 'L0_ffn_g2': _L0_ffn_in['g2'], 'L0_ffn_w_router': _L0_ffn_in['w_router'], 'L0_ffn_w1': _L0_ffn_in['w1'], 'L0_ffn_w2': _L0_ffn_in['w2'], 'L1_attn_w_qkv': _L1_attn_in['w_qkv'], 'L1_attn_w_out': _L1_attn_in['w_out'], 'L1_attn_ln_g': _L1_attn_in['ln_g'], 'L1_attn_ln_b': _L1_attn_in['ln_b'], 'L1_attn_mem_beta': _L1_attn_in['mem_beta'], 'L1_ffn_weight': _L1_ffn_in['weight'], 'L1_ffn_bias': _L1_ffn_in['bias']}
    _x0 = _d['L0_attn_x']
    _d['L0_attn_x'] = jax.random.normal(jax.random.fold_in(jax.random.key(seed), 1), (16, 512, 128), dtype=_x0.dtype)
    del _x0
    return _d

def reference(L0_attn_x, L0_attn_Wq, L0_attn_Wk, L0_attn_Wv, L0_attn_Wo, L0_attn_W_down_kv, L0_attn_W_up_k, L0_attn_W_up_v, L0_ffn_g1, L0_ffn_w_qkv, L0_ffn_w_o, L0_ffn_g2, L0_ffn_w_router, L0_ffn_w1, L0_ffn_w2, L1_attn_w_qkv, L1_attn_w_out, L1_attn_ln_g, L1_attn_ln_b, L1_attn_mem_beta, L1_ffn_weight, L1_ffn_bias):

    def _L0_attn_ref(x, Wq, Wk, Wv, Wo, W_down_kv, W_up_k, W_up_v):
        import jax, jax.numpy as jnp
        import numpy as np
        D_MODEL = 128
        N_HEADS = 16
        HEAD_DIM = D_MODEL // N_HEADS
        D_LATENT = 32
        LAMBDA_DECAY = 0.01
        TIME_STEP = 0.01
        CLAMP = 10000.0

        def _reference_tuple_inner(x, Wq, Wk, Wv, Wo, W_down_kv, W_up_k, W_up_v):
            B, S, _ = x.shape
            q = x @ Wq
            k = x @ Wk
            v = x @ Wv
            latent_kv = (k + v) @ W_down_kv
            k_rec = latent_kv @ W_up_k
            v_rec = latent_kv @ W_up_v

            def heads(t):
                return t.reshape(B, S, N_HEADS, HEAD_DIM).transpose(0, 2, 1, 3)
            qh, kh, vh = (heads(q), heads(k_rec), heads(v_rec))
            scale = 1.0 / (jnp.sqrt(jnp.float32(D_MODEL)) + 1e-08)
            scores = jnp.einsum('bhqd,bhkd->bhqk', qh, kh) * scale
            scores = jnp.clip(jnp.nan_to_num(scores, nan=-1000000000.0), -CLAMP, CLAMP)
            idx = jnp.arange(S, dtype=jnp.float32)
            decay = jnp.exp(-LAMBDA_DECAY * TIME_STEP * jnp.abs(idx[:, None] - idx[None, :]))
            scores = scores * decay[None, None, :, :]
            scores = jnp.clip(jnp.nan_to_num(scores, nan=-1000000000.0), -CLAMP, CLAMP)
            attn = jax.nn.softmax(scores, axis=-1)
            out = jnp.einsum('bhqk,bhkd->bhqd', attn, vh)
            out = out.transpose(0, 2, 1, 3).reshape(B, S, D_MODEL)
            return (out @ Wo, latent_kv)
        return _reference_tuple_inner(x, Wq, Wk, Wv, Wo, W_down_kv, W_up_k, W_up_v)[0]

    def _L0_ffn_ref(x, g1, w_qkv, w_o, g2, w_router, w1, w2):
        import jax, jax.numpy as jnp
        import numpy as np
        import math
        B, S, D = (2, 256, 128)
        H = 16
        HD = D // H
        FFN = 256
        E = 8
        TOP_K = 2
        CAP_FACTOR = 1.25
        EPS = 1e-06
        BASE = 10000.0
        CAP = max(math.ceil(B * S * TOP_K * CAP_FACTOR / E), 1)

        def _rmsnorm(x, w):
            rms = jax.lax.rsqrt(jnp.mean(x * x, axis=-1, keepdims=True) + EPS)
            return w * x * rms

        def _rope(x, cos, sin):
            xr = x[..., 0::2]
            xi = x[..., 1::2]
            c = cos[None, None]
            s_ = sin[None, None]
            out_r = xr * c - xi * s_
            out_i = xr * s_ + xi * c
            return jnp.stack([out_r, out_i], axis=-1).reshape(x.shape)

        def _mha(x, w_qkv, w_o):
            b, s, d = x.shape
            qkv = x @ w_qkv
            q, k, v = jnp.split(qkv, 3, axis=-1)
            to_heads = lambda z: z.reshape(b, s, H, HD).transpose(0, 2, 1, 3)
            q, k, v = (to_heads(q), to_heads(k), to_heads(v))
            theta = BASE ** (-2.0 * (jnp.arange(HD // 2, dtype=jnp.float32) / HD))
            freqs = jnp.arange(s, dtype=jnp.float32)[:, None] * theta[None, :]
            cos, sin = (jnp.cos(freqs), jnp.sin(freqs))
            q = _rope(q, cos, sin)
            k = _rope(k, cos, sin)
            scores = jnp.einsum('bhqd,bhkd->bhqk', q, k) / jnp.sqrt(jnp.float32(HD))
            causal = jnp.tril(jnp.ones((s, s), dtype=bool))
            scores = jnp.where(causal, scores, -jnp.inf)
            attn = jax.nn.softmax(scores, axis=-1)
            y = jnp.einsum('bhqk,bhkd->bhqd', attn, v)
            y = y.transpose(0, 2, 1, 3).reshape(b, s, d)
            return y @ w_o

        def _moe(x, w_router, w1, w2):
            b, s, d = x.shape
            t = b * s
            xf = x.reshape(t, d)
            logits = xf.astype(jnp.float32) @ w_router.astype(jnp.float32)
            probs = jax.nn.softmax(logits, axis=-1)
            g, eidx = jax.lax.top_k(probs, TOP_K)
            fg = g.reshape(t * TOP_K)
            fe = eidx.reshape(t * TOP_K)
            tok_of = jnp.arange(t * TOP_K) // TOP_K
            masked = jnp.where(fe[None, :] == jnp.arange(E)[:, None], fg[None, :], -jnp.inf)
            vals, idx = jax.lax.top_k(masked, CAP)
            valid = jnp.isfinite(vals)
            gates = jnp.where(valid, vals, 0.0)
            tok = tok_of[idx]
            xe = xf[tok]
            h = jax.nn.relu(jnp.einsum('ecd,edf->ecf', xe, w1))
            ye = jnp.einsum('ecf,efd->ecd', h, w2) * gates[..., None]
            y = jnp.zeros_like(xf).at[tok.reshape(-1)].add(ye.reshape(-1, d))
            return y.reshape(b, s, d)
        x = x + _mha(_rmsnorm(x, g1), w_qkv, w_o)
        x = x + _moe(_rmsnorm(x, g2), w_router, w1, w2)
        return x

    def _L1_attn_ref(x, w_qkv, w_out, ln_g, ln_b, mem_beta):
        import jax, jax.numpy as jnp
        import numpy as np
        HEADS = 16
        DIM_HEAD = 64
        SEG = 32
        SCALE = DIM_HEAD ** (-0.5)
        INNER = HEADS * DIM_HEAD

        def elu1(x):
            return jax.nn.elu(x) + 1.0

        def rope(t, pos):
            d = t.shape[-1]
            freqs = 10000.0 ** (-jnp.arange(0, d, 2, dtype=jnp.float32) / d)
            ang = pos[:, None] * freqs
            cos = jnp.repeat(jnp.cos(ang), 2, axis=-1)
            sin = jnp.repeat(jnp.sin(ang), 2, axis=-1)
            t2 = t.reshape(t.shape[:-1] + (d // 2, 2))
            rot = jnp.stack((-t2[..., 1], t2[..., 0]), axis=-1).reshape(t.shape)
            return t * cos + rot * sin

        def _reference_tuple_inner(x, w_qkv, w_out, ln_g, ln_b, mem_beta):
            B, N, D = x.shape
            mu = x.mean(-1, keepdims=True)
            var = x.var(-1, keepdims=True)
            xn = (x - mu) / jnp.sqrt(var + 1e-05) * ln_g + ln_b
            qkv = xn @ w_qkv
            q, k, v = jnp.split(qkv, 3, axis=-1)

            def to_heads(t):
                return t.reshape(B, N, HEADS, DIM_HEAD).transpose(0, 2, 1, 3)
            q, k, v = map(to_heads, (q, k, v))
            next_k, next_v = (k, v)
            pos = jnp.arange(N, dtype=jnp.float32)
            qr, kr = (rope(q, pos), rope(k, pos))
            W = N // SEG

            def to_segs(t):
                return t.reshape(B, HEADS, W, SEG, DIM_HEAD).transpose(2, 0, 1, 3, 4)
            qs, ks, vs, qnope, knope = map(to_segs, (qr, kr, v, q, k))
            mask = jnp.tril(jnp.ones((SEG, SEG), bool))
            beta = jax.nn.sigmoid(mem_beta)
            mem0 = jnp.zeros((B, HEADS, DIM_HEAD, DIM_HEAD), x.dtype)
            z0 = jnp.full((B, HEADS, DIM_HEAD), 1e-06, x.dtype)

            def step(carry, inp):
                mem, z = carry
                q_s, k_s, v_s, qn_s, kn_s = inp
                scores = jnp.einsum('bhnd,bhmd->bhnm', q_s, k_s) * SCALE
                scores = jnp.where(mask, scores, -jnp.inf)
                sdpa = jnp.einsum('bhnm,bhmd->bhnd', jax.nn.softmax(scores, axis=-1), v_s)
                sq = elu1(qn_s)
                num = jnp.einsum('bhnk,bhkv->bhnv', sq, mem)
                den = jnp.einsum('bhnk,bhk->bhn', sq, z)[..., None]
                mem_out = num / (den + 1e-06)
                out = beta * mem_out + (1.0 - beta) * sdpa
                sk = elu1(kn_s)
                prev_v = jnp.einsum('bhnk,bhkv->bhnv', sk, mem) / jnp.einsum('bhnk,bhk->bhn', sk, z)[..., None]
                mem = mem + jnp.einsum('bhnk,bhnv->bhkv', sk, v_s - prev_v)
                z = z + sk.sum(axis=2)
                return ((mem, z), out)
            _, outs = jax.lax.scan(step, (mem0, z0), (qs, ks, vs, qnope, knope))
            o = outs.transpose(1, 0, 3, 2, 4).reshape(B, N, INNER)
            out = o @ w_out
            return (out, next_k, next_v)
        return _reference_tuple_inner(x, w_qkv, w_out, ln_g, ln_b, mem_beta)[0]

    def _L1_ffn_ref(x, weight, bias):
        import jax, jax.numpy as jnp
        import numpy as np
        FP8_E4M3_MAX = 448.0

        def fake_quant_fp8(t):
            amax = jnp.max(jnp.abs(t))
            scale = FP8_E4M3_MAX / jnp.maximum(amax, 1e-12)
            q = (t * scale).astype(jnp.float8_e4m3fn).astype(jnp.float32)
            return q / scale
        xq = fake_quant_fp8(x)
        wq = fake_quant_fp8(weight)
        return jnp.einsum('bsd,od->bso', xq, wq) + bias
    x = L0_attn_x
    xn = _layernorm(x, axis=-1)
    x = x + _L0_attn_ref(xn, L0_attn_Wq, L0_attn_Wk, L0_attn_Wv, L0_attn_Wo, L0_attn_W_down_kv, L0_attn_W_up_k, L0_attn_W_up_v) + _L0_ffn_ref(xn, L0_ffn_g1, L0_ffn_w_qkv, L0_ffn_w_o, L0_ffn_g2, L0_ffn_w_router, L0_ffn_w1, L0_ffn_w2)
    xn = _layernorm(x, axis=-1)
    x = x + _L1_attn_ref(xn, L1_attn_w_qkv, L1_attn_w_out, L1_attn_ln_g, L1_attn_ln_b, L1_attn_mem_beta) + _L1_ffn_ref(xn, L1_ffn_weight, L1_ffn_bias)
    return x

_drawn_inputs = setup_inputs


def setup_inputs(seed=0):
    import zlib

    import numpy as np

    out = dict(_drawn_inputs(seed))
    spreads = {'L0_ffn_g1': (1.0, 0.6),
     'L0_ffn_g2': (1.0, 0.6),
     'L1_attn_ln_g': (1.0, 0.6),
     'L1_attn_ln_b': (0.0, 0.8),
     'L1_attn_mem_beta': (0.0, 0.8)}
    factors = {'L0_attn_Wq': 8.0,
     'L0_attn_Wk': 8.0,
     'L0_attn_Wv': 8.0,
     'L0_attn_Wo': 8.0,
     'L0_attn_W_down_kv': 8.0,
     'L0_attn_W_up_k': 8.0,
     'L0_attn_W_up_v': 8.0,
     'L0_ffn_w_qkv': 8.0,
     'L0_ffn_w_o': 8.0,
     'L0_ffn_w_router': 8.0,
     'L0_ffn_w1': 8.0,
     'L0_ffn_w2': 8.0,
     'L1_attn_w_qkv': 4.392,
     'L1_attn_w_out': 4.497,
     'L1_ffn_bias': 39.205}
    for name, (base, spread) in spreads.items():
        noise = np.random.default_rng([zlib.crc32(name.encode()), seed]).standard_normal(out[name].shape)
        drawn = base * np.exp(spread * noise) if base else spread * noise
        out[name] = jnp.asarray(drawn.astype(out[name].dtype))
    for name, factor in factors.items():
        out[name] = (out[name] * factor).astype(out[name].dtype)
    return out
```

```python
from contextlib import ExitStack

import numpy as np
import concourse.bass as bass
from concourse import mybir

F32 = mybir.dt.float32
BF16 = mybir.dt.bfloat16
I32 = mybir.dt.int32
U32 = mybir.dt.uint32
ALU = mybir.AluOpType
ACT = mybir.ActivationFunctionType
AX = mybir.AxisListType

P = 128
NB, S, D = 16, 512, 128
NC = S // P
NT = NB * S // P
H, HD = 16, 8
NG = H // 4
E, TOPK, FF = 8, 2, 256
CAP = 160
HALF = CAP // 2
CLAMP = 10000.0
SCALE_A = float(1.0 / (np.sqrt(np.float32(128.0)) + 1e-8))
SCALE_B = float(1.0 / np.sqrt(np.float32(HD)))
UNITS = H * NC
MASKED = -1e30


def bc(ap, n):
    return ap.unsqueeze(len(ap.shape)).broadcast_to(list(ap.shape) + [n])


def clear(nc, sems):
    nums = sorted(s.num for s in sems)
    assert nums == list(range(nums[0], nums[-1] + 1))
    nc.sync.sem_clear(range(nums[0], nums[-1] + 1))
    nc.all_engine_barrier()


def fold_weights(nc, c, W):
    with ExitStack() as ctx:
        sb = lambda n, s, d=F32: ctx.enter_context(nc.sbuf_tensor(n, s, d))
        sem = lambda n: ctx.enter_context(nc.semaphore(n))
        wk, wv, wsum, wsumT = sb("fw_k", [P, D]), sb("fw_v", [P, D]), sb("fw_s", [P, D]), sb("fw_sT", [P, D])
        wd, wuk, wuv = sb("fw_d", [P, 32]), sb("fw_uk", [32, D]), sb("fw_uv", [32, D])
        bT = sb("fw_bT", [32, D])
        wqkv, g1 = sb("fw_qkv", [P, 3 * D]), sb("fw_g1", [P, 1])
        ps = ctx.enter_context(nc.psum_tensor("fw_ps", [P, 4, 512], F32))
        s_in, s_sum, s_pe, s_cp = sem("fw_in"), sem("fw_sum"), sem("fw_pe"), sem("fw_cp")
        block = ctx.enter_context(nc.Block())
        loads = [(wk, c["Wk"]), (wv, c["Wv"]), (wd, c["Wdown"]), (wuk, c["Wuk"]), (wuv, c["Wuv"]),
                 (wqkv, c["Wqkv"]), (g1, c["g1"]), (W["wqA"], c["Wq"]), (W["woA"], c["WoA"]), (W["woB"], c["WoB"]),
                 (W["ident"], c["ident"]), (W["decay"], c["decay"]), (W["cmask"], c["cmask"]),
                 (W["hmask"], c["hmask"]), (W["cosA"], c["cosA"]), (W["sinA"], c["sinA"]),
                 (W["g2b"], c["g2b"]), (W["wr"], c["Wr"])]

        @block.sync
        def _(sp):
            for dst, src in loads:
                sp.dma_start(dst[:], src).then_inc(s_in, 16)

        @block.vector
        def _(dve):
            dve.wait_ge(s_in, 16 * len(loads))
            dve.tensor_tensor(wsum[:], wk[:], wv[:], ALU.add).then_inc(s_sum, 1)
            dve.tensor_scalar(W["wB"][:, 0:3 * D], wqkv[:], g1[:, 0:1], None, ALU.mult).then_inc(s_sum, 1)
            dve.wait_ge(s_sum, 2)
            for t in range(2):
                src = W["wB"][:, t * D:(t + 1) * D].rearrange("p (n two) -> p n two", two=2)
                dst = W["wB"][:, (3 + t) * D:(4 + t) * D].rearrange("p (n two) -> p n two", two=2)
                dve.tensor_copy(dst[:, :, 0], src[:, :, 1])
                dve.tensor_copy(dst[:, :, 1], src[:, :, 0])
            dve.memset(W["vA"][:], 0.0)
            dve.memset(W["vB"][:], 0.0)
            dve.memset(W["mhalf"][:], -0.5).then_inc(s_sum, 1)
            dve.wait_ge(s_pe, 1)
            dve.tensor_copy(wsumT[:], ps[:, 0, 0:D]).then_inc(s_cp, 1)
            dve.wait_ge(s_pe, 2)
            dve.tensor_copy(bT[:], ps[0:32, 1, 0:D]).then_inc(s_cp, 1)
            dve.wait_ge(s_pe, 4)
            dve.tensor_copy(W["mk"][:], ps[:, 2, 0:D])
            dve.tensor_copy(W["mv"][:], ps[:, 3, 0:D]).then_inc(s_cp, 1)
            dve.wait_ge(s_cp, 3)

        @block.tensor
        def _(pe):
            pe.wait_ge(s_sum, 1)
            pe.transpose(ps[:, 0, 0:D], wsum[:], W["ident"][:]).then_inc(s_pe, 1)
            pe.wait_ge(s_cp, 1)
            pe.matmul(ps[0:32, 1, 0:D], wd[:], wsumT[:], start=True, stop=True).then_inc(s_pe, 1)
            pe.wait_ge(s_cp, 2)
            pe.matmul(ps[:, 2, 0:D], bT[:], wuk[:], start=True, stop=True).then_inc(s_pe, 1)
            pe.matmul(ps[:, 3, 0:D], bT[:], wuv[:], start=True, stop=True).then_inc(s_pe, 1)


def attend(nc, c, W, nb):
    with ExitStack() as ctx:
        sb = lambda n, s, d=F32: ctx.enter_context(nc.sbuf_tensor("at_" + n, s, d))
        sems = []

        def sem(n):
            sems.append(ctx.enter_context(nc.semaphore(n)))
            return sems[-1]

        x = sb("x", [P, NC, D])
        xn, hn = sb("xn", [P, NC, D]), sb("hn", [P, NC, D])
        hs = sb("hs", [P, NC, D])
        x1, xf = sb("x1", [P, NC, D]), sb("xf", [P, NC, D])
        st, mv = sb("st", [P, NC, 6]), sb("mv", [P, NC, 2])
        sc = sb("sc", [P, 8, NC])
        xnT, hnT, xfT = sb("xnT", [P, S]), sb("hnT", [P, S]), sb("xfT", [P, S])
        q = [sb("qA", [P, S]), sb("qB", [P, S])]
        k = [sb("kA", [P, S]), sb("kB", [P, S])]
        v = [W["vA"], W["vB"]]
        r1, r2 = sb("r1", [P, 2, S]), sb("r2", [P, 2, S])
        qm = sb("qm", [P, 4, S])
        clip = sb("clip", [P, 2, S])
        tt = sb("tt", [P, 2, S])
        prob = sb("prob", [P, 3, S])
        pT = sb("pT", [P, 2, 4, NC, S])
        mx, nm, rs = sb("mx", [P, 2 * UNITS]), sb("nm", [P, 2 * UNITS]), sb("rs", [P, 2 * UNITS])
        rr = sb("rr", [P, 16])
        oT = sb("oT", [P, S])
        on, onT = sb("on", [P, NC, D]), sb("onT", [P, S])
        lg, ex, pr = sb("lg", [P, NC, E]), sb("ex", [P, NC, E]), sb("pr", [P, NC, E])
        ps = ctx.enter_context(nc.psum_tensor("ps", [P, 8, 512], F32))

        x_in = sem("x_in")
        v_step, p_step = sem("v_step"), sem("p_step")
        stats, factors, normed = sem("stats"), sem("factors"), sem("normed")
        turned, turned_cp = sem("turned"), sem("turned_cp")
        proj, proj_v, proj_a = sem("proj"), sem("proj_v"), sem("proj_a")
        roped = sem("roped")
        masked = sem("masked")
        scored, clipped, maxed, exped = sem("scored"), sem("clipped"), sem("maxed"), sem("exped")
        transposed, evA, evB = sem("transposed"), sem("evA"), sem("evB")
        pv, ot_cp, ot_t, weighed = sem("pv"), sem("ot_cp"), sem("ot_t"), sem("weighed")
        on_t, on_cp, projo, added = sem("on_t"), sem("on_cp"), sem("projo"), sem("added")
        based = sem("based")
        xfd, xft, xfc, logit, lsub, lexp, probd, stored = (sem("xfd"), sem("xft"), sem("xfc"), sem("logit"),
                                                           sem("lsub"), sem("lexp"), sem("probd"), sem("stored"))
        S0, TP0, OT, OTT, M0, M1 = 0, 2, 4, 5, 6, 7

        def wait(eng, s, n):
            if n > 0:
                eng.wait_ge(s, n)

        width = lambda u: S if u < UNITS else (u % NC + 1) * P
        LAST = 2 * UNITS + 18

        def ev_wait(eng, wait, u):
            if u < UNITS:
                wait(eng, evA, u + 1)
            else:
                wait(eng, evB, u - UNITS + 1)

        with nc.Fori(0, nb) as i:
            clear(nc, sems)
            with nc.Block() as block:

                @block.sync
                def _(sp):
                    wait(sp, normed, 0)
                    wait(sp, based, 0)
                    sp.dma_start(x[:], c["x"][bass.ds(i, 1)].rearrange("o (c p) d -> p (o c) d", p=P)).then_inc(x_in, 16)
                    wait(sp, added, 2)
                    sp.dma_start(c["h_d"][bass.ds(i, 1)].rearrange("o (c p) d -> p (o c) d", p=P), hs[:]).then_inc(stored, 16)
                    wait(sp, xfd, 1)
                    sp.dma_start(c["xf_d"][bass.ds(i, 1)].rearrange("o (c p) d -> p (o c) d", p=P), xf[:]).then_inc(stored, 16)
                    wait(sp, probd, 1)
                    sp.dma_start(c["pr_d"][:, bass.ds(i, 1)].rearrange("p o c e -> p (o c) e"), pr[:]).then_inc(stored, 16)
                    sp.wait_ge(stored, 48)

                @block.gpsimd
                def _(pool):
                    step = [0]

                    def link(ins):
                        step[0] += 1
                        ins.then_inc(p_step, 1)
                        wait(pool, p_step, step[0])

                    wait(pool, stats, 1)
                    wait(pool, normed, 0)
                    link(pool.tensor_scalar(sc[:, 0], mv[:, :, 1], 1e-5, None, ALU.add))
                    link(pool.tensor_tensor(sc[:, 1], sc[:, 0], W["mhalf"][:, 0:NC], ALU.pow))
                    link(pool.tensor_tensor(sc[:, 2], mv[:, :, 1], sc[:, 1], ALU.mult))
                    link(pool.tensor_tensor(sc[:, 2], sc[:, 2], sc[:, 1], ALU.mult))
                    link(pool.tensor_scalar(sc[:, 2], sc[:, 2], 1e-6, None, ALU.add))
                    link(pool.tensor_tensor(sc[:, 3], sc[:, 2], W["mhalf"][:, 0:NC], ALU.pow))
                    pool.tensor_tensor(sc[:, 4], sc[:, 1], sc[:, 3], ALU.mult).then_inc(factors, 1)
                    wait(pool, normed, 1)
                    wait(pool, stored, 0)
                    pool.tensor_copy(hs[:], x[:]).then_inc(based, 1)
                    for n in range(2 * H):
                        a, h = divmod(n, H)
                        if h == 0:
                            wait(pool, *((proj_a, 1) if a == 0 else (roped, 1)))
                        wait(pool, scored, NC * (n - 3))
                        pool.tensor_scalar(qm[:, n % 4], q[a][:], W["hmask"][:, n:n + 1], None, ALU.mult).then_inc(masked, 1)
                    wait(pool, stats, 2)
                    link(pool.tensor_scalar(sc[:, 5], sc[:, 5], 1e-6, None, ALU.add))
                    pool.tensor_tensor(sc[:, 6], sc[:, 5], W["mhalf"][:, 0:NC], ALU.pow).then_inc(factors, 1)

                @block.tensor
                def _(pe):
                    wait(pe, normed, 1)
                    wait(pe, probd, 0)
                    wait(pe, added, 0)
                    for n in range(2):
                        for j in range(NC):
                            ins = pe.transpose(ps[:, n, j * P:(j + 1) * P], (xn, hn)[n][:, j, :], W["ident"][:])
                        ins.then_inc(turned, 1)
                    wait(pe, turned_cp, 1)
                    pe.matmul(ps[:, 2, :], W["wqA"][:], xnT[:], start=True, stop=True).then_inc(proj, 1)
                    pe.matmul(ps[:, 3, :], W["mk"][:], xnT[:], start=True, stop=True).then_inc(proj, 1)
                    for j in range(NC):
                        ins = pe.matmul(ps[:, 4, j * P:(j + 1) * P], xnT[:, j * P:(j + 1) * P], W["mv"][:], start=True, stop=True)
                    ins.then_inc(proj, 1)
                    wait(pe, turned_cp, 2)
                    for n, col in enumerate((0, 3, 1, 4)):
                        bank = (5, 6, 7, 0)[n]
                        pe.matmul(ps[:, bank, :], W["wB"][:, col * D:(col + 1) * D], hnT[:], start=True, stop=True).then_inc(proj, 1)
                    for j in range(NC):
                        ins = pe.matmul(ps[:, 1, j * P:(j + 1) * P], hnT[:, j * P:(j + 1) * P], W["wB"][:, 2 * D:3 * D], start=True, stop=True)
                    ins.then_inc(proj, 1)
                    wait(pe, proj_v, 5)
                    wait(pe, proj_a, 3)
                    for t in range(LAST):
                        if t < 2 * UNITS:
                            u, n, w = t, t // NC, width(t)
                            a = n // H
                            wait(pe, masked, n + 1)
                            if u == UNITS:
                                wait(pe, roped, 2)
                            wait(pe, clipped, u - 1)
                            pe.matmul(ps[:, S0 + u % 2, 0:w], qm[:, n % 4, (u % NC) * P:(u % NC + 1) * P], k[a][:, 0:w],
                                      start=True, stop=True).then_inc(scored, 1)
                        u = t - 2
                        if 0 <= u < 2 * UNITS:
                            wait(pe, exped, u + 1)
                            if u >= 2:
                                ev_wait(pe, wait, u - 2)
                            for j in range(width(u) // P):
                                ins = pe.transpose(ps[:, TP0 + u % 2, j * P:(j + 1) * P], prob[:, u % 3, j * P:(j + 1) * P], W["ident"][:])
                            ins.then_inc(transposed, 1)
                        g, m = divmod(t - 20, 16)
                        if m == 0 and 0 <= g < 8:
                            ev_wait(pe, wait, 16 * g + 15)
                            wait(pe, ot_cp, g)
                            for j in range(NC):
                                q0 = 0 if g < 4 else j * P
                                for s in range(4):
                                    ins = pe.matmul(ps[32 * s:32 * s + 32, OT, q0:S], v[g // 4][:, j, (g % 4) * 4 + s, :],
                                                    pT[:, g % 2, s, j, q0:S], start=(j == 0), stop=(j == NC - 1))
                            ins.then_inc(pv, 1)
                        g, m = divmod(t - 23, 16)
                        if m == 0 and 0 <= g < 8:
                            wait(pe, ot_cp, g + 1)
                            wait(pe, weighed, g)
                            for j in range(NC):
                                ins = pe.transpose(ps[:, OTT, j * P:(j + 1) * P], oT[:, j * P:(j + 1) * P], W["ident"][:])
                            ins.then_inc(ot_t, 1)
                        for a in range(2):
                            if t == UNITS * (a + 1) + 11:
                                wait(pe, weighed, 4 * (a + 1))
                                for j in range(NC):
                                    ins = pe.transpose(ps[:, M0, j * P:(j + 1) * P], on[:, j, :], W["ident"][:])
                                ins.then_inc(on_t, 1)
                            if t == UNITS * (a + 1) + 13:
                                wait(pe, on_cp, a + 1)
                                wait(pe, added, a)
                                for j in range(NC):
                                    ins = pe.matmul(ps[:, M1, j * P:(j + 1) * P], onT[:, j * P:(j + 1) * P], W[("woA", "woB")[a]][:], start=True, stop=True)
                                ins.then_inc(projo, 1)
                    wait(pe, xfd, 1)
                    for j in range(NC):
                        ins = pe.transpose(ps[:, M0, j * P:(j + 1) * P], xf[:, j, :], W["ident"][:])
                    ins.then_inc(xft, 1)
                    wait(pe, xfc, 1)
                    for j in range(NC):
                        ins = pe.matmul(ps[:, M1, j * E:(j + 1) * E], xfT[:, j * P:(j + 1) * P], W["wr"][:], start=True, stop=True)
                    ins.then_inc(logit, 1)

                @block.scalar
                def _(act):
                    for n in range(2):
                        wait(act, turned, n + 1)
                        act.copy((xnT, hnT)[n][:], ps[:, n, :]).then_inc(turned_cp, 1)
                    wait(act, proj, 1)
                    act.copy(q[0][:], ps[:, 2, :]).then_inc(proj_a, 1)
                    wait(act, proj, 3)
                    heads = lambda bank: ps[:, bank, :].rearrange("p (c h d) -> p (c h) d", c=NC, d=HD)
                    act.copy(v[0][:, :, :, 0:HD].rearrange("p c h d -> p (c h) d"), heads(4)).then_inc(proj_a, 1)
                    wait(act, proj, 8)
                    act.copy(v[1][:, :, :, 0:HD].rearrange("p c h d -> p (c h) d"), heads(1)).then_inc(proj_a, 1)
                    for t in range(LAST):
                        if t < 2 * UNITS:
                            u, w = t, width(t)
                            wait(act, maxed, u + 1)
                            wait(act, transposed, u - 2)
                            act.activation(prob[:, u % 3, 0:w], tt[:, u % 2, 0:w], ACT.Exp, bias=nm[:, u:u + 1],
                                           accum_out=rs[:, u:u + 1]).then_inc(exped, 1)
                        u = t - 3
                        if 0 <= u < UNITS:
                            wait(act, transposed, u + 1)
                            wait(act, pv, u // 16 - 1)
                            act.copy(pT[:, (u // 16) % 2, (u // NC) % 4, :, (u % NC) * P:(u % NC + 1) * P],
                                     ps[:, TP0 + u % 2, :].rearrange("p (j r) -> p j r", j=NC)).then_inc(evA, 1)
                        g, m = divmod(t - 21, 16)
                        if m == 0 and 0 <= g < 8:
                            wait(act, pv, g + 1)
                            wait(act, ot_t, g)
                            act.copy(oT[:], ps[:, OT, :]).then_inc(ot_cp, 1)
                        for a in range(2):
                            if t == UNITS * (a + 1) + 12:
                                wait(act, on_t, a + 1)
                                wait(act, projo, a)
                                act.copy(onT[:], ps[:, M0, :]).then_inc(on_cp, 1)
                    wait(act, xft, 1)
                    act.copy(xfT[:], ps[:, M0, :]).then_inc(xfc, 1)
                    wait(act, lsub, 1)
                    act.activation(ex[:], lg[:], ACT.Exp).then_inc(lexp, 1)

                @block.vector
                def _(dve):
                    step = [0]

                    def link(ins):
                        step[0] += 1
                        ins.then_inc(v_step, 1)
                        wait(dve, v_step, step[0])

                    wait(dve, x_in, 16)
                    for j in range(NC):
                        ins = dve.bn_stats(st[:, j], x[:, j, :])
                    link(ins)
                    for j in range(NC):
                        ins = dve.bn_aggr(mv[:, j], st[:, j])
                    ins.then_inc(stats, 1)
                    wait(dve, factors, 1)
                    for j in range(NC):
                        dve.tensor_scalar(xn[:, j], x[:, j], mv[:, j, 0:1], sc[:, 1, j:j + 1], ALU.subtract, ALU.mult)
                    for j in range(NC):
                        ins = dve.tensor_scalar(hn[:, j], x[:, j], mv[:, j, 0:1], sc[:, 4, j:j + 1], ALU.subtract, ALU.mult)
                    ins.then_inc(normed, 1)
                    wait(dve, proj, 2)
                    dve.tensor_copy(k[0][:], ps[:, 3, :]).then_inc(proj_v, 1)
                    for n, bank in enumerate((5, 6, 7, 0)):
                        wait(dve, proj, 4 + n)
                        dst = (r1 if n < 2 else r2)[:, n % 2]
                        dve.tensor_tensor(dst, ps[:, bank, :], W[("cosA", "sinA")[n % 2]][:], ALU.mult).then_inc(proj_v, 1)
                    wait(dve, proj_v, 5)
                    dve.tensor_tensor(q[1][:], r1[:, 0], r1[:, 1], ALU.add).then_inc(roped, 1)
                    dve.tensor_tensor(k[1][:], r2[:, 0], r2[:, 1], ALU.add).then_inc(roped, 1)
                    for t in range(LAST):
                        if t < 2 * UNITS:
                            u, w, n = t, width(t), t % NC
                            wait(dve, scored, u + 1)
                            wait(dve, exped, u - 1)
                            if u < UNITS:
                                dve.tensor_scalar(clip[:, u % 2], ps[:, S0 + u % 2, :], CLAMP, -CLAMP, ALU.min, ALU.max).then_inc(clipped, 1)
                                wait(dve, clipped, u + 1)
                                link(dve.tensor_tensor_reduce(tt[:, u % 2], clip[:, u % 2], W["decay"][:, n], 1.0, -3e38,
                                                              ALU.mult, ALU.max, mx[:, u:u + 1]))
                            else:
                                dve.tensor_tensor_reduce(tt[:, u % 2, 0:w], ps[:, S0 + u % 2, 0:w], W["cmask"][:, S - w:S], 1.0, -3e38,
                                                         ALU.add, ALU.max, mx[:, u:u + 1]).then_inc(clipped, 1)
                                wait(dve, clipped, u + 1)
                            dve.tensor_scalar(nm[:, u:u + 1], mx[:, u:u + 1], -1.0, None, ALU.mult).then_inc(maxed, 1)
                        u = t - 3
                        if UNITS <= u < 2 * UNITS:
                            wait(dve, transposed, u + 1)
                            wait(dve, pv, u // 16 - 1)
                            w = width(u)
                            dve.tensor_copy(pT[:, (u // 16) % 2, (u // NC) % 4, 0:w // P, (u % NC) * P:(u % NC + 1) * P],
                                            ps[:, TP0 + u % 2, 0:w].rearrange("p (j r) -> p j r", r=P)).then_inc(evB, 1)
                        g, m = divmod(t - 25, 16)
                        if m == 0 and 0 <= g < 8:
                            wait(dve, exped, 16 * g + 16)
                            link(dve.reciprocal(rr[:], rs[:, 16 * g:16 * g + 16]))
                            wait(dve, ot_t, g + 1)
                            if g == 4:
                                wait(dve, on_t, 1)
                            for j in range(NC):
                                ins = dve.tensor_tensor(
                                    on[:, j, 32 * (g % 4):32 * (g % 4) + 32].rearrange("p (s d) -> p s d", d=HD),
                                    ps[:, OTT, j * P:(j + 1) * P].rearrange("p (s d) -> p s d", s=4)[:, :, 0:HD],
                                    bc(rr[:].rearrange("p (s c) -> p s c", c=NC)[:, :, j], HD),
                                    ALU.mult)
                            ins.then_inc(weighed, 1)
                        if t == UNITS + 16:
                            wait(dve, projo, 1)
                            wait(dve, based, 1)
                            dve.tensor_tensor(hs[:].rearrange("p c d -> p (c d)"), hs[:].rearrange("p c d -> p (c d)"), ps[:, M1, :], ALU.add).then_inc(added, 1)
                    wait(dve, projo, 2)
                    wait(dve, added, 1)
                    link(dve.tensor_tensor(x1[:].rearrange("p c d -> p (c d)"), xn[:].rearrange("p c d -> p (c d)"), ps[:, M1, :], ALU.add))
                    dve.tensor_tensor(hs[:], hs[:], x1[:], ALU.add).then_inc(added, 1)
                    for j in range(NC):
                        ins = dve.bn_stats(st[:, j], x1[:, j, :])
                    link(ins)
                    for j in range(NC):
                        ins = dve.bn_aggr(mv[:, j], st[:, j])
                    link(ins)
                    link(dve.tensor_tensor(sc[:, 7], mv[:, :, 0], mv[:, :, 0], ALU.mult))
                    dve.tensor_tensor(sc[:, 5], sc[:, 7], mv[:, :, 1], ALU.add).then_inc(stats, 1)
                    wait(dve, factors, 2)
                    wait(dve, stored, 0)
                    for j in range(NC):
                        ins = dve.scalar_tensor_tensor(xf[:, j], x1[:, j], sc[:, 6, j:j + 1], W["g2b"][:], ALU.mult, ALU.mult)
                    ins.then_inc(xfd, 1)
                    wait(dve, logit, 1)
                    link(dve.tensor_reduce(sc[:, 7], ps[:, M1, 0:NC * E].rearrange("p (c e) -> p c e", e=E), AX.X, ALU.max))
                    dve.tensor_tensor(lg[:], ps[:, M1, 0:NC * E].rearrange("p (c e) -> p c e", e=E), bc(sc[:, 7], E), ALU.subtract).then_inc(lsub, 1)
                    wait(dve, lexp, 1)
                    link(dve.tensor_reduce(sc[:, 7], ex[:], AX.X, ALU.add))
                    link(dve.reciprocal(sc[:, 7], sc[:, 7]))
                    dve.tensor_tensor(pr[:], ex[:], bc(sc[:, 7], E), ALU.mult).then_inc(probd, 1)


def route(nc, c, W, R):
    with ExitStack() as ctx:
        sb = lambda n, s, d=F32: ctx.enter_context(nc.sbuf_tensor("rt_" + n, s, d))
        sem = lambda n: ctx.enter_context(nc.semaphore(n))
        NE = NT * E
        prob = sb("prob", [P, NT, E])
        rank, eqs = sb("rank", [P, NT, E]), sb("eqs", [P, NT, E])
        cmp = sb("cmp", [P, NT, E, E])
        gate = sb("gate", [P, NT, E])
        gt = sb("gt", [P, E, NT])
        hit = sb("hit", [P, E, NT])
        low = sb("low", [P, E, E])
        ones, before = sb("ones", [P, P]), sb("before", [P, P])
        restart = sb("restart", [P, NE])
        cnt, need = sb("cnt", [P, E]), sb("need", [P, E])
        thr, cand, bit, add = (sb("thr", [P, E], I32), sb("cand", [P, E], I32), sb("bit", [P, E], I32), sb("add", [P, E], I32))
        bitf = sb("bitf", [P, E])
        above, equal, keep = sb("above", [P, E, NT]), sb("equal", [P, E, NT]), sb("keep", [P, E, NT])
        incl, pos = sb("incl", [P, NE]), sb("pos", [P, E, NT])
        slots = sb("slots", [P, E, CAP])
        onehot = sb("onehot", [P, 2, E * CAP], BF16)
        ptid = sb("ptid", [P, NT, 2])
        pt = sb("pt", [P, 2, 2], BF16)
        place = sb("place", [2, E * CAP])
        mix = sb("mix", [2, 2])
        ps = ctx.enter_context(nc.psum_tensor("rt_ps", [P, 8, 512], F32))
        s_in, step, counted, scanned = sem("rt_in"), sem("rt_step"), sem("rt_counted"), sem("rt_scanned")
        cnt_ready, bit_step, ranked = sem("rt_cnt_ready"), sem("rt_bit_step"), sem("rt_ranked")
        hot, placed, copied, turned, gated = sem("rt_hot"), sem("rt_placed"), sem("rt_copied"), sem("rt_turned"), sem("rt_gated")
        hot_prep = sem("rt_hot_prep")
        BITS = 30
        block = ctx.enter_context(nc.Block())
        loads = [(prob[:].rearrange("p t e -> p (t e)"), c["pr_d"].rearrange("p b c e -> p (b c e)")),
                 (low[:].rearrange("p a b -> p (a b)"), c["low"]), (before[:], c["before"]), (restart[:], c["restart"]),
                 (slots[:].rearrange("p a b -> p (a b)"), c["slots"]), (ptid[:].rearrange("p a b -> p (a b)"), c["ptid"]),
                 (mix[:], c["mix"])]
        flat = lambda ap: ap.rearrange("p a b -> p (a b)")
        ET = [P, E, NT]

        @block.sync
        def _(sp):
            for dst, src in loads:
                sp.dma_start(dst, src).then_inc(s_in, 16)
            sp.wait_ge(gated, 1)
            sp.dma_start(c["gate_d"].rearrange("(p t) e -> p (t e)", p=P), flat(gate[:])).then_inc(s_in, 16)
            sp.wait_ge(s_in, 16 * (len(loads) + 1))

        @block.vector
        def _(dve):
            n = [0]

            def link(ins):
                n[0] += 1
                ins.then_inc(step, 1)
                dve.wait_ge(step, n[0])

            dve.memset(ones[:], 1.0)
            dve.memset(ps[0:2, 3:6, :], 0.0).then_inc(placed, 1)
            dve.memset(thr[:], 0)
            dve.memset(bit[:], 1 << (BITS - 1))
            link(dve.memset(bitf[:], float(1 << (BITS - 1))))
            dve.wait_ge(s_in, 16 * len(loads))
            other = prob[:].unsqueeze(2).broadcast_to([P, NT, E, E])
            mine = bc(prob[:], E)
            link(dve.tensor_tensor(cmp[:], other, mine, ALU.is_gt))
            link(dve.tensor_reduce(rank[:], cmp[:], AX.X, ALU.add))
            link(dve.tensor_tensor(cmp[:], other, mine, ALU.is_equal))
            link(dve.tensor_tensor(cmp[:], cmp[:], low[:].unsqueeze(1).broadcast_to([P, NT, E, E]), ALU.mult))
            link(dve.tensor_reduce(eqs[:], cmp[:], AX.X, ALU.add))
            link(dve.tensor_tensor(rank[:], rank[:], eqs[:], ALU.add))
            dve.scalar_tensor_tensor(gate[:], rank[:], float(TOPK), prob[:], ALU.is_lt, ALU.mult).then_inc(gated, 1)
            dve.wait_ge(gated, 1)
            link(dve.tensor_copy(gt[:], gate[:].rearrange("p t e -> p e t")))
            with dve.Fori(0, BITS) as i:
                dve.tensor_tensor(cand[:], thr[:], bit[:], ALU.bitwise_or).then_inc(bit_step, 1)
                dve.wait_ge(bit_step, i * 4 + 1)
                dve.tensor_tensor(hit[:], gt[:], bc(cand[:].bitcast(F32), NT), ALU.is_ge).then_inc(bit_step, 1)
                dve.wait_ge(bit_step, i * 4 + 2)
                dve.tensor_reduce(cnt[:], hit[:], AX.X, ALU.add).then_inc(cnt_ready, 1)
                dve.wait_ge(counted, i + 1)
                dve.scalar_tensor_tensor(add[:], ps[:, 0, 0:E], float(CAP), bitf[:], ALU.is_ge, ALU.mult).then_inc(bit_step, 1)
                dve.wait_ge(bit_step, i * 4 + 3)
                dve.tensor_tensor(thr[:], thr[:], add[:], ALU.bitwise_or)
                dve.tensor_scalar(bit[:], bit[:], 1, None, ALU.logical_shift_right)
                dve.tensor_scalar(bitf[:], bitf[:], 0.5, None, ALU.mult).then_inc(bit_step, 1)
                dve.wait_ge(bit_step, i * 4 + 4)
            cut = bc(thr[:].bitcast(F32), NT)
            dve.tensor_tensor(above[:], gt[:], cut, ALU.is_gt)
            link(dve.tensor_tensor(equal[:], gt[:], cut, ALU.is_equal))
            dve.tensor_reduce(cnt[:], above[:], AX.X, ALU.add).then_inc(cnt_ready, 1)
            dve.wait_ge(counted, BITS + 1)
            link(dve.tensor_scalar(need[:], ps[:, 0, 0:E], -1.0, float(CAP), ALU.mult, ALU.add))

            def rank_before(k):
                dve.wait_ge(ranked, k)
                link(dve.tensor_tensor_scan(incl[:], restart[:], ps[:, 2, :], 0.0, ALU.mult, ALU.add))
                link(dve.tensor_tensor(incl[:], incl[:], ps[:, 2, :], ALU.subtract))
                link(dve.tensor_tensor(flat(pos[:]), incl[:], ps[:, 1, :], ALU.add))

            rank_before(1)
            link(dve.tensor_tensor(pos[:], pos[:], bc(need[:], NT), ALU.is_lt))
            link(dve.tensor_tensor(pos[:], pos[:], equal[:], ALU.mult))
            dve.tensor_tensor(keep[:], above[:], pos[:], ALU.add).then_inc(scanned, 1)
            rank_before(2)
            link(dve.scalar_tensor_tensor(pos[:], pos[:], 1.0, keep[:], ALU.add, ALU.mult))
            link(dve.tensor_scalar(pos[:], pos[:], -1.0, None, ALU.add))
            with dve.Fori(0, NT // 2) as i:
                for b in range(2):
                    dve.wait_ge(placed, i * 2 + 1)
                    dve.tensor_copy(pt[:, b], ptid[:, bass.ds(i * 2 + b, 1)].rearrange("p a b -> p (a b)"))
                    dve.tensor_tensor(onehot[:, b].rearrange("p (e s) -> p e s", e=E), slots[:],
                                      pos[:, :, bass.ds(i * 2 + b, 1)].broadcast_to([P, E, CAP]), ALU.is_equal).then_inc(hot, 1)
            dve.wait_ge(placed, NT + 1)
            for b in range(3):
                w = min(512, E * CAP - 512 * b)
                ins = dve.tensor_copy(place[:, 512 * b:512 * b + w], ps[0:2, 3 + b, 0:w])
            ins.then_inc(copied, 1)
            dve.wait_ge(turned, 1)
            link(dve.tensor_copy(R["rows"][0:HALF], ps[0:HALF, 6, 0:64].rearrange("p (m k) -> p m k", k=2)[:, 0:2 * E, :]))

        @block.tensor
        def _(pe):
            pe.wait_ge(step, 1)
            with pe.Fori(0, BITS + 1) as i:
                pe.wait_ge(cnt_ready, i + 1)
                pe.matmul(ps[:, 0, 0:E], ones[:], cnt[:], start=True, stop=True).then_inc(counted, 1)
            for k, marked in enumerate((equal, keep)):
                pe.wait_ge(*((step, 10) if k == 0 else (scanned, 1)))
                pe.matmul(ps[:, 1, :], before[:], flat(marked[:]), start=True, stop=True)
                pe.matmul(ps[:, 2, :], ones[:], flat(marked[:]), start=True, stop=True).then_inc(ranked, 1)
            with pe.Fori(0, NT // 2) as i:
                for b in range(2):
                    pe.wait_ge(hot, i * 2 + b + 1)
                    for m in range(3):
                        w = min(512, E * CAP - 512 * m)
                        ins = pe.matmul(ps[0:2, 3 + m, 0:w], pt[:, b], onehot[:, b, 512 * m:512 * m + w],
                                        start=False, stop=False, skip_group_check=True)
                    ins.then_inc(placed, 1)
            pe.wait_ge(copied, 1)
            for m in range(2 * E):
                ins = pe.matmul(ps[0:HALF, 6, 2 * m:2 * m + 2], place[:, HALF * m:HALF * (m + 1)], mix[:], start=True, stop=True)
            ins.then_inc(turned, 1)


def experts(nc, c, W, R):
    with ExitStack() as ctx:
        sb = lambda n, s, d=F32: ctx.enter_context(nc.sbuf_tensor("ex_" + n, s, d))
        sem = lambda n: ctx.enter_context(nc.semaphore(n))
        w1, w2 = sb("w1", [P, E, FF]), sb("w2", [P, E, 2, D])
        xe, ge = sb("xe", [P, 2 * E, D]), sb("ge", [P, 2 * E, E])
        xeT, hT = sb("xeT", [P, 2, CAP]), sb("hT", [P, 2, 2, CAP])
        ye = sb("ye", [P, 2 * E, D])
        ps = ctx.enter_context(nc.psum_tensor("ex_ps", [P, 8, 512], F32))
        s_in = sem("ex_in")
        fetched = [sem(f"ex_fetched{e}") for e in range(E)]
        turned, turned_cp, hidden, relued, out, scaled, summed = (sem("ex_turned"), sem("ex_turned_cp"), sem("ex_hidden"),
                                                                  sem("ex_relued"), sem("ex_out"), sem("ex_scaled"), sem("ex_summed"))
        rows = R["rows"]
        block = ctx.enter_context(nc.Block())

        @block.sync
        def _(sp):
            sp.dma_start(w1[:], c["w1"].rearrange("e d f -> d e f")).then_inc(s_in, 16)
            sp.dma_start(w2[:].rearrange("p e h d -> p (e h) d"), c["w2"].rearrange("e (h p) d -> p (e h) d", p=P)).then_inc(s_in, 16)

        @block.gpsimd
        def _(pool):
            for m in range(2 * E):
                pool.indirect_dma_start(xe[0:HALF, m, :], None, c["xf_d"].rearrange("b s d -> (b s) d"),
                                        bass.IndirectOffsetOnAxis(rows[0:HALF, m, 0:1], 0)).then_inc(fetched[m // 2], 16)
                pool.indirect_dma_start(ge[0:HALF, m, :], None, c["gate_d"],
                                        bass.IndirectOffsetOnAxis(rows[0:HALF, m, 1:2], 0)).then_inc(fetched[m // 2], 16)
            for m in range(2 * E):
                e = m // 2
                pool.wait_ge(scaled, e + 1)
                pool.wait_ge(summed, 32 * e)
                pool.indirect_dma_start(c["h_d"].rearrange("b s d -> (b s) d"),
                                        bass.IndirectOffsetOnAxis(rows[0:HALF, m, 0:1], 0), ye[0:HALF, m, :], None,
                                        compute_op=ALU.add).then_inc(summed, 16)
            pool.wait_ge(summed, 32 * E)

        @block.tensor
        def _(pe):
            for e in range(E):
                b = e % 2
                pe.wait_ge(fetched[e], 64)
                if e >= 2:
                    pe.wait_ge(turned_cp, e - 1)
                for k in range(2):
                    ins = pe.transpose(ps[:, b, k * HALF:(k + 1) * HALF], xe[0:HALF, 2 * e + k, :], W["ident"][0:HALF, 0:HALF])
                ins.then_inc(turned, 1)
                pe.wait_ge(turned_cp, e + 1)
                pe.wait_ge(s_in, 32)
                if e >= 2:
                    pe.wait_ge(relued, e - 1)
                for f in range(2):
                    ins = pe.matmul(ps[:, 2 + b, f * CAP:(f + 1) * CAP], w1[:, e, f * P:(f + 1) * P], xeT[:, b], start=True, stop=True)
                ins.then_inc(hidden, 1)
                pe.wait_ge(relued, e + 1)
                if e >= 2:
                    pe.wait_ge(scaled, e - 1)
                for k in range(2):
                    for f in range(2):
                        ins = pe.matmul(ps[0:HALF, 4 + b, k * D:(k + 1) * D], hT[:, b, f, k * HALF:(k + 1) * HALF], w2[:, e, f, :],
                                        start=(f == 0), stop=(f == 1))
                ins.then_inc(out, 1)

        @block.scalar
        def _(act):
            for e in range(E):
                b = e % 2
                act.wait_ge(turned, e + 1)
                act.copy(xeT[:, b], ps[:, b, 0:CAP]).then_inc(turned_cp, 1)
                act.wait_ge(hidden, e + 1)
                act.activation(hT[:, b].rearrange("p f s -> p (f s)"), ps[:, 2 + b, 0:2 * CAP], ACT.Relu).then_inc(relued, 1)

        @block.vector
        def _(dve):
            for e in range(E):
                dve.wait_ge(out, e + 1)
                for k in range(2):
                    m = 2 * e + k
                    ins = dve.tensor_scalar(ye[0:HALF, m, :], ps[0:HALF, 4 + e % 2, k * D:(k + 1) * D], ge[0:HALF, m, e:e + 1], None, ALU.mult)
                ins.then_inc(scaled, 1)


B1, SEG, DH = 4, 32, 64
NSEG = S // SEG
BG = NB // B1
PAIRS = H // 2
VE = DH + 1
QMAX = 448.0
Q_ROUND = 1.5 * 2.0 ** 20
Q_LEAST = 2.0 ** -6


def quantize(dve, link, dst, src, scale, tmp, mag):
    link(dve.tensor_scalar(tmp, src, scale, None, ALU.mult))
    link(dve.tensor_scalar(mag.bitcast(I32), tmp.bitcast(I32), 0x7F800000, None, ALU.bitwise_and))
    link(dve.tensor_scalar(mag, mag, Q_LEAST, Q_ROUND, ALU.max, ALU.mult))
    link(dve.tensor_tensor(tmp, tmp, mag, ALU.add))
    return dve.tensor_tensor(dst, tmp, mag, ALU.subtract)


def scale_factors(nc, c, V):
    with ExitStack() as ctx:
        sb = lambda n, s, d=F32: ctx.enter_context(nc.sbuf_tensor("sf_" + n, s, d))
        sem = lambda n: ctx.enter_context(nc.semaphore(n))
        NL = 4
        h = sb("h", [P, 2, NT // NL, D])
        st, mv = sb("st", [P, NT // NL, 6]), sb("mv", [P, NT // NL, 2])
        ve, rstd = sb("ve", [P, NT // NL]), sb("rstd", [P, NT // NL])
        half = sb("half", [P, NT // NL])
        lohi, am = sb("lohi", [P, 2, NT // NL]), sb("am", [P, NL, 2])
        top = sb("top", [P, 2])
        row, mrow, srow = sb("row", [2, P]), sb("mrow", [2, 1]), sb("srow", [2, 1])
        dia = sb("dia", [2, 2])
        ones2 = sb("ones2", [2, P])
        w, wT, tmp, mag = sb("w", [P, D]), sb("wT", [P, D]), sb("tmp", [P, D]), sb("mag", [P, D])
        beta = sb("beta", [P, H])
        ps = ctx.enter_context(nc.psum_tensor("sf_ps", [P, 8, 512], F32))
        s_w, s_h = sem("sf_w"), [sem("sf_h0"), sem("sf_h1")]
        step, stat, fact, used = sem("sf_step"), sem("sf_stat"), sem("sf_fact"), sem("sf_used")
        pe_s, act_s, halves = sem("sf_pe"), sem("sf_act"), sem("sf_halves")
        loads = [(V["wqkv"][:, 0:3072], c["w1qkv"]), (V["wout"][:], c["wout"].rearrange("(j p) d -> p j d", p=P)),
                 (V["g"][:], c["ln_g"]), (V["b"][:], c["ln_b"]), (V["bias"][:], c["bias"]), (beta[:], c["beta"]),
                 (V["ident"][:], c["ident"]), (V["cos"][:], c["cos1"]), (V["sin"][:], c["sin1"]), (V["mask"][:], c["mask1"]),
                 (w[:], c["wffn"])]
        block = ctx.enter_context(nc.Block())
        h_all = c["h_d"].rearrange("b (k p) d -> p (b k) d", p=P)
        K = NT // NL

        @block.sync
        def _(sp):
            for n in range(NL):
                if n >= 2:
                    sp.wait_ge(used, n - 1)
                sp.dma_start(h[:, n % 2], h_all[:, n * K:(n + 1) * K, :]).then_inc(s_h[n % 2], 16)
                if n == 1:
                    for dst, src in loads:
                        sp.dma_start(dst, src).then_inc(s_w, 16)

        @block.gpsimd
        def _(pool):
            pool.memset(half[:], -0.5).then_inc(halves, 1)
            pool.memset(V["mhalf"][:], -0.5)
            pool.memset(V["uu"][:], 1.0)
            pool.memset(V["mem"][:, :, :, 0:DH], 0.0)
            pool.memset(V["mem"][:, :, :, DH:VE], 1e-6)
            pool.wait_ge(halves, 1)
            for n in range(NL):
                pool.wait_ge(stat, n + 1)
                pool.tensor_tensor(rstd[:], ve[:], half[:], ALU.pow).then_inc(fact, 1)

        @block.scalar
        def _(act):
            act.wait_ge(s_w, 16 * len(loads))
            act.activation(V["beta"][:], beta[:], ACT.Exp, scale=-1.0).then_inc(act_s, 1)

        @block.tensor
        def _(pe):
            pe.wait_ge(s_w, 16 * len(loads))
            pe.transpose(ps[:, 0, 0:D], w[:], V["ident"][:]).then_inc(pe_s, 1)
            pe.wait_ge(used, NL + 1)
            pe.transpose(ps[0:2, 1, 0:P], top[:], V["ident"][:]).then_inc(pe_s, 1)
            pe.wait_ge(used, NL + 2)
            pe.matmul(ps[:, 2, 0:2], ones2[:], dia[:], start=True, stop=True).then_inc(pe_s, 1)

        @block.vector
        def _(dve):
            n_ = [0]

            def link(ins):
                n_[0] += 1
                ins.then_inc(step, 1)
                dve.wait_ge(step, n_[0])

            for n in range(NL):
                dve.wait_ge(s_h[n % 2], 16 * (n // 2 + 1))
                for j in range(K):
                    ins = dve.bn_stats(st[:, j], h[:, n % 2, j])
                link(ins)
                for j in range(K):
                    ins = dve.bn_aggr(mv[:, j], st[:, j])
                link(ins)
                dve.tensor_scalar(ve[:], mv[:, :, 1], 1e-5, None, ALU.add).then_inc(stat, 1)
                dve.tensor_reduce(lohi[:, 0], h[:, n % 2], AX.X, ALU.min)
                link(dve.tensor_reduce(lohi[:, 1], h[:, n % 2], AX.X, ALU.max))
                link(dve.tensor_tensor(lohi[:], lohi[:], mv[:, :, 0].unsqueeze(1).broadcast_to([P, 2, K]), ALU.subtract))
                dve.wait_ge(fact, n + 1)
                link(dve.tensor_tensor(lohi[:], lohi[:], rstd[:].unsqueeze(1).broadcast_to([P, 2, K]), ALU.mult))
                dve.tensor_reduce(am[:, n, 0:1], lohi[:], AX.XY, ALU.max)
                dve.tensor_reduce(am[:, n, 1:2], lohi[:], AX.XY, ALU.min).then_inc(used, 1)
            dve.wait_ge(used, NL)
            link(dve.tensor_scalar(am[:, :, 1], am[:, :, 1], -1.0, None, ALU.mult))
            dve.tensor_reduce(top[:, 0:1], am[:], AX.XY, ALU.max)
            dve.wait_ge(s_w, 16 * len(loads))
            dve.memset(ones2[:], 1.0)
            dve.tensor_reduce(top[:, 1:2], w[:], AX.X, ALU.max, apply_absolute_value=True).then_inc(used, 1)
            for t in range(2):
                src = V["wqkv"][:, 1024 * t:1024 * (t + 1)].rearrange("p (n two) -> p n two", two=2)
                dst = V["wqkv"][:, 3072 + 1024 * t:3072 + 1024 * (t + 1)].rearrange("p (n two) -> p n two", two=2)
                dve.tensor_copy(dst[:, :, 0], src[:, :, 1])
                dve.tensor_copy(dst[:, :, 1], src[:, :, 0])
            link(dve.tensor_copy(V["ident_bf"][:], V["ident"][:]))
            dve.wait_ge(pe_s, 1)
            link(dve.tensor_copy(wT[:], ps[:, 0, 0:D]))
            dve.wait_ge(act_s, 1)
            link(dve.tensor_scalar(V["beta"][:], V["beta"][:], 1.0, None, ALU.add))
            link(dve.reciprocal(V["beta"][:], V["beta"][:]))
            link(dve.tensor_scalar(V["rest"][:], V["beta"][:], -1.0, 1.0, ALU.mult, ALU.add))
            dve.wait_ge(pe_s, 2)
            link(dve.tensor_reduce(mrow[:], ps[0:2, 1, 0:P], AX.X, ALU.max))
            link(dve.tensor_scalar(mrow[:], mrow[:], 1e-12, None, ALU.max))
            link(dve.reciprocal(srow[:], mrow[:]))
            link(dve.tensor_scalar(srow[:], srow[:], QMAX, None, ALU.mult))
            dve.tensor_scalar(dia[:], V["ident"][0:2, 0:2], srow[:, 0:1], None, ALU.mult).then_inc(used, 1)
            dve.wait_ge(pe_s, 3)
            link(dve.tensor_copy(V["qs"][:, 0:2], ps[:, 2, 0:2]))
            link(dve.reciprocal(V["qs"][:, 2:4], V["qs"][:, 0:2]))
            link(dve.tensor_tensor(V["qs"][:, 4:5], V["qs"][:, 2:3], V["qs"][:, 3:4], ALU.mult))
            link(quantize(dve, link, V["wq"][:], wT[:], V["qs"][:, 1:2], tmp[:], mag[:]))


def scan(nc, c, V, out, nseg):
    with ExitStack() as ctx:
        sb = lambda n, s, d=F32: ctx.enter_context(nc.sbuf_tensor("sc_" + n, s, d))
        sems = []

        def sem(n):
            sems.append(ctx.enter_context(nc.semaphore(n)))
            return sems[-1]
        ht, xn = sb("ht", [P, BG, D]), sb("xn", [P, BG, D])
        y = sb("y", [P, BG, D])
        hb = sb("hb", [P, BG, D])
        st, mv, sc = sb("st", [P, BG, 6]), sb("mv", [P, BG, 2]), sb("sc", [P, 4, BG])
        xnn = sb("xnn", [P, BG, D])
        tq, mq, xq = sb("tq", [P, BG, D]), sb("mq", [P, BG, D]), sb("xq", [P, BG, D], BF16)
        xT, xqT = sb("xT", [P, S]), sb("xqT", [P, S], BF16)
        uu = V["uu"]
        ol = sb("ol", [P, BG, H, DH])
        sigT = [sb("sqT", [P, PAIRS, S]), sb("skT", [P, PAIRS, S])]
        skN = sb("skN", [P, BG, PAIRS * P])
        ee = sb("ee", [P, 2, S])
        ra, rb = sb("ra", [P, 2, S]), sb("rb", [P, 2, S])
        rot = [sb("qr", [P, 2, S]), sb("kr", [P, 2, S])]
        HC = 8 * BG
        ss = sb("ss", [P, HC, SEG])
        pT = sb("pT", [P, 2, HC, SEG])
        mx, sm = sb("mx", [P, HC]), sb("sm", [P, 2, HC])
        rk, rq = sb("rk", [P, 2, BG]), sb("rq", [P, 2, BG])
        t1, t2 = sb("t1", [P, 2, 2, BG * DH]), sb("t2", [P, 2, 2, BG * DH])
        oT = sb("oT", [P, 2, PAIRS, P])
        ps = ctx.enter_context(nc.psum_tensor("sc_ps", [P, 8, 512], F32))
        names = ("h_in stat fact xn_d xnn_d xq_d step xt xt_c xqt xqt_c ffn ffn_c hb_d vp v_a v_d pj ex mn rp sg add_d sS skt skc "
                 "smask sx se pt pvd old kr_s qr_s kd ud qd od up mu ott otc_a otc_d oproj ydone stored").split()
        G = {n: sem("sc_" + n) for n in names}
        h_seg = c["h_d"].rearrange("(g f) (s i) d -> f s i g d", f=B1, i=SEG)
        o_seg = out.rearrange("(g f) (s i) d -> f s i g d", f=B1, i=SEG)

        def wait(eng, name, n):
            if n > 0:
                eng.wait_ge(G[name], n)

        flat = lambda ap: ap.rearrange("p g d -> p (g d)")
        pair_cols = lambda p: slice(p * P, (p + 1) * P)

        with nc.Fori(0, nseg) as i:
            clear(nc, sems)
            with nc.Block() as block:

                @block.sync
                def _(sp):
                    wait(sp, "xn_d", 0)
                    wait(sp, "hb_d", 0)
                    for f in range(B1):
                        sp.dma_start(ht[32 * f:32 * f + 32], h_seg[f, bass.ds(i, 1)].rearrange("o i g d -> (o i) g d")).then_inc(G["h_in"], 16)
                    wait(sp, "ydone", 1)
                    for f in range(B1):
                        sp.dma_start(o_seg[f, bass.ds(i, 1)].rearrange("o i g d -> (o i) g d"), y[32 * f:32 * f + 32]).then_inc(G["stored"], 16)
                    sp.wait_ge(G["stored"], 64)

                @block.gpsimd
                def _(pool):
                    wait(pool, "stat", 1)
                    pool.tensor_tensor(sc[:, 1], sc[:, 0], V["mhalf"][:, 0:BG], ALU.pow).then_inc(G["fact"], 1)
                    wait(pool, "ffn_c", 0)
                    wait(pool, "h_in", 64)
                    pool.tensor_tensor(hb[:], ht[:], V["bias"][:].unsqueeze(1).broadcast_to([P, BG, D]), ALU.add).then_inc(G["hb_d"], 1)
                    wait(pool, "stat", 2)
                    pool.tensor_tensor(sc[:, 3], sc[:, 2], V["mhalf"][:, 0:BG], ALU.pow).then_inc(G["fact"], 1)
                    for n in range(16):
                        wait(pool, "ex", n + 1)
                        pool.tensor_scalar(ee[:, n % 2], ee[:, n % 2], 1.0, None, ALU.min).then_inc(G["mn"], 1)
                        wait(pool, "rp", n + 1)
                        wait(pool, "sS", n // 2 - 1)
                        pool.tensor_tensor(rot[n % 2][:, (n // 2) % 2], ra[:, n % 2], rb[:, n % 2], ALU.add).then_inc(G["add_d"], 1)
                    for p in range(PAIRS):
                        wait(pool, "kd", p + 1)
                        wait(pool, "pvd", p + 1)
                        for hh in range(2):
                            ins = pool.tensor_tensor(uu[:, :, 2 * p + hh, 0:DH], uu[:, :, 2 * p + hh, 0:DH],
                                                     t1[:, p % 2, hh].rearrange("p (g d) -> p g d", g=BG), ALU.subtract)
                        ins.then_inc(G["ud"], 1)
                        wait(pool, "qd", p + 1)
                        for hh in range(2):
                            ins = pool.tensor_tensor(ol[:, :, 2 * p + hh, :], ol[:, :, 2 * p + hh, :],
                                                     t2[:, p % 2, hh].rearrange("p (g d) -> p g d", g=BG), ALU.add)
                        ins.then_inc(G["od"], 1)

                @block.tensor
                def _(pe):
                    wait(pe, "ydone", 0)
                    wait(pe, "xnn_d", 1)
                    for g in range(BG):
                        ins = pe.transpose(ps[:, 7, g * P:(g + 1) * P], xnn[:, g], V["ident"][:])
                    ins.then_inc(G["xt"], 1)
                    wait(pe, "xt_c", 1)
                    for n in range(8):
                        g, half = divmod(n, 2)
                        if n >= 4:
                            wait(pe, "v_a" if n % 2 == 0 else "v_d", n // 2 - 1)
                        pe.matmul(ps[:, n % 4, :], xT[:, g * P:(g + 1) * P], V["wqkv"][:, 2048 + 512 * half:2560 + 512 * half],
                                  start=True, stop=True).then_inc(G["vp"], 1)
                    wait(pe, "xq_d", 1)
                    qbank = ps[:, 6, 0:256].bitcast(BF16)
                    for g in range(BG):
                        ins = pe.transpose(qbank[:, g * P:(g + 1) * P], xq[:, g], V["ident_bf"][:])
                    ins.then_inc(G["xqt"], 1)
                    wait(pe, "v_a", 4)
                    wait(pe, "v_d", 4)
                    for n in range(20):
                        if n < 16:
                            which, p = n % 2, n // 2
                            wait(pe, "sg", n - 1)
                            pe.matmul(ps[:, 2 * (n % 2), :], V["wqkv"][:, 1024 * which + p * P:1024 * which + (p + 1) * P], xT[:], start=True, stop=True)
                            pe.matmul(ps[:, 2 * (n % 2) + 1, :], V["wqkv"][:, 3072 + 1024 * which + p * P:3072 + 1024 * which + (p + 1) * P], xT[:],
                                      start=True, stop=True).then_inc(G["pj"], 1)
                        if n == 1:
                            wait(pe, "xqt_c", 1)
                            for g in range(BG):
                                ins = pe.matmul(ps[:, 7, g * P:(g + 1) * P], xqT[:, g * P:(g + 1) * P], V["wq"][:], start=True, stop=True)
                            ins.then_inc(G["ffn"], 1)
                        if n >= 3 and n % 2 == 1 and (n - 3) // 2 < PAIRS:
                            p = (n - 3) // 2
                            wait(pe, "add_d", 2 * p + 2)
                            if p == 4:
                                wait(pe, "smask", 1)
                            for hh in range(2):
                                for g in range(BG):
                                    for f in range(B1):
                                        cols = slice(g * P + 32 * f, g * P + 32 * f + 32)
                                        at_ = (p % 4) * P + g * SEG
                                        ins = pe.matmul(ps[32 * f:32 * f + 32, 4 + hh, at_:at_ + SEG],
                                                        rot[0][64 * hh:64 * hh + 64, p % 2, cols], rot[1][64 * hh:64 * hh + 64, p % 2, cols],
                                                        start=True, stop=True)
                            ins.then_inc(G["sS"], 1)
                            wait(pe, "sg", 2 * p + 2)
                            wait(pe, "skc", p)
                            for g in range(BG):
                                ins = pe.transpose(ps[:, 6, g * P:(g + 1) * P], sigT[1][:, p, g * P:(g + 1) * P], V["ident"][:])
                            ins.then_inc(G["skt"], 1)
                    wait(pe, "skc", 8)
                    wait(pe, "smask", 2)
                    for n in range(PAIRS + 1):
                        if n < PAIRS:
                            p = n
                            wait(pe, "sg", 16)
                            for q in range(2):
                                wait(pe, ("qd", "kd")[q], (p, p + 1)[q])
                                for hh in range(2):
                                    for g in range(BG):
                                        for f in range(B1):
                                            ins = pe.matmul(ps[32 * f:32 * f + 32, hh, g * VE:(g + 1) * VE],
                                                            sigT[1 - q][64 * hh:64 * hh + 64, p, g * P + 32 * f:g * P + 32 * f + 32],
                                                            V["mem"][64 * hh:64 * hh + 64, p, 4 * g + f, :], start=True, stop=True)
                                ins.then_inc(G[("kr_s", "qr_s")[q]], 1)
                            wait(pe, "pt", p // 4 + 1)
                            wait(pe, "old", p)
                            for hh in range(2):
                                for g in range(BG):
                                    for f in range(B1):
                                        ins = pe.matmul(ps[32 * f:32 * f + 32, 6, (hh * BG + g) * DH:(hh * BG + g + 1) * DH],
                                                        pT[32 * f:32 * f + 32, p // 4, (hh * 4 + p % 4) * BG + g, :],
                                                        uu[32 * f:32 * f + 32, g, 2 * p + hh, 0:DH], start=True, stop=True)
                            ins.then_inc(G["pvd"], 1)
                        if n >= 1:
                            p = n - 1
                            wait(pe, "ud", p + 1)
                            for f in range(B1):
                                wait(pe, "mu", 4 * (p - 1) + f + 1 if p else 0)
                                for g in range(BG):
                                    for hh in range(2):
                                        ins = pe.matmul(ps[64 * hh:64 * hh + 64, 2 + f, g * VE:(g + 1) * VE],
                                                        skN[32 * f:32 * f + 32, g, p * P + 64 * hh:p * P + 64 * hh + 64],
                                                        uu[32 * f:32 * f + 32, g, 2 * p + hh, :], start=True, stop=True)
                                ins.then_inc(G["up"], 1)
                    wait(pe, "od", PAIRS)
                    wait(pe, "kd", PAIRS)
                    wait(pe, "qd", PAIRS)
                    wait(pe, "ffn_c", 1)
                    wait(pe, "mu", 4 * PAIRS)
                    for n in range(BG + 1):
                        if n < BG:
                            g = n
                            wait(pe, "otc_a", g - 1)
                            wait(pe, "otc_d", g - 1)
                            for p in range(PAIRS):
                                ins = pe.transpose(ps[:, 2 * (g % 2) + p // 4, (p % 4) * P:(p % 4 + 1) * P],
                                                   ol[:, g, 2 * p:2 * p + 2, :].rearrange("p h d -> p (h d)"), V["ident"][:])
                            ins.then_inc(G["ott"], 1)
                        if n >= 1:
                            g = n - 1
                            wait(pe, "otc_a", g + 1)
                            wait(pe, "otc_d", g + 1)
                            for p in range(PAIRS):
                                ins = pe.matmul(ps[:, 7, g * P:(g + 1) * P], oT[:, g % 2, p], V["wout"][:, p], start=(p == 0), stop=(p == PAIRS - 1))
                    ins.then_inc(G["oproj"], 1)

                @block.scalar
                def _(act):
                    wait(act, "xt", 1)
                    act.activation(xT[:], ps[:, 7, :], ACT.Identity, bias=V["b"][:, 0:1], scale=V["g"][:, 0:1]).then_inc(G["xt_c"], 1)
                    for n in range(0, 8, 2):
                        wait(act, "vp", n + 1)
                        act.copy(uu[:, n // 2, 0:8, 0:DH], ps[:, n % 4, :].rearrange("p (h d) -> p h d", d=DH)).then_inc(G["v_a"], 1)
                    wait(act, "xqt", 1)
                    act.copy(xqT[:], ps[:, 6, 0:256].bitcast(BF16)).then_inc(G["xqt_c"], 1)
                    for n in range(22):
                        if n < 16:
                            wait(act, "pj", n + 1)
                            wait(act, "sg", n - 1)
                            act.activation(ee[:, n % 2], ps[:, 2 * (n % 2), :], ACT.Exp).then_inc(G["ex"], 1)
                        if n >= 4 and n % 2 == 0 and (n - 4) // 2 < PAIRS:
                            p = (n - 4) // 2
                            wait(act, "skt", p + 1)
                            act.copy(skN[:, :, pair_cols(p)], ps[:, 6, :].rearrange("p (g r) -> p g r", g=BG)).then_inc(G["skc"], 1)
                        if n in (12, 21):
                            hf = (n - 12) // 9
                            wait(act, "sx", hf + 1)
                            act.activation(ss[:], ss[:], ACT.Exp).then_inc(G["se"], 1)
                    for g in range(BG):
                        wait(act, "ott", g + 1)
                        act.copy(oT[:, g % 2, 0:4].rearrange("p a b -> p (a b)"), ps[:, 2 * (g % 2), :]).then_inc(G["otc_a"], 1)

                @block.vector
                def _(dve):
                    n_ = [0]

                    def link(ins):
                        n_[0] += 1
                        ins.then_inc(G["step"], 1)
                        wait(dve, "step", n_[0])

                    def normalize(dst, src, k, done):
                        for g in range(BG):
                            ins = dve.bn_stats(st[:, g], src[:, g])
                        link(ins)
                        for g in range(BG):
                            ins = dve.bn_aggr(mv[:, g], st[:, g])
                        link(ins)
                        dve.tensor_scalar(sc[:, 2 * k], mv[:, :, 1], 1e-5, None, ALU.add).then_inc(G["stat"], 1)
                        wait(dve, "fact", k + 1)
                        for g in range(BG):
                            ins = dve.tensor_scalar(dst[:, g], src[:, g], mv[:, g, 0:1], sc[:, 2 * k + 1, g:g + 1], ALU.subtract, ALU.mult)
                        ins.then_inc(G[done], 1)

                    wait(dve, "h_in", 64)
                    normalize(xn, ht, 0, "xn_d")
                    wait(dve, "xn_d", 1)
                    normalize(xnn, xn, 1, "xnn_d")
                    quantize(dve, link, flat(xq[:]), flat(xn[:]), V["qs"][:, 0:1], flat(tq[:]), flat(mq[:])).then_inc(G["xq_d"], 1)
                    for n in range(1, 8, 2):
                        wait(dve, "vp", n + 1)
                        dve.tensor_copy(uu[:, n // 2, 8:16, 0:DH], ps[:, n % 4, :].rearrange("p (h d) -> p h d", d=DH)).then_inc(G["v_d"], 1)

                    by_head = lambda ap: ap.rearrange("p (h g) -> p h g", g=BG)

                    def softmax(hf):
                        wait(dve, "sS", 4 * hf + 4)
                        dve.tensor_tensor(ss[:], ps[:, 4:6, :].rearrange("p b (c j) -> p (b c) j", j=SEG),
                                          V["mask"][:].unsqueeze(1).broadcast_to([P, HC, SEG]), ALU.add).then_inc(G["smask"], 1)
                        wait(dve, "smask", hf + 1)
                        link(dve.tensor_reduce(mx[:], ss[:], AX.X, ALU.max))
                        dve.tensor_tensor(ss[:], ss[:], bc(mx[:], SEG), ALU.subtract).then_inc(G["sx"], 1)

                    def softmax_end(hf):
                        wait(dve, "se", hf + 1)
                        dve.transpose(pT[:, hf].rearrange("p c j -> p (c j)"), ss[:].rearrange("p c j -> p (c j)"))
                        link(dve.tensor_reduce(sm[:, hf], ss[:], AX.X, ALU.add))
                        link(dve.reciprocal(sm[:, hf], sm[:, hf]))
                        for hh in range(2):
                            share = by_head(sm[:, hf])[:, 4 * hh:4 * hh + 4]
                            ins = dve.tensor_tensor(share, share, bc(V["rest"][:, 8 * hf + hh:8 * hf + 8:2], BG), ALU.mult)
                        ins.then_inc(G["pt"], 1)

                    by_pos = lambda ap: ap.rearrange("p (n i) -> p n i", i=SEG)
                    table = lambda name, q: V[name][:, q].unsqueeze(1).broadcast_to([P, S // SEG, SEG])
                    for n in range(21):
                        if n < 16:
                            wait(dve, "pj", n + 1)
                            wait(dve, "add_d", n - 1)
                            dve.tensor_tensor(by_pos(rb[:, n % 2]), by_pos(ps[:, 2 * (n % 2) + 1, :]), table("sin", n % 2), ALU.mult)
                            wait(dve, "ex", n + 1)
                            dve.tensor_tensor(by_pos(ra[:, n % 2]), by_pos(ps[:, 2 * (n % 2), :]), table("cos", n % 2), ALU.mult).then_inc(G["rp"], 1)
                            wait(dve, "mn", n + 1)
                            dve.scalar_tensor_tensor(sigT[n % 2][:, n // 2], ps[:, 2 * (n % 2), :], 1.0, ee[:, n % 2], ALU.add, ALU.max).then_inc(G["sg"], 1)
                        if n == 2:
                            wait(dve, "ffn", 1)
                            wait(dve, "hb_d", 1)
                            wait(dve, "stored", 0)
                            dve.scalar_tensor_tensor(flat(y[:]), ps[:, 7, :], V["qs"][:, 4:5], flat(hb[:]), ALU.mult, ALU.add).then_inc(G["ffn_c"], 1)
                        if n == 11:
                            softmax(0)
                        if n == 13:
                            softmax_end(0)
                        if n == 19:
                            softmax(1)
                        if n == 20:
                            softmax_end(1)
                    for n in range(PAIRS + 1):
                        if n < PAIRS:
                            p = n
                            for q in range(2):
                                den = ps[:, 0:2, 0:BG * VE].rearrange("p h (g v) -> p h g v", v=VE)
                                r, tile = (rk, rq)[q], (t1, t2)[q]
                                wait(dve, ("kr_s", "qr_s")[q], p + 1)
                                if q == 1:
                                    link(dve.tensor_scalar(r[:], den[:, :, :, DH], 1e-6, None, ALU.add))
                                    link(dve.reciprocal(r[:], r[:]))
                                    link(dve.tensor_tensor(r[:], r[:], bc(V["beta"][:, 2 * p:2 * p + 2], BG), ALU.mult))
                                else:
                                    link(dve.reciprocal(r[:], den[:, :, :, DH]))
                                wait(dve, ("ud", "od")[q], p - 1)
                                for hh in range(2):
                                    ins = dve.tensor_tensor(tile[:, p % 2, hh].rearrange("p (g d) -> p g d", g=BG), den[:, hh, :, 0:DH],
                                                            bc(r[:, hh], DH), ALU.mult)
                                ins.then_inc(G[("kd", "qd")[q]], 1)
                                if q == 0:
                                    wait(dve, "pvd", p + 1)
                                    wait(dve, "pt", 2)
                                    for hh in range(2):
                                        ins = dve.tensor_tensor(ol[:, :, 2 * p + hh, :], ps[:, 6, hh * 256:hh * 256 + 256].rearrange("p (g d) -> p g d", g=BG),
                                                                bc(by_head(sm[:, p // 4])[:, hh * 4 + p % 4, :], DH), ALU.mult)
                                    ins.then_inc(G["old"], 1)
                                    wait(dve, "old", p + 1)
                        if n >= 1:
                            p = n - 1
                            for f in range(B1):
                                wait(dve, "up", 4 * p + f + 1)
                                m = V["mem"][:, p, f::B1, :]
                                dve.tensor_tensor(m, m, ps[:, 2 + f, 0:BG * VE].rearrange("p (g v) -> p g v", g=BG), ALU.add).then_inc(G["mu"], 1)
                    for g in range(BG):
                        wait(dve, "ott", g + 1)
                        dve.tensor_copy(oT[:, g % 2, 4:8].rearrange("p a b -> p (a b)"), ps[:, 2 * (g % 2) + 1, :]).then_inc(G["otc_d"], 1)
                    wait(dve, "oproj", 1)
                    dve.tensor_tensor(flat(y[:]), flat(y[:]), ps[:, 7, :], ALU.add).then_inc(G["ydone"], 1)


def block1_tensors(nc, ctx):
    sb = lambda n, s, d=F32: ctx.enter_context(nc.sbuf_tensor("v_" + n, s, d))
    shapes = dict(wqkv=[P, 5120], wout=[P, PAIRS, D], g=[P, 1], b=[P, 1], bias=[P, D], beta=[P, H], rest=[P, H],
                  ident=[P, P], cos=[P, 2, SEG], sin=[P, 2, SEG], mask=[P, SEG], qs=[P, 5], mem=[P, PAIRS, NB, VE],
                  uu=[P, BG, H, VE], mhalf=[P, BG])
    V = {n: sb(n, s) for n, s in shapes.items()}
    V["wq"], V["ident_bf"] = sb("wq", [P, D], BF16), sb("ident_bf", [P, P], BF16)
    return V


def weights(nc, ctx):
    sb = lambda n, s, d=F32: ctx.enter_context(nc.sbuf_tensor("w_" + n, s, d))
    shapes = dict(wqA=[P, D], mk=[P, D], mv=[P, D], woA=[P, D], woB=[P, D], wB=[P, 5 * D], ident=[P, P],
                  decay=[P, NC, S], cmask=[P, S], hmask=[P, 2 * H], cosA=[P, S], sinA=[P, S], g2b=[P, D], wr=[P, E],
                  vA=[P, NC, H, 32], vB=[P, NC, H, 32], mhalf=[P, 64])
    return {n: sb(n, s) for n, s in shapes.items()}


def shape_constants():
    f32 = np.float32
    pos = np.arange(S, dtype=f32)
    d = np.exp(f32(-0.01 * 0.01) * np.abs(pos[:, None] - pos[None, :])).astype(f32)
    decay = d.reshape(NC, P, S).transpose(1, 0, 2).copy()
    cmask = np.zeros((P, S), f32)
    cmask[:, S - P:] = np.where(np.arange(P)[None, :] <= np.arange(P)[:, None], 0.0, MASKED)
    own = (np.arange(P)[:, None] // HD == np.arange(H)[None, :])
    hmask = np.concatenate([own * f32(SCALE_A), own * f32(SCALE_B)], 1).astype(f32)
    theta = (f32(10000.0) ** (f32(-2.0) * (np.arange(HD // 2, dtype=f32) / HD))).astype(f32)
    ang = (pos[:, None] * theta[None, :]).astype(f32)
    row = (np.arange(P) % HD) // 2
    sign = np.where(np.arange(P) % 2 == 0, -1.0, 1.0).astype(f32)
    cosA = np.cos(ang)[:, row].T.astype(f32)
    sinA = (np.sin(ang)[:, row].T * sign[:, None]).astype(f32)
    seq = np.arange(P)
    low = np.broadcast_to((np.arange(E)[None, :] < np.arange(E)[:, None]).reshape(1, E * E), (P, E * E)).astype(f32)
    restart = np.broadcast_to((np.arange(E * NT) % NT != 0).astype(f32)[None], (P, E * NT)).copy()
    slots = np.broadcast_to((np.arange(E * CAP) % CAP).astype(f32)[None], (P, E * CAP)).copy()
    ptid = np.stack([np.broadcast_to(seq[:, None], (P, NT)), np.broadcast_to(np.arange(NT)[None], (P, NT))], 2)
    route = dict(low=low, before=(seq[:, None] < seq[None, :]).astype(f32), restart=restart, slots=slots,
                 ptid=ptid.reshape(P, 2 * NT).astype(f32), mix=np.array([[1, NT], [P, 1]], f32))
    freqs = f32(10000.0) ** (-np.arange(0, DH, 2, dtype=f32) / f32(DH))
    ang1 = (np.arange(SEG, dtype=f32)[:, None] * freqs[None, :]).astype(f32)
    row1, sign1 = (seq % DH) // 2, np.where(seq % 2 == 0, -1.0, 1.0).astype(f32)
    cos1 = np.cos(ang1)[:, row1].T.astype(f32)
    sin1 = (np.sin(ang1)[:, row1].T * sign1[:, None]).astype(f32)
    per_side = lambda t: np.stack([t * f32(DH ** -0.5), t], 1).copy()
    i, j = np.arange(P)[:, None] % SEG, np.arange(SEG)[None, :]
    scan = dict(cos1=per_side(cos1), sin1=per_side(sin1), mask1=np.where(j <= i, 0.0, MASKED).astype(f32))
    return dict(**route, **scan, ident=np.eye(P, dtype=f32), decay=decay, cmask=cmask, hmask=hmask, cosA=cosA.copy(), sinA=sinA.copy())


def inputs_of(a):
    c = dict(
        x=a["L0_attn_x"], Wq=a["L0_attn_Wq"], Wk=a["L0_attn_Wk"], Wv=a["L0_attn_Wv"], WoA=a["L0_attn_Wo"],
        Wdown=a["L0_attn_W_down_kv"], Wuk=a["L0_attn_W_up_k"], Wuv=a["L0_attn_W_up_v"],
        g1=a["L0_ffn_g1"].reshape(P, 1), Wqkv=a["L0_ffn_w_qkv"], WoB=a["L0_ffn_w_o"],
        g2b=np.broadcast_to(a["L0_ffn_g2"].reshape(1, D), (P, D)), Wr=a["L0_ffn_w_router"], w1=a["L0_ffn_w1"], w2=a["L0_ffn_w2"],
        w1qkv=a["L1_attn_w_qkv"], wout=a["L1_attn_w_out"], ln_g=a["L1_attn_ln_g"].reshape(P, 1), ln_b=a["L1_attn_ln_b"].reshape(P, 1),
        beta=np.broadcast_to(a["L1_attn_mem_beta"].reshape(1, H), (P, H)), wffn=a["L1_ffn_weight"],
        bias=np.broadcast_to(a["L1_ffn_bias"].reshape(1, D), (P, D)))
    c.update(shape_constants())
    return c


def program(nc, c):
    c["h_d"] = nc.dram_tensor("h_scratch", (NB, S, D), F32, kind="Internal").ap()
    c["xf_d"] = nc.dram_tensor("xf_scratch", (NB, S, D), F32, kind="Internal").ap()
    c["pr_d"] = nc.dram_tensor("pr_scratch", (P, NB, NC, E), F32, kind="Internal").ap()
    c["gate_d"] = nc.dram_tensor("gate_scratch", (NT * P, E), F32, kind="Internal").ap()
    with ExitStack() as ctx:
        W = weights(nc, ctx)
        R = {"rows": ctx.enter_context(nc.sbuf_tensor("rows", [P, 2 * E, 2], U32))}
        fold_weights(nc, c, W)
        attend(nc, c, W, NB)
        route(nc, c, W, R)
        experts(nc, c, W, R)
    with ExitStack() as ctx:
        V = block1_tensors(nc, ctx)
        scale_factors(nc, c, V)
        scan(nc, c, V, c["out"], NSEG)


def kernel(**inputs):
    import concourse.bacc as _bacc
    from concourse.bass_utils import run_bass_kernel_spmd as _run

    nc = _bacc.Bacc("TRN2", target_bir_lowering=False, num_devices=1)
    arrays, c = {}, {}
    for name, a in inputs_of({k: np.asarray(v) for k, v in inputs.items()}).items():
        a = np.ascontiguousarray(a)
        arrays["in_" + name] = a
        c[name] = nc.dram_tensor("in_" + name, a.shape, mybir.dt.from_np(a.dtype), kind="ExternalInput").ap()
    c["out"] = nc.dram_tensor("out_dram", (NB, S, D), F32, kind="ExternalOutput").ap()
    program(nc, c)
    return _run(nc, [arrays], core_ids=[0]).results[0]["out_dram"]
```

```python
from contextlib import ExitStack

import numpy as np
import concourse.bass as bass
from concourse import mybir

F32 = mybir.dt.float32
BF16 = mybir.dt.bfloat16
I32 = mybir.dt.int32
U32 = mybir.dt.uint32
ALU = mybir.AluOpType
ACT = mybir.ActivationFunctionType
AX = mybir.AxisListType

P = 128
NB, S, D = 16, 512, 128
NC = S // P
NT = NB * S // P
H, HD = 16, 8
NG = H // 4
E, TOPK, FF = 8, 2, 256
CAP = 160
HALF = CAP // 2
CLAMP = 10000.0
SCALE_A = float(1.0 / (np.sqrt(np.float32(128.0)) + 1e-8))
SCALE_B = float(1.0 / np.sqrt(np.float32(HD)))
UNITS = H * NC
MASKED = -1e30


def bc(ap, n):
    return ap.unsqueeze(len(ap.shape)).broadcast_to(list(ap.shape) + [n])


def clear(nc, sems):
    nums = sorted(s.num for s in sems)
    starts = [n for n in nums if n - 1 not in nums]
    ends = [n + 1 for n in nums if n + 1 not in nums]
    for a, b in zip(starts, ends):
        nc.sync.sem_clear(range(a, b))
    nc.all_engine_barrier()


def fold_weights(nc, c, W):
    with ExitStack() as ctx:
        sb = lambda n, s, d=F32: ctx.enter_context(nc.sbuf_tensor(n, s, d))
        sem = lambda n: ctx.enter_context(nc.semaphore(n))
        wk, wv, wsum, wsumT = sb("fw_k", [P, D]), sb("fw_v", [P, D]), sb("fw_s", [P, D]), sb("fw_sT", [P, D])
        wd, wuk, wuv = sb("fw_d", [P, 32]), sb("fw_uk", [32, D]), sb("fw_uv", [32, D])
        bT = sb("fw_bT", [32, D])
        wqkv, wqkv_g, g1 = sb("fw_qkv", [P, 3 * D]), sb("fw_qkv_g", [P, 3 * D]), sb("fw_g1", [P, 1])
        wq, cmaskT = sb("fw_q", [P, D]), sb("fw_cmaskT", [P, P])
        ps = ctx.enter_context(nc.psum_tensor("fw_ps", [P, 4, 512], F32))
        s_in, s_sum, s_pe, s_cp = sem("fw_in"), sem("fw_sum"), sem("fw_pe"), sem("fw_cp")
        block = ctx.enter_context(nc.Block())
        loads = [(wk, c["Wk"]), (wv, c["Wv"]), (wd, c["Wdown"]), (wuk, c["Wuk"]), (wuv, c["Wuv"]),
                 (wqkv, c["Wqkv"]), (g1, c["g1"]), (wq, c["Wq"]), (W["woA"], c["WoA"]), (W["woB"], c["WoB"]),
                 (W["ident"], c["ident"]), (W["hsum"], c["hsum"]), (cmaskT, c["cmaskT"]),
                 (W["decay"], c["decay"]), (W["cmask"], c["cmask"]), (W["g2b"], c["g2b"]), (W["wr"], c["Wr"])]
        by_head = lambda ap: ap.rearrange("p (h d) -> p h d", d=HD)
        by_feature = lambda ap: ap.rearrange("p (d h) -> p h d", d=HD)

        @block.sync
        def _(sp):
            for dst, src in loads:
                sp.dma_start(dst[:], src).then_inc(s_in, 16)

        @block.vector
        def _(dve):
            dve.wait_ge(s_in, 16 * len(loads))
            dve.tensor_tensor(wsum[:], wk[:], wv[:], ALU.add).then_inc(s_sum, 1)
            dve.tensor_scalar(wqkv_g[:], wqkv[:], g1[:, 0:1], None, ALU.mult).then_inc(s_sum, 1)
            dve.tensor_copy(by_feature(W["wqA"][:]), by_head(wq[:]))
            dve.tensor_copy(W["ident_bf"][:], W["ident"][:])
            dve.tensor_copy(W["cmaskT"][:], cmaskT[:])
            dve.memset(W["mhalf"][:], -0.5)
            dve.wait_ge(s_sum, 2)
            dve.tensor_copy(W["wB"][:, 2 * D:3 * D], wqkv_g[:, 2 * D:3 * D])
            for t in range(2):
                src = by_head(wqkv_g[:, t * D:(t + 1) * D])
                dve.tensor_copy(by_feature(W["wB"][:, t * D:(t + 1) * D]), src)
                pairs = src.rearrange("p h (n two) -> p h n two", two=2)
                dst = by_feature(W["wB"][:, (3 + t) * D:(4 + t) * D]).rearrange("p h (n two) -> p h n two", two=2)
                dve.tensor_copy(dst[:, :, :, 0], pairs[:, :, :, 1])
                dve.tensor_copy(dst[:, :, :, 1], pairs[:, :, :, 0])
            dve.wait_ge(s_pe, 1)
            dve.tensor_copy(wsumT[:], ps[:, 0, 0:D]).then_inc(s_cp, 1)
            dve.wait_ge(s_pe, 2)
            dve.tensor_copy(bT[:], ps[0:32, 1, 0:D]).then_inc(s_cp, 1)
            dve.wait_ge(s_pe, 4)
            dve.tensor_copy(by_feature(W["mk"][:]), by_head(ps[:, 2, 0:D]))
            dve.tensor_copy(W["mv"][:], ps[:, 3, 0:D]).then_inc(s_cp, 1)
            dve.wait_ge(s_cp, 3)

        @block.tensor
        def _(pe):
            pe.wait_ge(s_sum, 1)
            pe.transpose(ps[:, 0, 0:D], wsum[:], W["ident"][:]).then_inc(s_pe, 1)
            pe.wait_ge(s_cp, 1)
            pe.matmul(ps[0:32, 1, 0:D], wd[:], wsumT[:], start=True, stop=True).then_inc(s_pe, 1)
            pe.wait_ge(s_cp, 2)
            pe.matmul(ps[:, 2, 0:D], bT[:], wuk[:], start=True, stop=True).then_inc(s_pe, 1)
            pe.matmul(ps[:, 3, 0:D], bT[:], wuv[:], start=True, stop=True).then_inc(s_pe, 1)


VW = H * (HD + 1) + 32
ROWS = 9 * HD
LIMIT = 64.0


def front(nc, c, W, nb, K=2):
    with ExitStack() as ctx:
        sb = lambda n, s, d=F32: ctx.enter_context(nc.sbuf_tensor("fr_" + n, s, d))
        sems = []

        def sem(n):
            sems.append(ctx.enter_context(nc.semaphore("fr_" + n)))
            return sems[-1]

        x, xn, hn = sb("x", [P, K, NC, D]), sb("xn", [P, K, NC, D]), sb("hn", [P, K, NC, D])
        st, mv, sc = sb("st", [P, K, NC, 6]), sb("mv", [P, K, NC, 2]), sb("sc", [P, K, 5, NC])
        xnT, hnT = sb("xnT", [P, K, S]), sb("hnT", [P, K, S])
        r = sb("r", [P, K, 4, S])
        qk = sb("qk", [P, K, 4, S])
        sq = sb("sq", [P, K, 2, S])
        res = sb("res", [P, K, 4, S])
        parts = sb("parts", [P, K, 4, 3, S], BF16)
        v = sb("v", [P, K, 2, NC, VW])
        rope = sb("rope", [P, 4, S])
        rope_in = ctx.enter_context(nc.semaphore("fr_rope_in"))
        ps = ctx.enter_context(nc.psum_tensor("fr_ps", [P, 8, 512], F32))
        x_in, stats, factors, normed, v_step, p_step = (sem(n) for n in "x_in stats factors normed v_step p_step".split())
        turned, turned_cp, pa, qa_cp, ka_cp, va_cp = (sem(n) for n in "turned turned_cp pa qa_cp ka_cp va_cp".split())
        pb, roped_ps, roped, vb_cp, squared, normsq, nmax = (sem(n) for n in "pb roped_ps roped vb_cp squared normsq nmax".split())
        part1, rest1, part2, part3, stored, ones_set = (sem(n) for n in "part1 rest1 part2 part3 stored ones_set".split())

        with nc.Block() as block:

            @block.sync
            def _(sp):
                sp.dma_start(rope[:], c["rope"]).then_inc(rope_in, 16)
                sp.wait_ge(rope_in, 16)

        with nc.Fori(0, nb // K) as i:
            clear(nc, sems)
            with nc.Block() as block:

                @block.sync
                def _(sp):
                    for k in range(K):
                        sp.dma_start(x[:, k], c["x"][bass.ds(i * K + k, 1)].rearrange("o (c p) d -> p (o c) d", p=P)).then_inc(x_in, 16)
                    n = 0
                    for k in range(K):
                        sp.wait_ge(normed, k + 1)
                        sp.dma_start(c["xn_d"][bass.ds(i * K + k, 1)].rearrange("o (c p) d -> p (o c) d", p=P), xn[:, k]).then_inc(stored, 16)
                        n += 1
                    for k in range(K):
                        for a in range(2):
                            sp.wait_ge((va_cp, vb_cp)[a], k + 1)
                            sp.dma_start(c["v_d"][bass.ds((i * K + k) * 2 + a, 1)].rearrange("o p f -> p (o f)"),
                                         v[:, k, a].rearrange("p c f -> p (c f)")).then_inc(stored, 16)
                            n += 1
                    for k in range(K):
                        for t in range(4):
                            sp.wait_ge(part3, 4 * k + t + 1)
                            dst = c["parts_d"][bass.ds((i * K + k) * 4 + t, 1)].rearrange("o s p f -> p (o s) f")
                            sp.dma_start(dst[:, 0:3], parts[:, k, t]).then_inc(stored, 16)
                            n += 1
                            if t % 2 == 0:
                                sp.dma_start(dst[:, 3:5], parts[:, k, t, 0:2]).then_inc(stored, 16)
                                n += 1
                    sp.wait_ge(stored, 16 * n)

                @block.gpsimd
                def _(pool):
                    step = [0]

                    def link(ins):
                        step[0] += 1
                        ins.then_inc(p_step, 1)
                        pool.wait_ge(p_step, step[0])

                    pool.memset(v[:], 1.0).then_inc(ones_set, 1)
                    for k in range(K):
                        s_ = sc[:, k]
                        pool.wait_ge(stats, k + 1)
                        link(pool.tensor_scalar(s_[:, 0], mv[:, k, :, 1], 1e-5, None, ALU.add))
                        link(pool.tensor_tensor(s_[:, 1], s_[:, 0], W["mhalf"][:, 0:NC], ALU.pow))
                        link(pool.tensor_tensor(s_[:, 2], mv[:, k, :, 1], s_[:, 1], ALU.mult))
                        link(pool.tensor_tensor(s_[:, 2], s_[:, 2], s_[:, 1], ALU.mult))
                        link(pool.tensor_scalar(s_[:, 2], s_[:, 2], 1e-6, None, ALU.add))
                        link(pool.tensor_tensor(s_[:, 3], s_[:, 2], W["mhalf"][:, 0:NC], ALU.pow))
                        pool.tensor_tensor(s_[:, 4], s_[:, 1], s_[:, 3], ALU.mult).then_inc(factors, 1)

                    def split(k, t):
                        pool.wait_ge(part1, 4 * k + t + 1)
                        pool.tensor_tensor(res[:, k, t], qk[:, k, t], parts[:, k, t, 0], ALU.subtract).then_inc(rest1, 1)
                        pool.wait_ge(part2, 4 * k + t + 1)
                        pool.tensor_tensor(parts[:, k, t, 2], res[:, k, t], parts[:, k, t, 1], ALU.subtract).then_inc(part3, 1)

                    for k in range(K):
                        pool.wait_ge(qa_cp, k + 1)
                        pool.wait_ge(ka_cp, k + 1)
                        for t in range(2):
                            ins = pool.tensor_tensor(sq[:, k, t], qk[:, k, t], qk[:, k, t], ALU.mult)
                        ins.then_inc(squared, 1)
                        split(k, 0)
                        split(k, 1)
                        for t in range(2):
                            pool.wait_ge(roped_ps, 4 * k + 2 * t + 2)
                            pool.tensor_tensor(qk[:, k, 2 + t], r[:, k, 2 * t], r[:, k, 2 * t + 1], ALU.add).then_inc(roped, 1)
                        split(k, 2)
                        split(k, 3)

                @block.tensor
                def _(pe):
                    for k in range(K):
                        B = 4 * k
                        pe.wait_ge(normed, k + 1)
                        for n in range(2):
                            for j in range(NC):
                                ins = pe.transpose(ps[:, B + n, j * P:(j + 1) * P], (xn, hn)[n][:, k, j, :], W["ident"][:])
                            ins.then_inc(turned, 1)
                    for k in range(K):
                        B = 4 * k
                        pe.wait_ge(turned_cp, 2 * k + 1)
                        pe.matmul(ps[:, B + 2, :], W["wqA"][:], xnT[:, k], start=True, stop=True).then_inc(pa, 1)
                        pe.matmul(ps[:, B + 3, :], W["mk"][:], xnT[:, k], start=True, stop=True).then_inc(pa, 1)
                        for j in range(NC):
                            ins = pe.matmul(ps[:, B, j * P:(j + 1) * P], xnT[:, k, j * P:(j + 1) * P], W["mv"][:], start=True, stop=True)
                        ins.then_inc(pa, 1)
                    for k in range(K):
                        B = 4 * k
                        pe.wait_ge(turned_cp, 2 * k + 2)
                        waits = ((turned_cp, 2 * k + 2), (qa_cp, k + 1), (ka_cp, k + 1), (va_cp, k + 1))
                        for n, col in enumerate((0, 3, 1, 4)):
                            pe.wait_ge(*waits[n])
                            pe.matmul(ps[:, B + (n + 1) % 4, :], W["wB"][:, col * D:(col + 1) * D], hnT[:, k], start=True, stop=True).then_inc(pb, 1)
                        pe.wait_ge(roped_ps, 4 * k + 1)
                        for j in range(NC):
                            ins = pe.matmul(ps[:, B + 1, j * P:(j + 1) * P], hnT[:, k, j * P:(j + 1) * P], W["wB"][:, 2 * D:3 * D], start=True, stop=True)
                        ins.then_inc(pb, 1)
                    for k in range(K):
                        pe.wait_ge(squared, k + 1)
                        pe.wait_ge(roped_ps, 4 * k + 4)
                        pe.matmul(ps[0:H, 4 * k + 2, :], W["hsum"][:], sq[:, k, 0], start=True, stop=True)
                        pe.matmul(ps[0:H, 4 * k + 3, :], W["hsum"][:], sq[:, k, 1], start=True, stop=True).then_inc(normsq, 1)

                @block.scalar
                def _(act):
                    for k in range(K):
                        for n in range(2):
                            act.wait_ge(turned, 2 * k + n + 1)
                            act.copy((xnT, hnT)[n][:, k], ps[:, 4 * k + n, :]).then_inc(turned_cp, 1)
                    heads = lambda bank: ps[:, bank, :].rearrange("p (c h d) -> p c h d", c=NC, d=HD)
                    values = lambda k, a: v[:, k, a, :, 0:H * (HD + 1)].rearrange("p c (h e) -> p c h e", e=HD + 1)[:, :, :, 0:HD]
                    act.wait_ge(ones_set, 1)
                    for k in range(K):
                        act.wait_ge(pa, 3 * k + 1)
                        act.mul(qk[:, k, 0], ps[:, 4 * k + 2, :], SCALE_A).then_inc(qa_cp, 1)
                        act.wait_ge(pa, 3 * k + 3)
                        for j in range(NC):
                            ins = act.copy(values(k, 0)[:, j], heads(4 * k)[:, j])
                        ins.then_inc(va_cp, 1)
                    for k in range(K):
                        act.wait_ge(qa_cp, k + 1)
                        act.copy(parts[:, k, 0, 0], qk[:, k, 0]).then_inc(part1, 1)
                        act.wait_ge(ka_cp, k + 1)
                        act.copy(parts[:, k, 1, 0], qk[:, k, 1]).then_inc(part1, 1)
                        act.wait_ge(pb, 5 * k + 5)
                        for j in range(NC):
                            ins = act.copy(values(k, 1)[:, j], heads(4 * k + 1)[:, j])
                        ins.then_inc(vb_cp, 1)
                        for t in range(2):
                            act.wait_ge(roped, 2 * k + t + 1)
                            act.copy(parts[:, k, 2 + t, 0], qk[:, k, 2 + t]).then_inc(part1, 1)

                @block.vector
                def _(dve):
                    step = [0]

                    def link(ins):
                        step[0] += 1
                        ins.then_inc(v_step, 1)
                        dve.wait_ge(v_step, step[0])

                    dve.wait_ge(x_in, 16 * K)
                    for k in range(K):
                        for j in range(NC):
                            ins = dve.bn_stats(st[:, k, j], x[:, k, j, :])
                    link(ins)
                    for k in range(K):
                        for j in range(NC):
                            ins = dve.bn_aggr(mv[:, k, j], st[:, k, j])
                        ins.then_inc(stats, 1)
                    for k in range(K):
                        dve.wait_ge(factors, k + 1)
                        for j in range(NC):
                            dve.tensor_scalar(xn[:, k, j], x[:, k, j], mv[:, k, j, 0:1], sc[:, k, 1, j:j + 1], ALU.subtract, ALU.mult)
                        for j in range(NC):
                            ins = dve.tensor_scalar(hn[:, k, j], x[:, k, j], mv[:, k, j, 0:1], sc[:, k, 4, j:j + 1], ALU.subtract, ALU.mult)
                        ins.then_inc(normed, 1)
                    for k in range(K):
                        dve.wait_ge(pa, 3 * k + 2)
                        dve.tensor_copy(qk[:, k, 1], ps[:, 4 * k + 3, :]).then_inc(ka_cp, 1)

                    def second(k, t):
                        dve.wait_ge(rest1, 4 * k + t + 1)
                        dve.tensor_copy(parts[:, k, t, 1], res[:, k, t]).then_inc(part2, 1)

                    for k in range(K):
                        for n in range(4):
                            dve.wait_ge(pb, 5 * k + n + 1)
                            dve.tensor_tensor(r[:, k, n], ps[:, 4 * k + (n + 1) % 4, :], rope[:, n], ALU.mult).then_inc(roped_ps, 1)
                        for t in range(4):
                            second(k, t)
                    for k in range(K):
                        dve.wait_ge(normsq, k + 1)
                        for t in range(2):
                            ins = dve.tensor_reduce(W["nmax"][:, bass.ds(i * (2 * K) + 2 * k + t, 1)], ps[0:H, 4 * k + 2 + t, :], AX.X, ALU.max)
                        ins.then_inc(nmax, 1)
                    dve.wait_ge(nmax, K)


def attend(nc, c, W, nb):
    with ExitStack() as ctx:
        sb = lambda n, s, d=F32: ctx.enter_context(nc.sbuf_tensor("at_" + n, s, d))
        sems = []

        def sem(n):
            sems.append(ctx.enter_context(nc.semaphore("at_" + n)))
            return sems[-1]

        KB = 2
        aq, ak = sb("aq", [ROWS, 2, 4, S], BF16), sb("ak", [ROWS, 2, 4, S], BF16)
        B_GROUPS = 6
        bq, bk = sb("bq", [ROWS + 3, 4 * B_GROUPS, S], BF16), sb("bk", [ROWS + 3, 4 * B_GROUPS, S], BF16)
        b_slot = lambda bb, h: (4 * bb + h // 4) % B_GROUPS * 4 + h % 4
        v = sb("v", [P, KB, 2, NC, VW])
        RING, B_WIDE = {"A": 8, "T": 6}, S * (NC + 1) // 2
        pT = {"A": sb("pA", [P, RING["A"], NC * S]), "T": sb("pB", [P, RING["T"], B_WIDE])}
        junk = sb("junk", [P, B_WIDE])
        mx = sb("mx", [P, KB, 4 * H])
        neg, res = sb("neg", [16, 2, P]), sb("res", [16, 2, P])
        mrow = sb("mrow", [16, 2, 3, P], BF16)
        oT = sb("oT", [P, 2, S])
        rr = sb("rr", [P, 2, 16])
        on = sb("on", [P, KB, 2, NC, D])
        ps = ctx.enter_context(nc.psum_tensor("at_ps", [P, 8, 512], F32))
        PV, JOB = 6, 7
        a_in = [sem(f"a_in{n}") for n in range(2)]
        b_in = [[sem(f"b_in{bb}{g}") for g in range(4)] for bb in range(KB)]
        v_in, filled, read_v, read_a, exped = (sem(n) for n in "v_in filled read_v read_a exped".split())
        pv, ot_cp, job, job_read, m_ready = (sem(n) for n in "pv ot_cp job job_read m_ready".split())
        m_in = [sem(f"m_in{n}") for n in range(4 * KB)]
        stored, v_step, p_step = (sem(n) for n in "stored v_step p_step".split())

        events = []
        for h in range(H):
            events += [("M", 0, h)] + ([("A", 0, h // 2)] if h % 2 else [])
        for h in range(H):
            events += [("T", 0, h), ("M", 1, h)] + ([("A", 0, H // 2 + h // 2)] if h % 2 else [])
        for h in range(H):
            events += [("T", 1, h), ("A", 1, h)]
        index = {e: n for n, e in enumerate(events)}
        kinds = {k: [e for e in events if e[0] == k] for k in "AMT"}
        seq_of = {e: n for es in kinds.values() for n, e in enumerate(es)}
        tiles_v = lambda n: 2 * sum(e[0] != "T" for e in events[:n])
        tiles_a = lambda n: 2 * sum(e[0] == "T" for e in events[:n])
        tile_ps = lambda t: ps[:, 2 * (t % 3):2 * (t % 3) + 2, :]
        B_AT = {0: 0, 1: 512, 3: 896, 2: 1024}
        DELAY = 2
        plan = {n: [] for n in range(len(events) + 20)}
        groups = [e for e in events if e[0] != "M" and e[2] % 4 == 3]
        gseq = {(e[0], seq_of[e] // 4): G for G, e in enumerate(groups)}
        wishes = [(index[e] + 2, ("MT", e[1], e[2] // 4)) for e in events if e[0] == "M" and e[2] % 4 == 3]
        pv_at = []
        for G, e in enumerate(groups):
            first = max(index[e] + (DELAY + 2 if e[0] == "A" else 2), pv_at[-1] + 2 if G else 0)
            for n, chunks in enumerate(((0,), (1,), (2, 3))):
                plan[first + n].append(("PV", G, e, chunks))
            pv_at.append(first + 2)
            wishes.append((pv_at[G] + 2, ("OT", G, e)))
        jobs, at = [], -3
        for n, what in sorted(wishes, key=lambda w: w[0]):
            at = max(n, at + 3)
            plan[at].append(what)
            jobs.append(what)
        jseq = {j: n for n, j in enumerate(jobs)}
        end = at + 3

        def slot_of(e):
            return pT[e[0]][:, seq_of[e] % RING[e[0]]]

        def free_slot(eng, e):
            if seq_of[e] >= RING[e[0]]:
                G = gseq[e[0], (seq_of[e] - RING[e[0]]) // 4]
                assert pv_at[G] < index[e]
                eng.wait_ge(pv, G + 1)

        LAST = end

        with nc.Block() as block:
            @block.vector
            def _(dve):
                dve.memset(bk[64:ROWS + 3], 1.0)

        with nc.Fori(0, nb // KB) as i:
            clear(nc, sems)
            with nc.Block() as block:

                @block.sync
                def _(sp):
                    def operand(dst, bb, t, rot, h0, nh, sem_):
                        src = c["parts_d"][bass.ds((i * KB + bb) * 4 + t, 1)][:, rot:rot + 3]
                        src = src.rearrange("o s (d h) f -> (o s d) h f", h=H)[:, h0:h0 + nh]
                        sp.dma_start(dst, src).then_inc(sem_, 16)

                    def load_a(n):
                        bb, g = divmod(n, 4)
                        if n >= 2:
                            e = ("A", (n - 2) // 4, 4 * ((n - 2) % 4) + 3)
                            sp.wait_ge(filled, 2 * index[e] + 2)
                        for a in range(3):
                            rows = slice(24 * a, 24 * a + 24)
                            operand(aq[rows, n % 2], bb, 0, a, 4 * g, 4, a_in[n % 2])
                            operand(ak[rows, n % 2], bb, 1, 0, 4 * g, 4, a_in[n % 2])

                    def load_b(n):
                        bb, g = divmod(n, 4)
                        if n >= B_GROUPS:
                            e = ("T", (n - B_GROUPS) // 4, 4 * ((n - B_GROUPS) % 4) + 3)
                            sp.wait_ge(filled, 2 * index[e] + 2)
                        for a in range(3):
                            rows = slice(24 * a, 24 * a + 24)
                            at_ = b_slot(bb, 4 * g)
                            operand(bq[rows, at_:at_ + 4], bb, 2, a, 4 * g, 4, b_in[bb][g])
                            operand(bk[rows, at_:at_ + 4], bb, 3, 0, 4 * g, 4, b_in[bb][g])

                    def load_m(n):
                        bb, g = divmod(n, 4)
                        sp.wait_ge(m_ready, n + 1)
                        for p in range(3):
                            at_ = b_slot(bb, 4 * g)
                            sp.dma_start(bq[ROWS + p:ROWS + p + 1, at_:at_ + 4], mrow[:, n % 2, p, :]).then_inc(m_in[n], 16)

                    load_b(0)
                    load_a(0)
                    for n in range(1, 4):
                        load_b(n)
                    load_a(1)
                    for a in range(2 * KB):
                        sp.dma_start(v[:, a // 2, a % 2].rearrange("p c f -> p (c f)"),
                                     c["v_d"][bass.ds(i * (2 * KB) + a, 1)].rearrange("o p f -> p (o f)")).then_inc(v_in, 16)
                    for n in range(4, B_GROUPS):
                        load_b(n)
                    steps = [(index["M", n // 4, 4 * (n % 4) + 3], load_m, n) for n in range(4 * KB)]
                    steps += [(index["A", (n - 2) // 4, 4 * ((n - 2) % 4) + 3], load_a, n) for n in range(2, 4 * KB)]
                    steps += [(index["T", (n - B_GROUPS) // 4, 4 * ((n - B_GROUPS) % 4) + 3], load_b, n) for n in range(B_GROUPS, 4 * KB)]
                    for _, load, n in sorted(steps, key=lambda w: w[0]):
                        load(n)
                    for bb in range(KB):
                        for a in range(2):
                            last = max(n for n, j in enumerate(jobs) if j[0] == "OT" and j[2][:2] == ("AT"[a], bb))
                            sp.wait_ge(job_read, last + 1)
                            sp.dma_start(c["on_d"][bass.ds((i * KB + bb) * 2 + a, 1)].rearrange("o p f -> p (o f)"),
                                         on[:, bb, a].rearrange("p c f -> p (c f)")).then_inc(stored, 16)
                    sp.wait_ge(stored, 16 * 2 * KB)

                @block.gpsimd
                def _(pool):
                    step = [0]

                    def link(ins):
                        step[0] += 1
                        ins.then_inc(p_step, 1)
                        pool.wait_ge(p_step, step[0])

                    for n in range(4 * KB):
                        b = n % 2
                        pool.wait_ge(job_read, jseq["MT", n // 4, n % 4] + 1)
                        if n >= 2:
                            pool.wait_ge(m_in[n - 2], 48)
                        link(pool.tensor_copy(mrow[:, b, 0], neg[:, b]))
                        link(pool.tensor_tensor(res[:, b], neg[:, b], mrow[:, b, 0], ALU.subtract))
                        link(pool.tensor_copy(mrow[:, b, 1], res[:, b]))
                        pool.tensor_tensor(mrow[:, b, 2], res[:, b], mrow[:, b, 1], ALU.subtract).then_inc(m_ready, 1)

                @block.tensor
                def _(pe):
                    for n in range(LAST):
                        if n < len(events):
                            kind, bb, h = events[n]
                            g = h // 4
                            if kind == "A" and h % 4 == 0:
                                m = 4 * bb + g
                                pe.wait_ge(a_in[m % 2], 96 * (m // 2 + 1))
                            if kind == "M" and h % 4 == 0:
                                pe.wait_ge(b_in[bb][g], 96)
                            if kind == "T" and h % 4 == 0:
                                pe.wait_ge(m_in[4 * bb + g], 48)
                            for half in range(2):
                                t = 2 * n + half
                                if t >= 3:
                                    n3, w3 = divmod(t - 3, 2)
                                    if events[n3][0] == "T":
                                        pe.wait_ge(read_a, tiles_a(n3) + w3 + 1)
                                    else:
                                        pe.wait_ge(read_v, tiles_v(n3) + w3 + 1)
                                dst = tile_ps(t)
                                if kind == "A":
                                    slot = (4 * bb + g) % 2
                                    for w in range(2):
                                        j = 2 * half + w
                                        ins = pe.matmul(dst[:, w], ak[:, slot, h % 4, j * P:(j + 1) * P], aq[:, slot, h % 4], start=True, stop=True)
                                elif kind == "M":
                                    for w in range(2):
                                        j = 2 * half + w
                                        wide = (j + 1) * P
                                        ins = pe.matmul(dst[:, w, 0:wide], bq[0:ROWS, b_slot(bb, h), j * P:(j + 1) * P], bk[0:ROWS, b_slot(bb, h), 0:wide],
                                                        start=True, stop=True)
                                else:
                                    for j in ((0, 1, 3), (2,))[half]:
                                        bank, col = divmod(B_AT[j] - 1024 * half, 512)
                                        pe.matmul(dst[:, bank, col:col + S - j * P], bk[:, b_slot(bb, h), j * P:(j + 1) * P], bq[:, b_slot(bb, h), j * P:S],
                                                  start=True, stop=False)
                                        ins = pe.matmul(dst[:, bank, col:col + P], W["ident_bf"][:], W["cmaskT"][:], start=False, stop=True)
                                ins.then_inc(filled, 1)
                        for what in plan[n]:
                            if what[0] == "PV":
                                _, G, (kind, bb, h), chunks = what
                                a = 0 if kind == "A" else 1
                                if G == 0:
                                    pe.wait_ge(v_in, 16 * 2 * KB)
                                if kind == "A":
                                    pe.wait_ge(exped, seq_of[kind, bb, h] + 1)
                                else:
                                    pe.wait_ge(read_a, tiles_a(index[kind, bb, h] + 1))
                                if G:
                                    pe.wait_ge(ot_cp, G)
                                for j in chunks:
                                    q0 = 0 if a == 0 else j * P
                                    at_ = j * S if a == 0 else B_AT[j]
                                    for s in range(4):
                                        hh = h - 3 + s
                                        probs = slot_of((kind, bb, hh))
                                        ins = pe.matmul(ps[32 * s:32 * s + 32, PV, q0:S], v[:, bb, a, j, hh * (HD + 1):hh * (HD + 1) + 32],
                                                        probs[:, at_:at_ + S - q0], start=(j == 0), stop=(j == NC - 1))
                                if chunks[-1] == NC - 1:
                                    ins.then_inc(pv, 1)
                            else:
                                m = jseq[what]
                                if m:
                                    pe.wait_ge(job_read, m)
                                if what[0] == "OT":
                                    G = what[1]
                                    pe.wait_ge(ot_cp, G + 1)
                                    for j in range(NC):
                                        ins = pe.transpose(ps[:, JOB, j * P:(j + 1) * P], oT[:, G % 2, j * P:(j + 1) * P], W["ident"][:])
                                else:
                                    _, bb, g = what
                                    pe.wait_ge(read_v, tiles_v(index["M", bb, 4 * g + 3] + 1))
                                    ins = pe.transpose(ps[0:16, JOB, 0:P], mx[:, bb, 16 * g:16 * g + 16], W["ident"][:])
                                ins.then_inc(job, 1)

                @block.scalar
                def _(act):
                    for n in range(LAST):
                        if 1 <= n <= len(events) and events[n - 1][0] == "T":
                            e = events[n - 1]
                            slot = slot_of(e)
                            free_slot(act, e)
                            for half in range(2):
                                t = 2 * (n - 1) + half
                                act.wait_ge(filled, t + 1)
                                if half == 0:
                                    act.activation(slot[:, 0:1024], tile_ps(t).rearrange("p b f -> p (b f)"), ACT.Exp).then_inc(read_a, 1)
                                else:
                                    act.activation(slot[:, 1024:1280], tile_ps(t)[:, 0, 0:256], ACT.Exp).then_inc(read_a, 1)
                        if DELAY <= n < len(events) + DELAY and events[n - DELAY][0] == "A":
                            slot = slot_of(events[n - DELAY])
                            act.wait_ge(read_v, tiles_v(n - DELAY + 1))
                            act.activation(slot, slot, ACT.Exp).then_inc(exped, 1)
                        for what in (plan[n - 1] if n else []):
                            if what[0] == "PV" and what[3][-1] == NC - 1:
                                G = what[1]
                                act.wait_ge(pv, G + 1)
                                if G >= 2:
                                    act.wait_ge(job, jseq[next(j for j in jobs if j[0] == "OT" and j[1] == G - 2)] + 1)
                                act.copy(oT[:, G % 2], ps[:, PV, :]).then_inc(ot_cp, 1)

                @block.vector
                def _(dve):
                    step = [0]

                    def link(ins):
                        step[0] += 1
                        ins.then_inc(v_step, 1)
                        dve.wait_ge(v_step, step[0])

                    for n in range(LAST):
                        if n < len(events) and events[n][0] == "A":
                            free_slot(dve, events[n])
                            for half in range(2):
                                t = 2 * n + half
                                dve.wait_ge(filled, t + 1)
                                dve.tensor_tensor(slot_of(events[n])[:, 1024 * half:1024 * half + 1024], tile_ps(t).rearrange("p b f -> p (b f)"),
                                                  W["decay"][:, 2 * half:2 * half + 2].rearrange("p b f -> p (b f)"), ALU.mult).then_inc(read_v, 1)
                        elif n < len(events) and events[n][0] == "M":
                            _, bb, h = events[n]
                            if seq_of[events[n]]:
                                dve.wait_ge(read_v, tiles_v(index[kinds["M"][seq_of[events[n]] - 1]] + 1))
                            for half in range(2):
                                t = 2 * n + half
                                dve.wait_ge(filled, t + 1)
                                for w in range(2):
                                    j = 2 * half + w
                                    wide = (j + 1) * P
                                    ins = dve.tensor_tensor_reduce(junk[:, P * j * (j + 1) // 2:P * (j + 1) * (j + 2) // 2], tile_ps(t)[:, w, 0:wide], W["cmask"][:, S - wide:S], 1.0, -3e38,
                                                                   ALU.add, ALU.max, mx[:, bb, 4 * h + j:4 * h + j + 1])
                                ins.then_inc(read_v, 1)
                        for what in (plan[n - 2] if n >= 2 else []):
                            if what[0] == "PV":
                                continue
                            m = jseq[what]
                            dve.wait_ge(job, m + 1)
                            if what[0] == "MT":
                                q = 4 * what[1] + what[2]
                                if q >= 2:
                                    dve.wait_ge(m_ready, q - 1)
                                dve.tensor_scalar(neg[:, q % 2], ps[0:16, JOB, 0:P], -1.0, None, ALU.mult).then_inc(job_read, 1)
                            else:
                                _, G, (kind, bb, h) = what
                                a, g = (0 if kind == "A" else 1), h // 4
                                src = ps[:, JOB, :].rearrange("p (c s d) -> p c s d", c=NC, s=4)
                                rcp = rr[:, G % 2].rearrange("p (c s) -> p c s", s=4)
                                link(dve.reciprocal(rcp, src[:, :, :, HD]))
                                dst = on[:, bb, a, :, 32 * g:32 * g + 32].rearrange("p c (s d) -> p c s d", d=HD)
                                dve.tensor_tensor(dst, src[:, :, :, 0:HD], bc(rcp, HD), ALU.mult).then_inc(job_read, 1)


def tail(nc, c, W, nb, K=2):
    with ExitStack() as ctx:
        sb = lambda n, s, d=F32: ctx.enter_context(nc.sbuf_tensor("tl_" + n, s, d))
        sems = []

        def sem(n):
            sems.append(ctx.enter_context(nc.semaphore("tl_" + n)))
            return sems[-1]

        x, xn = sb("x", [P, K, NC, D]), sb("xn", [P, K, NC, D])
        on, onT = sb("on", [P, K, 2, NC, D]), sb("onT", [P, K, 2, S])
        hs, x1, xf, xfT = sb("hs", [P, K, NC, D]), sb("x1", [P, K, NC, D]), sb("xf", [P, K, NC, D]), sb("xfT", [P, K, S])
        st, mv, sc = sb("st", [P, K, NC, 6]), sb("mv", [P, K, NC, 2]), sb("sc", [P, K, 5, NC])
        lg, ex, pr = sb("lg", [P, K, NC, E]), sb("ex", [P, K, NC, E]), sb("pr", [P, K, NC, E])
        ps = ctx.enter_context(nc.psum_tensor("tl_ps", [P, 8, 512], F32))
        loaded = [sem(f"loaded{k}") for k in range(K)]
        on_t, on_cp, outp, h_sum, x1d, stats, factors, xfd, xft, xfc = (
            sem(n) for n in "on_t on_cp outp h_sum x1d stats factors xfd xft xfc".split())
        hdone, logit, lsub, lexp, probd, stored, v_step, p_step = (sem(n) for n in "hdone logit lsub lexp probd stored v_step p_step".split())
        flat = lambda ap: ap.rearrange("p c d -> p (c d)")

        with nc.Fori(0, nb // K) as i:
            clear(nc, sems)
            with nc.Block() as block:

                @block.sync
                def _(sp):
                    seq = lambda t, k: t[bass.ds(i * K + k, 1)].rearrange("o (c p) d -> p (o c) d", p=P)
                    for k in range(K):
                        for a in range(2):
                            sp.dma_start(flat(on[:, k, a]), c["on_d"][bass.ds((i * K + k) * 2 + a, 1)].rearrange("o p f -> p (o f)")).then_inc(loaded[k], 16)
                        sp.dma_start(x[:, k], seq(c["x"], k)).then_inc(loaded[k], 16)
                        sp.dma_start(xn[:, k], seq(c["xn_d"], k)).then_inc(loaded[k], 16)
                    for k in range(K):
                        sp.wait_ge(x1d, k + 1)
                        sp.dma_start(seq(c["x1_d"], k), x1[:, k]).then_inc(stored, 16)
                        sp.wait_ge(hdone, k + 1)
                        sp.dma_start(seq(c["h_d"], k), hs[:, k]).then_inc(stored, 16)
                    for k in range(K):
                        sp.wait_ge(xfd, k + 1)
                        sp.dma_start(seq(c["xf_d"], k), xf[:, k]).then_inc(stored, 16)
                    for k in range(K):
                        sp.wait_ge(probd, k + 1)
                        sp.dma_start(c["pr_d"][:, bass.ds(i * K + k, 1)].rearrange("p o c e -> p (o c) e"), pr[:, k]).then_inc(stored, 16)
                    sp.wait_ge(stored, 64 * K)

                @block.gpsimd
                def _(pool):
                    for k in range(K):
                        pool.wait_ge(h_sum, k + 1)
                        pool.wait_ge(x1d, k + 1)
                        pool.tensor_tensor(hs[:, k], hs[:, k], x1[:, k], ALU.add).then_inc(hdone, 1)
                        pool.wait_ge(stats, k + 1)
                        pool.tensor_scalar(sc[:, k, 1], sc[:, k, 0], 1e-6, None, ALU.add).then_inc(p_step, 1)
                        pool.wait_ge(p_step, k + 1)
                        pool.tensor_tensor(sc[:, k, 2], sc[:, k, 1], W["mhalf"][:, 0:NC], ALU.pow).then_inc(factors, 1)

                @block.tensor
                def _(pe):
                    for k in range(K):
                        pe.wait_ge(loaded[k], 64)
                        for a in range(2):
                            for j in range(NC):
                                ins = pe.transpose(ps[:, 4 * k + a, j * P:(j + 1) * P], on[:, k, a, j, :], W["ident"][:])
                            ins.then_inc(on_t, 1)
                    for k in range(K):
                        for a in range(2):
                            pe.wait_ge(on_cp, 2 * k + a + 1)
                            for j in range(NC):
                                ins = pe.matmul(ps[:, 4 * k + 2 + a, j * P:(j + 1) * P], onT[:, k, a, j * P:(j + 1) * P], W[("woA", "woB")[a]][:],
                                                start=True, stop=True)
                            ins.then_inc(outp, 1)
                    for k in range(K):
                        pe.wait_ge(xfd, k + 1)
                        for j in range(NC):
                            ins = pe.transpose(ps[:, 4 * k, j * P:(j + 1) * P], xf[:, k, j, :], W["ident"][:])
                        ins.then_inc(xft, 1)
                    for k in range(K):
                        pe.wait_ge(xfc, k + 1)
                        for j in range(NC):
                            ins = pe.matmul(ps[:, 4 * k + 1, j * E:(j + 1) * E], xfT[:, k, j * P:(j + 1) * P], W["wr"][:], start=True, stop=True)
                        ins.then_inc(logit, 1)

                @block.scalar
                def _(act):
                    for k in range(K):
                        for a in range(2):
                            act.wait_ge(on_t, 2 * k + a + 1)
                            act.copy(onT[:, k, a], ps[:, 4 * k + a, :]).then_inc(on_cp, 1)
                    for k in range(K):
                        act.wait_ge(xft, k + 1)
                        act.copy(xfT[:, k], ps[:, 4 * k, :]).then_inc(xfc, 1)
                    for k in range(K):
                        act.wait_ge(lsub, k + 1)
                        act.activation(ex[:, k], lg[:, k], ACT.Exp).then_inc(lexp, 1)

                @block.vector
                def _(dve):
                    step = [0]

                    def link(ins):
                        step[0] += 1
                        ins.then_inc(v_step, 1)
                        dve.wait_ge(v_step, step[0])

                    for k in range(K):
                        dve.wait_ge(outp, 2 * k + 1)
                        dve.tensor_tensor(flat(hs[:, k]), flat(x[:, k]), ps[:, 4 * k + 2, :], ALU.add).then_inc(h_sum, 1)
                        dve.wait_ge(outp, 2 * k + 2)
                        dve.tensor_tensor(flat(x1[:, k]), flat(xn[:, k]), ps[:, 4 * k + 3, :], ALU.add).then_inc(x1d, 1)
                        dve.wait_ge(x1d, k + 1)
                        for j in range(NC):
                            ins = dve.bn_stats(st[:, k, j], x1[:, k, j, :])
                        link(ins)
                        for j in range(NC):
                            ins = dve.bn_aggr(mv[:, k, j], st[:, k, j])
                        link(ins)
                        link(dve.tensor_tensor(sc[:, k, 3], mv[:, k, :, 0], mv[:, k, :, 0], ALU.mult))
                        dve.tensor_tensor(sc[:, k, 0], sc[:, k, 3], mv[:, k, :, 1], ALU.add).then_inc(stats, 1)
                    for k in range(K):
                        dve.wait_ge(factors, k + 1)
                        for j in range(NC):
                            ins = dve.scalar_tensor_tensor(xf[:, k, j], x1[:, k, j], sc[:, k, 2, j:j + 1], W["g2b"][:], ALU.mult, ALU.mult)
                        ins.then_inc(xfd, 1)
                    logits = lambda k: ps[:, 4 * k + 1, 0:NC * E].rearrange("p (c e) -> p c e", e=E)
                    for k in range(K):
                        dve.wait_ge(logit, k + 1)
                        link(dve.tensor_reduce(sc[:, k, 4], logits(k), AX.X, ALU.max))
                        dve.tensor_tensor(lg[:, k], logits(k), bc(sc[:, k, 4], E), ALU.subtract).then_inc(lsub, 1)
                    for k in range(K):
                        dve.wait_ge(lexp, k + 1)
                        link(dve.tensor_reduce(sc[:, k, 3], ex[:, k], AX.X, ALU.add))
                        link(dve.reciprocal(sc[:, k, 4], sc[:, k, 3]))
                        dve.tensor_tensor(pr[:, k], ex[:, k], bc(sc[:, k, 4], E), ALU.mult).then_inc(probd, 1)


def bound_flag(nc, W, nb):
    with ExitStack() as ctx:
        sb = lambda n, s, d=F32: ctx.enter_context(nc.sbuf_tensor("bf_" + n, s, d))
        pb, m, row = sb("pb", [H, nb]), sb("m", [H, 2]), sb("row", [1, 1])
        ps = ctx.enter_context(nc.psum_tensor("bf_ps", [P, 512], F32))
        step, turned = ctx.enter_context(nc.semaphore("bf_step")), ctx.enter_context(nc.semaphore("bf_turned"))
        with nc.Block() as block:

            @block.vector
            def _(dve):
                pairs = W["nmax"][:, 0:2 * nb].rearrange("p (b t) -> p b t", t=2)
                dve.tensor_tensor(pb[:], pairs[:, :, 0], pairs[:, :, 1], ALU.mult).then_inc(step, 1)
                dve.wait_ge(step, 1)
                dve.tensor_reduce(m[:, 0:1], pb[:], AX.X, ALU.max).then_inc(step, 1)
                dve.wait_ge(turned, 1)
                dve.tensor_reduce(row[:], ps[0:1, 0:H], AX.X, ALU.max).then_inc(step, 1)
                dve.wait_ge(step, 3)
                dve.tensor_scalar(row[:], row[:], LIMIT * LIMIT, None, ALU.is_lt).then_inc(step, 1)
                dve.wait_ge(step, 4)
                dve.tensor_scalar(W["flag"][:], row[:], -1.0, 1.0, ALU.mult, ALU.add).then_inc(step, 1)
                dve.wait_ge(step, 5)

            @block.tensor
            def _(pe):
                pe.wait_ge(step, 2)
                pe.transpose(ps[0:1, 0:H], m[:, 0:1], W["ident"][0:H, 0:H]).then_inc(turned, 1)


def attend_any(nc, c, W, nb):
    with ExitStack() as ctx:
        sb = lambda n, s, d=F32: ctx.enter_context(nc.sbuf_tensor("an_" + n, s, d))
        sems = []

        def sem(n):
            sems.append(ctx.enter_context(nc.semaphore("an_" + n)))
            return sems[-1]

        x, xn, x1, hs = sb("x", [P, NC, D]), sb("xn", [P, NC, D]), sb("x1", [P, NC, D]), sb("hs", [P, NC, D])
        xnT = sb("xnT", [P, S])
        q, k, v = sb("q", [P, S]), sb("k", [P, S]), sb("v", [P, NC, H, 32])
        qm = sb("qm", [P, 4, S])
        clip, tt, prob = sb("clip", [P, 2, S]), sb("tt", [P, 2, S]), sb("prob", [P, 3, S])
        pT = sb("pT", [P, 2, 4, NC, S])
        mx, nm, rs = sb("mx", [P, UNITS]), sb("nm", [P, UNITS]), sb("rs", [P, UNITS])
        rr = sb("rr", [P, 16])
        oT = sb("oT", [P, S])
        on, onT = sb("on", [P, NC, D]), sb("onT", [P, S])
        ps = ctx.enter_context(nc.psum_tensor("an_ps", [P, 8, 512], F32))
        x_in, turned, turned_cp, proj, k_cp, qv_cp, masked = (sem(n) for n in "x_in turned turned_cp proj k_cp qv_cp masked".split())
        scored, clipped, reduced, maxed, exped = (sem(n) for n in "scored clipped reduced maxed exped".split())
        transposed, evacuated, pv, ot_cp, ot_t = (sem(n) for n in "transposed evacuated pv ot_cp ot_t".split())
        zeroed, inverted, weighed, on_t, on_cp, projo, based, added, stored = (
            sem(n) for n in "zeroed inverted weighed on_t on_cp projo based added stored".split())
        S0, TP0, OT, OTT, M0, M1 = 0, 2, 4, 5, 6, 7
        LAST = UNITS + 14

        def wait(eng, s, n):
            if n > 0:
                eng.wait_ge(s, n)

        with nc.Fori(0, nb) as i:
            clear(nc, sems)
            with nc.Block() as block:

                @block.sync
                def _(sp):
                    seq = lambda t: t[bass.ds(i, 1)].rearrange("o (c p) d -> p (o c) d", p=P)
                    for dst, src in ((xn, "xn_d"), (x, "x"), (x1, "x1_d")):
                        sp.dma_start(dst[:], seq(c[src])).then_inc(x_in, 16)
                    sp.wait_ge(added, 1)
                    sp.dma_start(seq(c["h_d"]), hs[:]).then_inc(stored, 16)
                    sp.wait_ge(stored, 16)

                @block.gpsimd
                def _(pool):
                    pool.wait_ge(x_in, 48)
                    pool.tensor_tensor(hs[:], x[:], x1[:], ALU.add).then_inc(based, 1)
                    pool.wait_ge(qv_cp, 1)
                    for n in range(H):
                        wait(pool, scored, NC * (n - 3))
                        pool.tensor_scalar(qm[:, n % 4], q[:], W["hsum"][:, n:n + 1], SCALE_A, ALU.mult, ALU.mult).then_inc(masked, 1)

                @block.tensor
                def _(pe):
                    pe.wait_ge(x_in, 48)
                    for j in range(NC):
                        ins = pe.transpose(ps[:, 0, j * P:(j + 1) * P], xn[:, j, :], W["ident"][:])
                    ins.then_inc(turned, 1)
                    pe.wait_ge(turned_cp, 1)
                    pe.matmul(ps[:, 2, :], W["wqA"][:], xnT[:], start=True, stop=True).then_inc(proj, 1)
                    pe.matmul(ps[:, 3, :], W["mk"][:], xnT[:], start=True, stop=True).then_inc(proj, 1)
                    for j in range(NC):
                        ins = pe.matmul(ps[:, 4, j * P:(j + 1) * P], xnT[:, j * P:(j + 1) * P], W["mv"][:], start=True, stop=True)
                    ins.then_inc(proj, 1)
                    pe.wait_ge(k_cp, 1)
                    pe.wait_ge(qv_cp, 2)
                    for t in range(LAST):
                        if t < UNITS:
                            n = t // NC
                            wait(pe, masked, n + 1)
                            wait(pe, clipped, t - 1)
                            pe.matmul(ps[:, S0 + t % 2, :], qm[:, n % 4, (t % NC) * P:(t % NC + 1) * P], k[:], start=True, stop=True).then_inc(scored, 1)
                        u = t - 2
                        if 0 <= u < UNITS:
                            wait(pe, exped, u + 1)
                            wait(pe, evacuated, u - 1)
                            for j in range(NC):
                                ins = pe.transpose(ps[:, TP0 + u % 2, j * P:(j + 1) * P], prob[:, u % 3, j * P:(j + 1) * P], W["ident"][:])
                            ins.then_inc(transposed, 1)
                        g, m = divmod(t - 20, 16)
                        if m == 0 and 0 <= g < NG:
                            wait(pe, evacuated, 16 * g + 16)
                            wait(pe, ot_cp, g)
                            for j in range(NC):
                                for s in range(4):
                                    ins = pe.matmul(ps[32 * s:32 * s + 32, OT, :], v[:, j, 4 * g + s, :], pT[:, g % 2, s, j],
                                                    start=(j == 0), stop=(j == NC - 1))
                            ins.then_inc(pv, 1)
                        g, m = divmod(t - 23, 16)
                        if m == 0 and 0 <= g < NG:
                            wait(pe, ot_cp, g + 1)
                            wait(pe, weighed, g)
                            for j in range(NC):
                                ins = pe.transpose(ps[:, OTT, j * P:(j + 1) * P], oT[:, j * P:(j + 1) * P], W["ident"][:])
                            ins.then_inc(ot_t, 1)
                    wait(pe, weighed, NG)
                    for j in range(NC):
                        ins = pe.transpose(ps[:, M0, j * P:(j + 1) * P], on[:, j, :], W["ident"][:])
                    ins.then_inc(on_t, 1)
                    wait(pe, on_cp, 1)
                    for j in range(NC):
                        ins = pe.matmul(ps[:, M1, j * P:(j + 1) * P], onT[:, j * P:(j + 1) * P], W["woA"][:], start=True, stop=True)
                    ins.then_inc(projo, 1)

                @block.scalar
                def _(act):
                    wait(act, turned, 1)
                    act.copy(xnT[:], ps[:, 0, :]).then_inc(turned_cp, 1)
                    wait(act, proj, 1)
                    act.copy(q[:], ps[:, 2, :]).then_inc(qv_cp, 1)
                    wait(act, proj, 3)
                    wait(act, zeroed, 1)
                    act.copy(v[:, :, :, 0:HD].rearrange("p c h d -> p (c h) d"),
                             ps[:, 4, :].rearrange("p (c h d) -> p (c h) d", c=NC, d=HD)).then_inc(qv_cp, 1)
                    for t in range(LAST):
                        if t < UNITS:
                            wait(act, maxed, t + 1)
                            wait(act, transposed, t - 2)
                            act.activation(prob[:, t % 3], tt[:, t % 2], ACT.Exp, bias=nm[:, t:t + 1], accum_out=rs[:, t:t + 1]).then_inc(exped, 1)
                        u = t - 3
                        if 0 <= u < UNITS:
                            wait(act, transposed, u + 1)
                            wait(act, pv, u // 16 - 1)
                            act.copy(pT[:, (u // 16) % 2, (u // NC) % 4, :, (u % NC) * P:(u % NC + 1) * P],
                                     ps[:, TP0 + u % 2, :].rearrange("p (j r) -> p j r", j=NC)).then_inc(evacuated, 1)
                        g, m = divmod(t - 21, 16)
                        if m == 0 and 0 <= g < NG:
                            wait(act, pv, g + 1)
                            wait(act, ot_t, g)
                            act.copy(oT[:], ps[:, OT, :]).then_inc(ot_cp, 1)
                    wait(act, on_t, 1)
                    act.copy(onT[:], ps[:, M0, :]).then_inc(on_cp, 1)

                @block.vector
                def _(dve):
                    dve.memset(v[:], 0.0).then_inc(zeroed, 1)
                    wait(dve, proj, 2)
                    dve.tensor_copy(k[:], ps[:, 3, :]).then_inc(k_cp, 1)
                    for t in range(UNITS + 14):
                        if t < UNITS:
                            wait(dve, scored, t + 1)
                            wait(dve, exped, t - 1)
                            dve.tensor_scalar(clip[:, t % 2], ps[:, S0 + t % 2, :], CLAMP, -CLAMP, ALU.min, ALU.max).then_inc(clipped, 1)
                            wait(dve, clipped, t + 1)
                            dve.tensor_tensor_reduce(tt[:, t % 2], clip[:, t % 2], W["decay"][:, t % NC], 1.0, -3e38,
                                                     ALU.mult, ALU.max, mx[:, t:t + 1]).then_inc(reduced, 1)
                            wait(dve, reduced, t + 1)
                            dve.tensor_scalar(nm[:, t:t + 1], mx[:, t:t + 1], -1.0, None, ALU.mult).then_inc(maxed, 1)
                        g, m = divmod(t - 25, 16)
                        if m == 0 and 0 <= g < NG:
                            wait(dve, exped, 16 * g + 16)
                            dve.reciprocal(rr[:], rs[:, 16 * g:16 * g + 16]).then_inc(inverted, 1)
                            wait(dve, inverted, g + 1)
                            wait(dve, ot_t, g + 1)
                            for j in range(NC):
                                ins = dve.tensor_tensor(
                                    on[:, j, 32 * g:32 * g + 32].rearrange("p (s d) -> p s d", d=HD),
                                    ps[:, OTT, j * P:(j + 1) * P].rearrange("p (s d) -> p s d", s=4)[:, :, 0:HD],
                                    bc(rr[:].rearrange("p (s c) -> p s c", c=NC)[:, :, j], HD),
                                    ALU.mult)
                            ins.then_inc(weighed, 1)
                    wait(dve, projo, 1)
                    wait(dve, based, 1)
                    flat = lambda t: t[:].rearrange("p c d -> p (c d)")
                    dve.tensor_tensor(flat(hs), flat(hs), ps[:, M1, :], ALU.add).then_inc(added, 1)


def route(nc, c, W, R):
    with ExitStack() as ctx:
        sb = lambda n, s, d=F32: ctx.enter_context(nc.sbuf_tensor("rt_" + n, s, d))
        sem = lambda n: ctx.enter_context(nc.semaphore(n))
        NE = NT * E
        prob = sb("prob", [P, NT, E])
        rank, eqs = sb("rank", [P, NT, E]), sb("eqs", [P, NT, E])
        cmp = sb("cmp", [P, NT, E, E])
        gate = sb("gate", [P, NT, E])
        gt = sb("gt", [P, E, NT])
        hit = sb("hit", [P, E, NT])
        low = sb("low", [P, E, E])
        ones, before = sb("ones", [P, P]), sb("before", [P, P])
        restart = sb("restart", [P, NE])
        cnt, need = sb("cnt", [P, E]), sb("need", [P, E])
        thr, cand, bit, add = (sb("thr", [P, E], I32), sb("cand", [P, E], I32), sb("bit", [P, E], I32), sb("add", [P, E], I32))
        bitf = sb("bitf", [P, E])
        above, equal, keep = sb("above", [P, E, NT]), sb("equal", [P, E, NT]), sb("keep", [P, E, NT])
        incl, pos = sb("incl", [P, NE]), sb("pos", [P, E, NT])
        slots = sb("slots", [P, E, CAP])
        onehot = sb("onehot", [P, 2, E * CAP], BF16)
        ptid = sb("ptid", [P, NT, 2])
        pt = sb("pt", [P, 2, 2], BF16)
        place = sb("place", [2, E * CAP])
        mix = sb("mix", [2, 2])
        ps = ctx.enter_context(nc.psum_tensor("rt_ps", [P, 8, 512], F32))
        s_in, step, counted, scanned = sem("rt_in"), sem("rt_step"), sem("rt_counted"), sem("rt_scanned")
        cnt_ready, bit_step, ranked = sem("rt_cnt_ready"), sem("rt_bit_step"), sem("rt_ranked")
        hot, placed, copied, turned, gated = sem("rt_hot"), sem("rt_placed"), sem("rt_copied"), sem("rt_turned"), sem("rt_gated")
        hot_prep = sem("rt_hot_prep")
        BITS = 30
        block = ctx.enter_context(nc.Block())
        loads = [(prob[:].rearrange("p t e -> p (t e)"), c["pr_d"].rearrange("p b c e -> p (b c e)")),
                 (low[:].rearrange("p a b -> p (a b)"), c["low"]), (before[:], c["before"]), (restart[:], c["restart"]),
                 (slots[:].rearrange("p a b -> p (a b)"), c["slots"]), (ptid[:].rearrange("p a b -> p (a b)"), c["ptid"]),
                 (mix[:], c["mix"])]
        flat = lambda ap: ap.rearrange("p a b -> p (a b)")
        ET = [P, E, NT]

        @block.sync
        def _(sp):
            for dst, src in loads:
                sp.dma_start(dst, src).then_inc(s_in, 16)
            sp.wait_ge(gated, 1)
            sp.dma_start(c["gate_d"].rearrange("(p t) e -> p (t e)", p=P), flat(gate[:])).then_inc(s_in, 16)
            sp.wait_ge(s_in, 16 * (len(loads) + 1))

        @block.vector
        def _(dve):
            n = [0]

            def link(ins):
                n[0] += 1
                ins.then_inc(step, 1)
                dve.wait_ge(step, n[0])

            dve.memset(ones[:], 1.0)
            dve.memset(ps[0:2, 3:6, :], 0.0).then_inc(placed, 1)
            dve.memset(thr[:], 0)
            dve.memset(bit[:], 1 << (BITS - 1))
            link(dve.memset(bitf[:], float(1 << (BITS - 1))))
            dve.wait_ge(s_in, 16 * len(loads))
            other = prob[:].unsqueeze(2).broadcast_to([P, NT, E, E])
            mine = bc(prob[:], E)
            link(dve.tensor_tensor(cmp[:], other, mine, ALU.is_gt))
            link(dve.tensor_reduce(rank[:], cmp[:], AX.X, ALU.add))
            link(dve.tensor_tensor(cmp[:], other, mine, ALU.is_equal))
            link(dve.tensor_tensor(cmp[:], cmp[:], low[:].unsqueeze(1).broadcast_to([P, NT, E, E]), ALU.mult))
            link(dve.tensor_reduce(eqs[:], cmp[:], AX.X, ALU.add))
            link(dve.tensor_tensor(rank[:], rank[:], eqs[:], ALU.add))
            dve.scalar_tensor_tensor(gate[:], rank[:], float(TOPK), prob[:], ALU.is_lt, ALU.mult).then_inc(gated, 1)
            dve.wait_ge(gated, 1)
            link(dve.tensor_copy(gt[:], gate[:].rearrange("p t e -> p e t")))
            with dve.Fori(0, BITS) as i:
                dve.tensor_tensor(cand[:], thr[:], bit[:], ALU.bitwise_or).then_inc(bit_step, 1)
                dve.wait_ge(bit_step, i * 4 + 1)
                dve.tensor_tensor(hit[:], gt[:], bc(cand[:].bitcast(F32), NT), ALU.is_ge).then_inc(bit_step, 1)
                dve.wait_ge(bit_step, i * 4 + 2)
                dve.tensor_reduce(cnt[:], hit[:], AX.X, ALU.add).then_inc(cnt_ready, 1)
                dve.wait_ge(counted, i + 1)
                dve.scalar_tensor_tensor(add[:], ps[:, 0, 0:E], float(CAP), bitf[:], ALU.is_ge, ALU.mult).then_inc(bit_step, 1)
                dve.wait_ge(bit_step, i * 4 + 3)
                dve.tensor_tensor(thr[:], thr[:], add[:], ALU.bitwise_or)
                dve.tensor_scalar(bit[:], bit[:], 1, None, ALU.logical_shift_right)
                dve.tensor_scalar(bitf[:], bitf[:], 0.5, None, ALU.mult).then_inc(bit_step, 1)
                dve.wait_ge(bit_step, i * 4 + 4)
            cut = bc(thr[:].bitcast(F32), NT)
            dve.tensor_tensor(above[:], gt[:], cut, ALU.is_gt)
            link(dve.tensor_tensor(equal[:], gt[:], cut, ALU.is_equal))
            dve.tensor_reduce(cnt[:], above[:], AX.X, ALU.add).then_inc(cnt_ready, 1)
            dve.wait_ge(counted, BITS + 1)
            link(dve.tensor_scalar(need[:], ps[:, 0, 0:E], -1.0, float(CAP), ALU.mult, ALU.add))

            def rank_before(k):
                dve.wait_ge(ranked, k)
                link(dve.tensor_tensor_scan(incl[:], restart[:], ps[:, 2, :], 0.0, ALU.mult, ALU.add))
                link(dve.tensor_tensor(incl[:], incl[:], ps[:, 2, :], ALU.subtract))
                link(dve.tensor_tensor(flat(pos[:]), incl[:], ps[:, 1, :], ALU.add))

            rank_before(1)
            link(dve.tensor_tensor(pos[:], pos[:], bc(need[:], NT), ALU.is_lt))
            link(dve.tensor_tensor(pos[:], pos[:], equal[:], ALU.mult))
            dve.tensor_tensor(keep[:], above[:], pos[:], ALU.add).then_inc(scanned, 1)
            rank_before(2)
            link(dve.scalar_tensor_tensor(pos[:], pos[:], 1.0, keep[:], ALU.add, ALU.mult))
            link(dve.tensor_scalar(pos[:], pos[:], -1.0, None, ALU.add))
            with dve.Fori(0, NT // 2) as i:
                for b in range(2):
                    dve.wait_ge(placed, i * 2 + 1)
                    dve.tensor_copy(pt[:, b], ptid[:, bass.ds(i * 2 + b, 1)].rearrange("p a b -> p (a b)"))
                    dve.tensor_tensor(onehot[:, b].rearrange("p (e s) -> p e s", e=E), slots[:],
                                      pos[:, :, bass.ds(i * 2 + b, 1)].broadcast_to([P, E, CAP]), ALU.is_equal).then_inc(hot, 1)
            dve.wait_ge(placed, NT + 1)
            for b in range(3):
                w = min(512, E * CAP - 512 * b)
                ins = dve.tensor_copy(place[:, 512 * b:512 * b + w], ps[0:2, 3 + b, 0:w])
            ins.then_inc(copied, 1)
            dve.wait_ge(turned, 1)
            link(dve.tensor_copy(R["rows"][0:HALF], ps[0:HALF, 6, 0:64].rearrange("p (m k) -> p m k", k=2)[:, 0:2 * E, :]))

        @block.tensor
        def _(pe):
            pe.wait_ge(step, 1)
            with pe.Fori(0, BITS + 1) as i:
                pe.wait_ge(cnt_ready, i + 1)
                pe.matmul(ps[:, 0, 0:E], ones[:], cnt[:], start=True, stop=True).then_inc(counted, 1)
            for k, marked in enumerate((equal, keep)):
                pe.wait_ge(*((step, 10) if k == 0 else (scanned, 1)))
                pe.matmul(ps[:, 1, :], before[:], flat(marked[:]), start=True, stop=True)
                pe.matmul(ps[:, 2, :], ones[:], flat(marked[:]), start=True, stop=True).then_inc(ranked, 1)
            with pe.Fori(0, NT // 2) as i:
                for b in range(2):
                    pe.wait_ge(hot, i * 2 + b + 1)
                    for m in range(3):
                        w = min(512, E * CAP - 512 * m)
                        ins = pe.matmul(ps[0:2, 3 + m, 0:w], pt[:, b], onehot[:, b, 512 * m:512 * m + w],
                                        start=False, stop=False, skip_group_check=True)
                    ins.then_inc(placed, 1)
            pe.wait_ge(copied, 1)
            for m in range(2 * E):
                ins = pe.matmul(ps[0:HALF, 6, 2 * m:2 * m + 2], place[:, HALF * m:HALF * (m + 1)], mix[:], start=True, stop=True)
            ins.then_inc(turned, 1)


def experts(nc, c, W, R):
    with ExitStack() as ctx:
        sb = lambda n, s, d=F32: ctx.enter_context(nc.sbuf_tensor("ex_" + n, s, d))
        sem = lambda n: ctx.enter_context(nc.semaphore(n))
        w1, w2 = sb("w1", [P, E, FF]), sb("w2", [P, E, 2, D])
        xe, ge = sb("xe", [P, 2 * E, D]), sb("ge", [P, 2 * E, E])
        xeT, hT = sb("xeT", [P, 2, CAP]), sb("hT", [P, 2, 2, CAP])
        ye = sb("ye", [P, 2 * E, D])
        ps = ctx.enter_context(nc.psum_tensor("ex_ps", [P, 8, 512], F32))
        s_in = sem("ex_in")
        fetched = [sem(f"ex_fetched{e}") for e in range(E)]
        turned, turned_cp, hidden, relued, out, scaled, summed = (sem("ex_turned"), sem("ex_turned_cp"), sem("ex_hidden"),
                                                                  sem("ex_relued"), sem("ex_out"), sem("ex_scaled"), sem("ex_summed"))
        rows = R["rows"]
        block = ctx.enter_context(nc.Block())

        @block.sync
        def _(sp):
            sp.dma_start(w1[:], c["w1"].rearrange("e d f -> d e f")).then_inc(s_in, 16)
            sp.dma_start(w2[:].rearrange("p e h d -> p (e h) d"), c["w2"].rearrange("e (h p) d -> p (e h) d", p=P)).then_inc(s_in, 16)

        @block.gpsimd
        def _(pool):
            for m in range(2 * E):
                pool.indirect_dma_start(xe[0:HALF, m, :], None, c["xf_d"].rearrange("b s d -> (b s) d"),
                                        bass.IndirectOffsetOnAxis(rows[0:HALF, m, 0:1], 0)).then_inc(fetched[m // 2], 16)
                pool.indirect_dma_start(ge[0:HALF, m, :], None, c["gate_d"],
                                        bass.IndirectOffsetOnAxis(rows[0:HALF, m, 1:2], 0)).then_inc(fetched[m // 2], 16)
            for m in range(2 * E):
                e = m // 2
                pool.wait_ge(scaled, e + 1)
                pool.wait_ge(summed, 32 * e)
                pool.indirect_dma_start(c["h_d"].rearrange("b s d -> (b s) d"),
                                        bass.IndirectOffsetOnAxis(rows[0:HALF, m, 0:1], 0), ye[0:HALF, m, :], None,
                                        compute_op=ALU.add).then_inc(summed, 16)
            pool.wait_ge(summed, 32 * E)

        @block.tensor
        def _(pe):
            for e in range(E):
                b = e % 2
                pe.wait_ge(fetched[e], 64)
                if e >= 2:
                    pe.wait_ge(turned_cp, e - 1)
                for k in range(2):
                    ins = pe.transpose(ps[:, b, k * HALF:(k + 1) * HALF], xe[0:HALF, 2 * e + k, :], W["ident"][0:HALF, 0:HALF])
                ins.then_inc(turned, 1)
                pe.wait_ge(turned_cp, e + 1)
                pe.wait_ge(s_in, 32)
                if e >= 2:
                    pe.wait_ge(relued, e - 1)
                for f in range(2):
                    ins = pe.matmul(ps[:, 2 + b, f * CAP:(f + 1) * CAP], w1[:, e, f * P:(f + 1) * P], xeT[:, b], start=True, stop=True)
                ins.then_inc(hidden, 1)
                pe.wait_ge(relued, e + 1)
                if e >= 2:
                    pe.wait_ge(scaled, e - 1)
                for k in range(2):
                    for f in range(2):
                        ins = pe.matmul(ps[0:HALF, 4 + b, k * D:(k + 1) * D], hT[:, b, f, k * HALF:(k + 1) * HALF], w2[:, e, f, :],
                                        start=(f == 0), stop=(f == 1))
                ins.then_inc(out, 1)

        @block.scalar
        def _(act):
            for e in range(E):
                b = e % 2
                act.wait_ge(turned, e + 1)
                act.copy(xeT[:, b], ps[:, b, 0:CAP]).then_inc(turned_cp, 1)
                act.wait_ge(hidden, e + 1)
                act.activation(hT[:, b].rearrange("p f s -> p (f s)"), ps[:, 2 + b, 0:2 * CAP], ACT.Relu).then_inc(relued, 1)

        @block.vector
        def _(dve):
            for e in range(E):
                dve.wait_ge(out, e + 1)
                for k in range(2):
                    m = 2 * e + k
                    ins = dve.tensor_scalar(ye[0:HALF, m, :], ps[0:HALF, 4 + e % 2, k * D:(k + 1) * D], ge[0:HALF, m, e:e + 1], None, ALU.mult)
                ins.then_inc(scaled, 1)


B1, SEG, DH = 4, 32, 64
NSEG = S // SEG
BG = NB // B1
PAIRS = H // 2
VE = DH + 1
QMAX = 448.0
Q_ROUND = 1.5 * 2.0 ** 20
Q_LEAST = 2.0 ** -6


def quantize(dve, link, dst, src, scale, tmp, mag):
    link(dve.tensor_scalar(tmp, src, scale, None, ALU.mult))
    link(dve.tensor_scalar(mag.bitcast(I32), tmp.bitcast(I32), 0x7F800000, None, ALU.bitwise_and))
    link(dve.tensor_scalar(mag, mag, Q_LEAST, Q_ROUND, ALU.max, ALU.mult))
    link(dve.tensor_tensor(tmp, tmp, mag, ALU.add))
    return dve.tensor_tensor(dst, tmp, mag, ALU.subtract)


def scale_factors(nc, c, V):
    with ExitStack() as ctx:
        sb = lambda n, s, d=F32: ctx.enter_context(nc.sbuf_tensor("sf_" + n, s, d))
        sem = lambda n: ctx.enter_context(nc.semaphore(n))
        NL = 4
        h = sb("h", [P, 2, NT // NL, D])
        st, mv = sb("st", [P, NT // NL, 6]), sb("mv", [P, NT // NL, 2])
        ve, rstd = sb("ve", [P, NT // NL]), sb("rstd", [P, NT // NL])
        half = sb("half", [P, NT // NL])
        lohi, am = sb("lohi", [P, 2, NT // NL]), sb("am", [P, NL, 2])
        top = sb("top", [P, 2])
        row, mrow, srow = sb("row", [2, P]), sb("mrow", [2, 1]), sb("srow", [2, 1])
        dia = sb("dia", [2, 2])
        ones2 = sb("ones2", [2, P])
        w, wT, tmp, mag = sb("w", [P, D]), sb("wT", [P, D]), sb("tmp", [P, D]), sb("mag", [P, D])
        beta = sb("beta", [P, H])
        ps = ctx.enter_context(nc.psum_tensor("sf_ps", [P, 8, 512], F32))
        s_w, s_h = sem("sf_w"), [sem("sf_h0"), sem("sf_h1")]
        step, stat, fact, used = sem("sf_step"), sem("sf_stat"), sem("sf_fact"), sem("sf_used")
        pe_s, act_s, halves = sem("sf_pe"), sem("sf_act"), sem("sf_halves")
        loads = [(V["wqkv"][:], c["w1qkv"]), (V["wout"][:], c["wout"].rearrange("(j p) d -> p j d", p=P)),
                 (V["g"][:], c["ln_g"]), (V["b"][:], c["ln_b"]), (V["bias"][:], c["bias"]), (beta[:], c["beta"]),
                 (V["ident"][:], c["ident"]), (V["cos"][:], c["cos1"]), (V["sin"][:], c["sin1"]), (V["mask"][:], c["mask1"]),
                 (w[:], c["wffn"])]
        block = ctx.enter_context(nc.Block())
        h_all = c["h_d"].rearrange("b (k p) d -> p (b k) d", p=P)
        K = NT // NL

        @block.sync
        def _(sp):
            for n in range(NL):
                if n >= 2:
                    sp.wait_ge(used, n - 1)
                sp.dma_start(h[:, n % 2], h_all[:, n * K:(n + 1) * K, :]).then_inc(s_h[n % 2], 16)
                if n == 1:
                    for dst, src in loads:
                        sp.dma_start(dst, src).then_inc(s_w, 16)

        @block.gpsimd
        def _(pool):
            pool.memset(half[:], -0.5).then_inc(halves, 1)
            pool.memset(V["mhalf"][:], -0.5)
            pool.memset(V["uu"][:], 1.0)
            pool.memset(V["mem"][:], 0.0).then_inc(halves, 1)
            pool.wait_ge(halves, 2)
            pool.memset(V["mem"][0:DH, :, :, DH:VE], 1e-6).then_inc(halves, 1)
            pool.wait_ge(halves, 3)
            pool.memset(V["mem"][DH:P, :, :, VE + DH:2 * VE], 1e-6).then_inc(halves, 1)
            pool.wait_ge(halves, 4)
            for n in range(NL):
                pool.wait_ge(stat, n + 1)
                pool.tensor_tensor(rstd[:], ve[:], half[:], ALU.pow).then_inc(fact, 1)

        @block.scalar
        def _(act):
            act.wait_ge(s_w, 16 * len(loads))
            act.activation(V["beta"][:], beta[:], ACT.Exp, scale=-1.0).then_inc(act_s, 1)

        @block.tensor
        def _(pe):
            pe.wait_ge(s_w, 16 * len(loads))
            pe.transpose(ps[:, 0, 0:D], w[:], V["ident"][:]).then_inc(pe_s, 1)
            pe.wait_ge(used, NL + 1)
            pe.transpose(ps[0:2, 1, 0:P], top[:], V["ident"][:]).then_inc(pe_s, 1)
            pe.wait_ge(used, NL + 2)
            pe.matmul(ps[:, 2, 0:2], ones2[:], dia[:], start=True, stop=True).then_inc(pe_s, 1)

        @block.vector
        def _(dve):
            n_ = [0]

            def link(ins):
                n_[0] += 1
                ins.then_inc(step, 1)
                dve.wait_ge(step, n_[0])

            for n in range(NL):
                dve.wait_ge(s_h[n % 2], 16 * (n // 2 + 1))
                for j in range(K):
                    ins = dve.bn_stats(st[:, j], h[:, n % 2, j])
                link(ins)
                for j in range(K):
                    ins = dve.bn_aggr(mv[:, j], st[:, j])
                link(ins)
                dve.tensor_scalar(ve[:], mv[:, :, 1], 1e-5, None, ALU.add).then_inc(stat, 1)
                dve.tensor_reduce(lohi[:, 0], h[:, n % 2], AX.X, ALU.min)
                link(dve.tensor_reduce(lohi[:, 1], h[:, n % 2], AX.X, ALU.max))
                link(dve.tensor_tensor(lohi[:], lohi[:], mv[:, :, 0].unsqueeze(1).broadcast_to([P, 2, K]), ALU.subtract))
                dve.wait_ge(fact, n + 1)
                link(dve.tensor_tensor(lohi[:], lohi[:], rstd[:].unsqueeze(1).broadcast_to([P, 2, K]), ALU.mult))
                dve.tensor_reduce(am[:, n, 0:1], lohi[:], AX.XY, ALU.max)
                dve.tensor_reduce(am[:, n, 1:2], lohi[:], AX.XY, ALU.min).then_inc(used, 1)
            dve.wait_ge(used, NL)
            link(dve.tensor_scalar(am[:, :, 1], am[:, :, 1], -1.0, None, ALU.mult))
            dve.tensor_reduce(top[:, 0:1], am[:], AX.XY, ALU.max)
            dve.wait_ge(s_w, 16 * len(loads))
            dve.memset(ones2[:], 1.0)
            dve.tensor_reduce(top[:, 1:2], w[:], AX.X, ALU.max, apply_absolute_value=True).then_inc(used, 1)
            link(dve.tensor_copy(V["ident_bf"][:], V["ident"][:]))
            dve.wait_ge(pe_s, 1)
            link(dve.tensor_copy(wT[:], ps[:, 0, 0:D]))
            dve.wait_ge(act_s, 1)
            link(dve.tensor_scalar(V["beta"][:], V["beta"][:], 1.0, None, ALU.add))
            link(dve.reciprocal(V["beta"][:], V["beta"][:]))
            link(dve.tensor_scalar(V["rest"][:], V["beta"][:], -1.0, 1.0, ALU.mult, ALU.add))
            dve.wait_ge(pe_s, 2)
            link(dve.tensor_reduce(mrow[:], ps[0:2, 1, 0:P], AX.X, ALU.max))
            link(dve.tensor_scalar(mrow[:], mrow[:], 1e-12, None, ALU.max))
            link(dve.reciprocal(srow[:], mrow[:]))
            link(dve.tensor_scalar(srow[:], srow[:], QMAX, None, ALU.mult))
            dve.tensor_scalar(dia[:], V["ident"][0:2, 0:2], srow[:, 0:1], None, ALU.mult).then_inc(used, 1)
            dve.wait_ge(pe_s, 3)
            link(dve.tensor_copy(V["qs"][:, 0:2], ps[:, 2, 0:2]))
            link(dve.reciprocal(V["qs"][:, 2:4], V["qs"][:, 0:2]))
            link(dve.tensor_tensor(V["qs"][:, 4:5], V["qs"][:, 2:3], V["qs"][:, 3:4], ALU.mult))
            link(quantize(dve, link, V["wq"][:], wT[:], V["qs"][:, 1:2], tmp[:], mag[:]))


def scan(nc, c, V, out, nseg):
    with ExitStack() as ctx:
        sb = lambda n, s, d=F32: ctx.enter_context(nc.sbuf_tensor("sc_" + n, s, d))
        sems = []

        def sem(n):
            sems.append(ctx.enter_context(nc.semaphore("sc_" + n)))
            return sems[-1]

        ht, xn, xnn = sb("ht", [P, BG, D]), sb("xn", [P, BG, D]), sb("xnn", [P, BG, D])
        y, hb = sb("y", [P, BG, D]), sb("hb", [P, BG, D])
        st, mv, sc = sb("st", [P, BG, 6]), sb("mv", [P, BG, 2]), sb("sc", [P, 4, BG])
        tq, mq, xq = sb("tq", [P, BG, D]), sb("mq", [P, BG, D]), sb("xq", [P, BG, D], BF16)
        xT, xqT = sb("xT", [P, S]), sb("xqT", [P, S], BF16)
        uu = V["uu"]
        sig = [sb("sq", [P, 4, S]), sb("sk", [P, 4, S])]
        skN = sb("skN", [P, 4, BG, P])
        ol = sb("ol", [P, 4, BG, 2, DH])
        ee, relu = sb("ee", [P, 2, S]), sb("relu", [P, 2, S])
        ra, rb = sb("ra", [P, 2, S]), sb("rb", [P, 2, S])
        rot = [sb("qr", [P, 2, S]), sb("kr", [P, 2, S])]
        GH = 2 * BG
        ss, pT = sb("ss", [P, 2, GH, SEG]), sb("pT", [P, 4, GH, SEG])
        mx, sm = sb("mx", [P, GH]), sb("sm", [P, 4, GH])
        rk, rq = sb("rk", [P, GH]), sb("rq", [P, GH])
        t1, t2 = sb("t1", [P, 2, GH, DH]), sb("t2", [P, 2, GH, DH])
        oT = sb("oT", [P, 2, S])
        ps = ctx.enter_context(nc.psum_tensor("sc_ps", [P, 8, 512], F32))
        names = ("h_in stat fact xn_d xnn_d xq_d step xt xt_c xqt xqt_c hb_d ffn ffn_c vp v_a v_d pj ex mn rp sn sg add_d sS skt skc "
                 "smask sx se pt pvd old kr_s qr_s kd ud qd od up mu ott otc oproj ydone stored").split()
        G = {n: sem(n) for n in names}
        h_seg = c["h_d"].rearrange("(g f) (s i) d -> f s i g d", f=B1, i=SEG)
        o_seg = out.rearrange("(g f) (s i) d -> f s i g d", f=B1, i=SEG)

        def wait(eng, name, n):
            if n > 0:
                eng.wait_ge(G[name], n)

        flat = lambda ap: ap.rearrange("p g d -> p (g d)")
        by_pos = lambda ap: ap.rearrange("p (n i) -> p n i", i=SEG)
        table = lambda name, q: V[name][:, q].unsqueeze(1).broadcast_to([P, S // SEG, SEG])

        def linker(eng):
            count = [0]

            def link(ins):
                count[0] += 1
                ins.then_inc(G["step"], 1)
                eng.wait_ge(G["step"], count[0])
            return link


        def load(sp, seg):
            for f in range(B1):
                sp.dma_start(ht[32 * f:32 * f + 32], h_seg[f, bass.ds(seg, 1)].rearrange("o i g d -> (o i) g d")).then_inc(G["h_in"], 16)

        def moments(dve, link, k):
            src = (ht, xn)[k]
            wait(dve, ("h_in", "xn_d")[k], (64, 1)[k])
            for g in range(BG):
                ins = dve.bn_stats(st[:, g], src[:, g])
            link(ins)
            for g in range(BG):
                ins = dve.bn_aggr(mv[:, g], st[:, g])
            link(ins)
            dve.tensor_scalar(sc[:, 2 * k], mv[:, :, 1], 1e-5, None, ALU.add).then_inc(G["stat"], 1)

        def root(pool, k):
            wait(pool, "stat", k + 1)
            pool.tensor_tensor(sc[:, 2 * k + 1], sc[:, 2 * k], V["mhalf"][:, 0:BG], ALU.pow).then_inc(G["fact"], 1)

        def normalize(dve, k):
            dst, src = (xn, xnn)[k], (ht, xn)[k]
            wait(dve, "fact", k + 1)
            for g in range(BG):
                ins = dve.tensor_scalar(dst[:, g], src[:, g], mv[:, g, 0:1], sc[:, 2 * k + 1, g:g + 1], ALU.subtract, ALU.mult)
            ins.then_inc(G[("xn_d", "xnn_d")[k]], 1)

        def add_bias(pool):
            wait(pool, "h_in", 64)
            pool.tensor_tensor(hb[:], ht[:], V["bias"][:].unsqueeze(1).broadcast_to([P, BG, D]), ALU.add).then_inc(G["hb_d"], 1)

        def round_fp8(dve, link):
            quantize(dve, link, flat(xq[:]), flat(xn[:]), V["qs"][:, 0:1], flat(tq[:]), flat(mq[:])).then_inc(G["xq_d"], 1)

        def turn_x(pe):
            wait(pe, "xnn_d", 1)
            for g in range(BG):
                ins = pe.transpose(ps[:, 0, g * P:(g + 1) * P], xnn[:, g], V["ident"][:])
            ins.then_inc(G["xt"], 1)

        def turn_xq(pe):
            wait(pe, "xq_d", 1)
            for g in range(BG):
                ins = pe.transpose(ps[:, 1, 0:256].bitcast(BF16)[:, g * P:(g + 1) * P], xq[:, g], V["ident_bf"][:])
            ins.then_inc(G["xqt"], 1)

        def take_x(act):
            wait(act, "xt", 1)
            act.activation(xT[:], ps[:, 0, :], ACT.Identity, bias=V["b"][:, 0:1], scale=V["g"][:, 0:1]).then_inc(G["xt_c"], 1)

        def take_xq(act):
            wait(act, "xqt", 1)
            act.copy(xqT[:], ps[:, 1, 0:256].bitcast(BF16)).then_inc(G["xqt_c"], 1)

        def prepare(seg):
            with nc.Block() as block:

                @block.sync
                def _(sp):
                    load(sp, seg)

                @block.vector
                def _(dve):
                    link = linker(dve)
                    for k in range(2):
                        moments(dve, link, k)
                        normalize(dve, k)
                    round_fp8(dve, link)

                @block.gpsimd
                def _(pool):
                    for k in range(2):
                        root(pool, k)
                    add_bias(pool)

                @block.tensor
                def _(pe):
                    turn_x(pe)
                    turn_xq(pe)

                @block.scalar
                def _(act):
                    take_x(act)
                    take_xq(act)

        STEPS = PAIRS + 4
        inside = lambda p: 0 <= p < PAIRS

        def turn(seg, following):
            with nc.Block() as block:

                @block.sync
                def _(sp):
                    if following is not None:
                        load(sp, following)
                    wait(sp, "ydone", 1)
                    for f in range(B1):
                        sp.dma_start(o_seg[f, bass.ds(seg, 1)].rearrange("o i g d -> (o i) g d"), y[32 * f:32 * f + 32]).then_inc(G["stored"], 16)
                    sp.wait_ge(G["stored"], 64)

                @block.gpsimd
                def _(pool):
                    def features(n):
                        p, which = divmod(n, 2)
                        wait(pool, "mn", n + 1)
                        wait(pool, "qr_s", p - 3)
                        wait(pool, "skt", p - 3)
                        pool.tensor_tensor(sig[which][:, p % 4], ee[:, n % 2], relu[:, n % 2], ALU.add).then_inc(G["sg"], 1)
                        wait(pool, "rp", n + 1)
                        pool.tensor_tensor(by_pos(rb[:, n % 2]), by_pos(rb[:, n % 2]), table("sin", which), ALU.mult).then_inc(G["sn"], 1)
                        wait(pool, "sn", n + 1)
                        wait(pool, "sS", p - 1)
                        pool.tensor_tensor(rot[which][:, p % 2], ra[:, n % 2], rb[:, n % 2], ALU.add).then_inc(G["add_d"], 1)

                    for s in range(STEPS):
                        p = s - 2
                        if s < PAIRS:
                            features(2 * s)
                        if inside(p):
                            new = uu[:, :, 2 * p:2 * p + 2, 0:DH]
                            wait(pool, "kd", p + 1)
                            wait(pool, "pvd", p + 1)
                            pool.tensor_tensor(new, new, t1[:, p % 2].rearrange("p (g h) d -> p g h d", h=2), ALU.subtract).then_inc(G["ud"], 1)
                        if s < PAIRS:
                            features(2 * s + 1)
                        if inside(p):
                            wait(pool, "qd", p + 1)
                            wait(pool, "old", p + 1)
                            o = ol[:, p % 4].rearrange("p g h d -> p (g h d)")
                            pool.tensor_tensor(o, o, t2[:, p % 2].rearrange("p c d -> p (c d)"), ALU.add).then_inc(G["od"], 1)
                        if following is not None:
                            if s in (1, 3):
                                root(pool, s // 2)
                            if s == 5:
                                wait(pool, "ffn_c", 1)
                                add_bias(pool)

                @block.tensor
                def _(pe):
                    def project(n):
                        p, which = divmod(n, 2)
                        wait(pe, "rp", n - 1)
                        col = 1024 * which + p * P
                        pe.matmul(ps[:, n % 2, :], V["wqkv"][:, col:col + P], xT[:], start=True, stop=True).then_inc(G["pj"], 1)

                    def values(n):
                        g, half = divmod(n, 2)
                        if n >= 4:
                            wait(pe, "v_a" if n % 2 == 0 else "v_d", n // 2 - 1)
                        pe.matmul(ps[:, 2 + n % 4, :], xT[:, g * P:(g + 1) * P], V["wqkv"][:, 2048 + 512 * half:2560 + 512 * half],
                                  start=True, stop=True).then_inc(G["vp"], 1)

                    def recall(p, which, done):
                        for g in range(BG):
                            for f in range(B1):
                                at_ = g * P + 32 * f
                                ins = pe.matmul(ps[32 * f:32 * f + 32, 2 + g // 2, (g % 2) * 2 * VE:(g % 2 + 1) * 2 * VE],
                                                sig[which][:, p % 4, at_:at_ + 32], V["mem"][:, p, 4 * g + f, :], start=True, stop=True)
                        ins.then_inc(G[done], 1)

                    def update(p, fs):
                        for f in fs:
                            for g in range(BG):
                                for hh in range(2):
                                    ins = pe.matmul(ps[64 * hh:64 * hh + 64, 4 + f % 2, g * VE:(g + 1) * VE],
                                                    skN[32 * f:32 * f + 32, p % 4, g, 64 * hh:64 * hh + 64],
                                                    uu[32 * f:32 * f + 32, g, 2 * p + hh, :], start=True, stop=True)
                        ins.then_inc(G["up"], 1)

                    for s in range(STEPS):
                        if s < PAIRS:
                            project(2 * s)
                        p = s - 2
                        if inside(p):
                            wait(pe, "sg", 2 * p + 2)
                            if p == 0:
                                wait(pe, "v_a", 4)
                                wait(pe, "v_d", 4)
                            wait(pe, "qd", p)
                            recall(p, 1, "kr_s")
                            wait(pe, "pt", p + 1)
                            if p == 0:
                                wait(pe, "ffn_c", 1)
                            wait(pe, "skc", p + 1)
                            wait(pe, "otc", p - 1)
                            for g in range(BG):
                                for hh in range(2):
                                    for f in range(B1):
                                        ch = 2 * g + hh
                                        ins = pe.matmul(ps[32 * f:32 * f + 32, 6, ch * DH:(ch + 1) * DH], pT[32 * f:32 * f + 32, p % 4, ch, :],
                                                        uu[32 * f:32 * f + 32, g, 2 * p + hh, 0:DH], start=True, stop=True)
                            ins.then_inc(G["pvd"], 1)
                        p = s - 1
                        if inside(p):
                            wait(pe, "add_d", 2 * p + 2)
                            if p == 0:
                                wait(pe, "v_a", 4)
                                wait(pe, "v_d", 4)
                            wait(pe, "mu", 2 * (s - 3))
                            for hh in range(2):
                                for g in range(BG):
                                    for f in range(B1):
                                        cols = slice(g * P + 32 * f, g * P + 32 * f + 32)
                                        ins = pe.matmul(ps[32 * f:32 * f + 32, 4 + hh, g * SEG:(g + 1) * SEG],
                                                        rot[0][64 * hh:64 * hh + 64, p % 2, cols], rot[1][64 * hh:64 * hh + 64, p % 2, cols],
                                                        start=True, stop=True)
                            ins.then_inc(G["sS"], 1)
                        if s < PAIRS:
                            project(2 * s + 1)
                        if s == 0:
                            for n in range(8):
                                values(n)
                            for g in range(BG):
                                ins = pe.matmul(ps[:, 6, g * P:(g + 1) * P], xqT[:, g * P:(g + 1) * P], V["wq"][:], start=True, stop=True)
                            ins.then_inc(G["ffn"], 1)
                        p = s - 2
                        if inside(p):
                            wait(pe, "kd", p + 1)
                            recall(p, 0, "qr_s")
                        p = s - 1
                        if inside(p):
                            wait(pe, "sg", 2 * p + 2)
                            wait(pe, "ffn_c", 1)
                            wait(pe, "old", p)
                            for g in range(BG):
                                ins = pe.transpose(ps[:, 6, g * P:(g + 1) * P], sig[1][:, p % 4, g * P:(g + 1) * P], V["ident"][:])
                            ins.then_inc(G["skt"], 1)
                        p = s - 3
                        if inside(p):
                            wait(pe, "ud", p + 1)
                            wait(pe, "skc", p + 1)
                            wait(pe, "smask", min(s, PAIRS))
                            wait(pe, "mu", 2 * p)
                            update(p, (0, 1))
                            wait(pe, "od", p + 1)
                            wait(pe, "skc", min(s, PAIRS))
                            wait(pe, "old", min(p + 2, PAIRS))
                            wait(pe, "otc", p)
                            for g in range(BG):
                                ins = pe.transpose(ps[:, 6, g * P:(g + 1) * P], ol[:, p % 4, g].rearrange("p h d -> p (h d)"), V["ident"][:])
                            ins.then_inc(G["ott"], 1)
                        p = s - 4
                        if inside(p):
                            wait(pe, "otc", p + 1)
                            for g in range(BG):
                                ins = pe.matmul(ps[:, 7, g * P:(g + 1) * P], oT[:, p % 2, g * P:(g + 1) * P], V["wout"][:, p],
                                                start=(p == 0 and g == 0), stop=(p == PAIRS - 1 and g == BG - 1))
                            ins.then_inc(G["oproj"], 1)
                        p = s - 3
                        if inside(p):
                            wait(pe, "mu", 2 * p + 1)
                            update(p, (2, 3))
                        if following is not None:
                            if s == PAIRS:
                                wait(pe, "rp", 2 * PAIRS)
                                turn_x(pe)
                            if s == PAIRS + 2:
                                turn_xq(pe)

                @block.scalar
                def _(act):
                    def features(n):
                        wait(act, "pj", n + 1)
                        wait(act, "sg", n - 1)
                        act.activation(ee[:, n % 2], ps[:, n % 2, :], ACT.Relu, scale=-1.0)
                        act.activation(relu[:, n % 2], ps[:, n % 2, :], ACT.Relu).then_inc(G["ex"], 1)
                        wait(act, "ex", n + 1)
                        act.activation(ee[:, n % 2], ee[:, n % 2], ACT.Exp, scale=-1.0).then_inc(G["mn"], 1)

                    def values(n):
                        wait(act, "vp", n + 1)
                        act.copy(uu[:, n // 2, 0:8, 0:DH], ps[:, 2 + n % 4, :].rearrange("p (h d) -> p h d", d=DH)).then_inc(G["v_a"], 1)

                    for s in range(STEPS):
                        if s < PAIRS:
                            features(2 * s)
                            features(2 * s + 1)
                        if s == 0:
                            for n in range(0, 8, 2):
                                values(n)
                        p = s - 1
                        if inside(p):
                            wait(act, "sx", p + 1)
                            act.activation(ss[:, p % 2], ss[:, p % 2], ACT.Exp).then_inc(G["se"], 1)
                            wait(act, "skt", p + 1)
                            wait(act, "up", 2 * (p - 3))
                            act.copy(skN[:, p % 4].rearrange("p g r -> p (g r)"), ps[:, 6, :]).then_inc(G["skc"], 1)
                        p = s - 3
                        if inside(p):
                            wait(act, "ott", p + 1)
                            wait(act, "oproj", p - 1)
                            act.copy(oT[:, p % 2], ps[:, 6, :]).then_inc(G["otc"], 1)
                        if following is not None:
                            if s == PAIRS:
                                take_x(act)
                            if s == PAIRS + 2:
                                take_xq(act)

                @block.vector
                def _(dve):
                    link = linker(dve)

                    def rope(n):
                        wait(dve, "ex", n + 1)
                        wait(dve, "add_d", n - 1)
                        dve.stream_shuffle(rb[:, n % 2], ps[:, n % 2, :], [lane ^ 1 for lane in range(32)])
                        dve.tensor_tensor(by_pos(ra[:, n % 2]), by_pos(ps[:, n % 2, :]), table("cos", n % 2), ALU.mult).then_inc(G["rp"], 1)

                    def values(n):
                        wait(dve, "vp", n + 1)
                        dve.tensor_copy(uu[:, n // 2, 8:16, 0:DH], ps[:, 2 + n % 4, :].rearrange("p (h d) -> p h d", d=DH)).then_inc(G["v_d"], 1)

                    recalled = ps[:, 2:4, 0:4 * VE].rearrange("p b (c v) -> p b c v", v=VE)
                    by_bank = lambda ap: ap.rearrange("p (b c) d -> p b c d", b=2)

                    def update(p, k):
                        wait(dve, "up", 2 * p + k + 1)
                        for hh in range(2):
                            rows = slice(64 * hh, 64 * hh + 64)
                            m = V["mem"][rows, p].rearrange("p (g f) v -> p f g v", f=B1)[:, 2 * k:2 * k + 2, :, hh * VE:(hh + 1) * VE]
                            ins = dve.tensor_tensor(m, m, ps[rows, 4:6, 0:BG * VE].rearrange("p b (g v) -> p b g v", g=BG), ALU.add)
                        ins.then_inc(G["mu"], 1)

                    for s in range(STEPS):
                        if s < PAIRS:
                            rope(2 * s)
                        p = s - 2
                        if inside(p):
                            wait(dve, "kr_s", p + 1)
                            link(dve.reciprocal(rk[:].rearrange("p (b c) -> p b c", b=2), recalled[:, :, :, DH]))
                            wait(dve, "ud", p - 1)
                            dve.tensor_tensor(by_bank(t1[:, p % 2]), recalled[:, :, :, 0:DH],
                                              bc(rk[:].rearrange("p (b c) -> p b c", b=2), DH), ALU.mult).then_inc(G["kd"], 1)
                            wait(dve, "pvd", p + 1)
                            wait(dve, "pt", p + 1)
                            wait(dve, "ott", p - 3)
                            dve.tensor_tensor(ol[:, p % 4].rearrange("p g h d -> p (g h) d"), ps[:, 6, :].rearrange("p (c d) -> p c d", d=DH),
                                              bc(sm[:, p % 4], DH), ALU.mult).then_inc(G["old"], 1)
                        p = s - 1
                        if inside(p):
                            wait(dve, "sS", p + 1)
                            by_head = ss[:, p % 2].rearrange("p (g h) j -> p h g j", h=2)
                            dve.tensor_tensor(by_head, ps[:, 4:6, 0:P].rearrange("p b (g j) -> p b g j", j=SEG),
                                              V["mask"][:].unsqueeze(1).unsqueeze(1).broadcast_to([P, 2, BG, SEG]), ALU.add).then_inc(G["smask"], 1)
                            wait(dve, "smask", p + 1)
                            link(dve.tensor_reduce(mx[:], ss[:, p % 2], AX.X, ALU.max))
                            dve.tensor_tensor(ss[:, p % 2], ss[:, p % 2], bc(mx[:], SEG), ALU.subtract).then_inc(G["sx"], 1)
                        if s < PAIRS:
                            rope(2 * s + 1)
                        if s == 0:
                            for n in range(1, 8, 2):
                                values(n)
                            wait(dve, "ffn", 1)
                            dve.scalar_tensor_tensor(flat(y[:]), ps[:, 6, :], V["qs"][:, 4:5], flat(hb[:]), ALU.mult, ALU.add).then_inc(G["ffn_c"], 1)
                        p = s - 2
                        if inside(p):
                            wait(dve, "qr_s", p + 1)
                            r = rq[:].rearrange("p (b c) -> p b c", b=2)
                            link(dve.tensor_scalar(r, recalled[:, :, :, DH], 1e-6, None, ALU.add))
                            link(dve.reciprocal(rq[:], rq[:]))
                            share = V["beta"][:, 2 * p:2 * p + 2].unsqueeze(1).broadcast_to([P, BG, 2])
                            pairs = rq[:].rearrange("p (g h) -> p g h", h=2)
                            link(dve.tensor_tensor(pairs, pairs, share, ALU.mult))
                            wait(dve, "od", p - 1)
                            dve.tensor_tensor(by_bank(t2[:, p % 2]), recalled[:, :, :, 0:DH], bc(r, DH), ALU.mult).then_inc(G["qd"], 1)
                        p = s - 3
                        if inside(p):
                            update(p, 0)
                        p = s - 1
                        if inside(p):
                            wait(dve, "se", p + 1)
                            dve.transpose(pT[:, p % 4].rearrange("p c j -> p (c j)"), ss[:, p % 2].rearrange("p c j -> p (c j)"))
                            s_ = sm[:, p % 4]
                            link(dve.tensor_reduce(s_, ss[:, p % 2], AX.X, ALU.add))
                            link(dve.reciprocal(s_, s_))
                            share = V["rest"][:, 2 * p:2 * p + 2].unsqueeze(1).broadcast_to([P, BG, 2])
                            pairs = s_.rearrange("p (g h) -> p g h", h=2)
                            dve.tensor_tensor(pairs, pairs, share, ALU.mult).then_inc(G["pt"], 1)
                        p = s - 3
                        if inside(p):
                            update(p, 1)
                        if following is not None:
                            if s in (1, 3):
                                moments(dve, link, s // 2)
                            if s in (2, 4):
                                normalize(dve, s // 2 - 1)
                            if s == PAIRS:
                                round_fp8(dve, link)
                    wait(dve, "oproj", PAIRS)
                    wait(dve, "ffn_c", 1)
                    dve.tensor_tensor(flat(y[:]), flat(y[:]), ps[:, 7, :], ALU.add).then_inc(G["ydone"], 1)

        clear(nc, sems)
        prepare(0)
        if nseg > 1:
            with nc.Fori(0, nseg - 1) as i:
                clear(nc, sems)
                turn(i, i + 1)
        clear(nc, sems)
        turn(nseg - 1, None)


def block1_tensors(nc, ctx):
    sb = lambda n, s, d=F32: ctx.enter_context(nc.sbuf_tensor("v_" + n, s, d))
    shapes = dict(wqkv=[P, 3072], wout=[P, PAIRS, D], g=[P, 1], b=[P, 1], bias=[P, D], beta=[P, H], rest=[P, H],
                  ident=[P, P], cos=[P, 2, SEG], sin=[P, 2, SEG], mask=[P, SEG], qs=[P, 5], mem=[P, PAIRS, NB, 2 * VE],
                  uu=[P, BG, H, VE], mhalf=[P, BG])
    V = {n: sb(n, s) for n, s in shapes.items()}
    V["wq"], V["ident_bf"] = sb("wq", [P, D], BF16), sb("ident_bf", [P, P], BF16)
    return V


def weights(nc, ctx):
    sb = lambda n, s, d=F32: ctx.enter_context(nc.sbuf_tensor("w_" + n, s, d))
    shapes = dict(wqA=[P, D], mk=[P, D], mv=[P, D], woA=[P, D], woB=[P, D], wB=[P, 5 * D], ident=[P, P],
                  decay=[P, NC, S], cmask=[P, S], hsum=[P, H], g2b=[P, D], wr=[P, E], mhalf=[P, 64],
                  nmax=[H, 2 * NB])
    W = {n: sb(n, s) for n, s in shapes.items()}
    W["ident_bf"], W["cmaskT"], W["flag"] = sb("ident_bf", [P, P], BF16), sb("cmaskT", [P, P], BF16), sb("flag", [1, 1], I32)
    return W


def shape_constants():
    f32 = np.float32
    pos = np.arange(S, dtype=f32)
    d = np.exp(f32(-0.01 * 0.01) * np.abs(pos[:, None] - pos[None, :])).astype(f32)
    decay = d.reshape(NC, P, S).transpose(1, 0, 2).copy()
    cmask = np.zeros((P, S), f32)
    cmask[:, S - P:] = np.where(np.arange(P)[None, :] <= np.arange(P)[:, None], 0.0, MASKED)
    hsum = (np.arange(P)[:, None] % H == np.arange(H)[None, :]).astype(f32)
    cmaskT = np.where(np.arange(P)[:, None] <= np.arange(P)[None, :], 0.0, MASKED).astype(f32)
    theta = (f32(10000.0) ** (f32(-2.0) * (np.arange(HD // 2, dtype=f32) / HD))).astype(f32)
    ang = (pos[:, None] * theta[None, :]).astype(f32)
    feature = np.arange(P) // H
    sign = np.where(feature % 2 == 0, -1.0, 1.0).astype(f32)
    cos, sin = np.cos(ang)[:, feature // 2].T, np.sin(ang)[:, feature // 2].T * sign[:, None]
    rope = np.stack([cos * f32(SCALE_B), sin * f32(SCALE_B), cos, sin], 1).astype(f32)
    seq = np.arange(P)
    low = np.broadcast_to((np.arange(E)[None, :] < np.arange(E)[:, None]).reshape(1, E * E), (P, E * E)).astype(f32)
    restart = np.broadcast_to((np.arange(E * NT) % NT != 0).astype(f32)[None], (P, E * NT)).copy()
    slots = np.broadcast_to((np.arange(E * CAP) % CAP).astype(f32)[None], (P, E * CAP)).copy()
    ptid = np.stack([np.broadcast_to(seq[:, None], (P, NT)), np.broadcast_to(np.arange(NT)[None], (P, NT))], 2)
    route = dict(low=low, before=(seq[:, None] < seq[None, :]).astype(f32), restart=restart, slots=slots,
                 ptid=ptid.reshape(P, 2 * NT).astype(f32), mix=np.array([[1, NT], [P, 1]], f32))
    freqs = f32(10000.0) ** (-np.arange(0, DH, 2, dtype=f32) / f32(DH))
    ang1 = (np.arange(SEG, dtype=f32)[:, None] * freqs[None, :]).astype(f32)
    row1, sign1 = (seq % DH) // 2, np.where(seq % 2 == 0, -1.0, 1.0).astype(f32)
    cos1 = np.cos(ang1)[:, row1].T.astype(f32)
    sin1 = (np.sin(ang1)[:, row1].T * sign1[:, None]).astype(f32)
    per_side = lambda t: np.stack([t * f32(DH ** -0.5), t], 1).copy()
    i, j = np.arange(P)[:, None] % SEG, np.arange(SEG)[None, :]
    scan = dict(cos1=per_side(cos1), sin1=per_side(sin1), mask1=np.where(j <= i, 0.0, MASKED).astype(f32))
    return dict(**route, **scan, ident=np.eye(P, dtype=f32), decay=decay, cmask=cmask,
                hsum=hsum, cmaskT=cmaskT, rope=rope)


def inputs_of(a):
    c = dict(
        x=a["L0_attn_x"], Wq=a["L0_attn_Wq"], Wk=a["L0_attn_Wk"], Wv=a["L0_attn_Wv"], WoA=a["L0_attn_Wo"],
        Wdown=a["L0_attn_W_down_kv"], Wuk=a["L0_attn_W_up_k"], Wuv=a["L0_attn_W_up_v"],
        g1=a["L0_ffn_g1"].reshape(P, 1), Wqkv=a["L0_ffn_w_qkv"], WoB=a["L0_ffn_w_o"],
        g2b=np.broadcast_to(a["L0_ffn_g2"].reshape(1, D), (P, D)), Wr=a["L0_ffn_w_router"], w1=a["L0_ffn_w1"], w2=a["L0_ffn_w2"],
        w1qkv=a["L1_attn_w_qkv"], wout=a["L1_attn_w_out"], ln_g=a["L1_attn_ln_g"].reshape(P, 1), ln_b=a["L1_attn_ln_b"].reshape(P, 1),
        beta=np.broadcast_to(a["L1_attn_mem_beta"].reshape(1, H), (P, H)), wffn=a["L1_ffn_weight"],
        bias=np.broadcast_to(a["L1_ffn_bias"].reshape(1, D), (P, D)))
    c.update(shape_constants())
    return c


def scratch(nc):
    shapes = dict(xn=((NB, S, D), F32), v=((NB * 2, P, NC * VW), F32), parts=((NB * 4, 5, P, S), BF16),
                  on=((NB * 2, P, NC * D), F32), x1=((NB, S, D), F32), h=((NB, S, D), F32), xf=((NB, S, D), F32),
                  pr=((P, NB, NC, E), F32), gate=((NT * P, E), F32))
    return {n + "_d": nc.dram_tensor(n + "_scratch", shape, dt, kind="Internal").ap() for n, (shape, dt) in shapes.items()}


def program(nc, c):
    c.update(scratch(nc))
    with ExitStack() as ctx:
        W = weights(nc, ctx)
        R = {"rows": ctx.enter_context(nc.sbuf_tensor("rows", [P, 2 * E, 2], U32))}
        fold_weights(nc, c, W)
        front(nc, c, W, NB)
        attend(nc, c, W, NB)
        tail(nc, c, W, NB)
        bound_flag(nc, W, NB)
        flag = nc.values_load(W["flag"][0:1, 0:1], min_val=0, max_val=1)
        with nc.If(flag > 0):
            attend_any(nc, c, W, NB)
        route(nc, c, W, R)
        experts(nc, c, W, R)
    with ExitStack() as ctx:
        V = block1_tensors(nc, ctx)
        scale_factors(nc, c, V)
        scan(nc, c, V, c["out"], NSEG)


def kernel(**inputs):
    import concourse.bacc as _bacc
    from concourse.bass_utils import run_bass_kernel_spmd as _run

    nc = _bacc.Bacc("TRN2", target_bir_lowering=False, num_devices=1)
    arrays, c = {}, {}
    for name, a in inputs_of({k: np.asarray(v) for k, v in inputs.items()}).items():
        a = np.ascontiguousarray(a)
        arrays["in_" + name] = a
        c[name] = nc.dram_tensor("in_" + name, a.shape, mybir.dt.from_np(a.dtype), kind="ExternalInput").ap()
    c["out"] = nc.dram_tensor("out_dram", (NB, S, D), F32, kind="ExternalOutput").ap()
    program(nc, c)
    return _run(nc, [arrays], core_ids=[0]).results[0]["out_dram"]
```

```python
from contextlib import ExitStack

import numpy as np
import concourse.bass as bass
from concourse import mybir

F32 = mybir.dt.float32
BF16 = mybir.dt.bfloat16
I32 = mybir.dt.int32
U32 = mybir.dt.uint32
ALU = mybir.AluOpType
ACT = mybir.ActivationFunctionType
AX = mybir.AxisListType

P = 128
NB, S, D = 16, 512, 128
NC = S // P
NT = NB * S // P
H, HD = 16, 8
NG = H // 4
E, TOPK, FF = 8, 2, 256
CAP = 160
HALF = CAP // 2
CLAMP = 10000.0
SCALE_A = float(1.0 / (np.sqrt(np.float32(128.0)) + 1e-8))
SCALE_B = float(1.0 / np.sqrt(np.float32(HD)))
UNITS = H * NC
MASKED = -1e30


def bc(ap, n):
    return ap.unsqueeze(len(ap.shape)).broadcast_to(list(ap.shape) + [n])


def clear(nc, sems):
    nums = sorted(s.num for s in sems)
    starts = [n for n in nums if n - 1 not in nums]
    ends = [n + 1 for n in nums if n + 1 not in nums]
    for a, b in zip(starts, ends):
        nc.sync.sem_clear(range(a, b))
    nc.all_engine_barrier()


def fold_weights(nc, c, W):
    with ExitStack() as ctx:
        sb = lambda n, s, d=F32: ctx.enter_context(nc.sbuf_tensor(n, s, d))
        sem = lambda n: ctx.enter_context(nc.semaphore(n))
        wk, wv, wsum, wsumT = sb("fw_k", [P, D]), sb("fw_v", [P, D]), sb("fw_s", [P, D]), sb("fw_sT", [P, D])
        wd, wuk, wuv = sb("fw_d", [P, 32]), sb("fw_uk", [32, D]), sb("fw_uv", [32, D])
        bT = sb("fw_bT", [32, D])
        wqkv, wqkv_g, g1 = sb("fw_qkv", [P, 3 * D]), sb("fw_qkv_g", [P, 3 * D]), sb("fw_g1", [P, 1])
        wq, cmaskT = sb("fw_q", [P, D]), sb("fw_cmaskT", [P, P])
        ps = ctx.enter_context(nc.psum_tensor("fw_ps", [P, 4, 512], F32))
        s_in, s_sum, s_pe, s_cp = sem("fw_in"), sem("fw_sum"), sem("fw_pe"), sem("fw_cp")
        block = ctx.enter_context(nc.Block())
        loads = [(wk, c["Wk"]), (wv, c["Wv"]), (wd, c["Wdown"]), (wuk, c["Wuk"]), (wuv, c["Wuv"]),
                 (wqkv, c["Wqkv"]), (g1, c["g1"]), (wq, c["Wq"]), (W["woA"], c["WoA"]), (W["woB"], c["WoB"]),
                 (W["ident"], c["ident"]), (W["hsum"], c["hsum"]), (cmaskT, c["cmaskT"]),
                 (W["decay"], c["decay"]), (W["cmask"], c["cmask"]), (W["g2b"], c["g2b"]), (W["wr"], c["Wr"])]
        by_head = lambda ap: ap.rearrange("p (h d) -> p h d", d=HD)
        by_feature = lambda ap: ap.rearrange("p (d h) -> p h d", d=HD)

        @block.sync
        def _(sp):
            for dst, src in loads:
                sp.dma_start(dst[:], src).then_inc(s_in, 16)

        @block.vector
        def _(dve):
            dve.wait_ge(s_in, 16 * len(loads))
            dve.tensor_tensor(wsum[:], wk[:], wv[:], ALU.add).then_inc(s_sum, 1)
            dve.tensor_scalar(wqkv_g[:], wqkv[:], g1[:, 0:1], None, ALU.mult).then_inc(s_sum, 1)
            dve.tensor_copy(by_feature(W["wqA"][:]), by_head(wq[:]))
            dve.tensor_copy(W["ident_bf"][:], W["ident"][:])
            dve.tensor_copy(W["cmaskT"][:], cmaskT[:])
            dve.memset(W["mhalf"][:], -0.5)
            dve.wait_ge(s_sum, 2)
            dve.tensor_copy(W["wB"][:, 2 * D:3 * D], wqkv_g[:, 2 * D:3 * D])
            for t in range(2):
                src = by_head(wqkv_g[:, t * D:(t + 1) * D])
                dve.tensor_copy(by_feature(W["wB"][:, t * D:(t + 1) * D]), src)
                pairs = src.rearrange("p h (n two) -> p h n two", two=2)
                dst = by_feature(W["wB"][:, (3 + t) * D:(4 + t) * D]).rearrange("p h (n two) -> p h n two", two=2)
                dve.tensor_copy(dst[:, :, :, 0], pairs[:, :, :, 1])
                dve.tensor_copy(dst[:, :, :, 1], pairs[:, :, :, 0])
            dve.wait_ge(s_pe, 1)
            dve.tensor_copy(wsumT[:], ps[:, 0, 0:D]).then_inc(s_cp, 1)
            dve.wait_ge(s_pe, 2)
            dve.tensor_copy(bT[:], ps[0:32, 1, 0:D]).then_inc(s_cp, 1)
            dve.wait_ge(s_pe, 4)
            dve.tensor_copy(by_feature(W["mk"][:]), by_head(ps[:, 2, 0:D]))
            dve.tensor_copy(W["mv"][:], ps[:, 3, 0:D]).then_inc(s_cp, 1)
            dve.wait_ge(s_cp, 3)

        @block.tensor
        def _(pe):
            pe.wait_ge(s_sum, 1)
            pe.transpose(ps[:, 0, 0:D], wsum[:], W["ident"][:]).then_inc(s_pe, 1)
            pe.wait_ge(s_cp, 1)
            pe.matmul(ps[0:32, 1, 0:D], wd[:], wsumT[:], start=True, stop=True).then_inc(s_pe, 1)
            pe.wait_ge(s_cp, 2)
            pe.matmul(ps[:, 2, 0:D], bT[:], wuk[:], start=True, stop=True).then_inc(s_pe, 1)
            pe.matmul(ps[:, 3, 0:D], bT[:], wuv[:], start=True, stop=True).then_inc(s_pe, 1)


VW = H * (HD + 1) + 32
ROWS = 9 * HD
LIMIT = 64.0


def front(nc, c, W, nb, K=4):
    with ExitStack() as ctx:
        sb = lambda n, s, d=F32: ctx.enter_context(nc.sbuf_tensor("fr_" + n, s, d))
        sems = []

        def sem(n):
            sems.append(ctx.enter_context(nc.semaphore("fr_" + n)))
            return sems[-1]

        x, xn, hn = sb("x", [P, K, NC, D]), sb("xn", [P, K, NC, D]), sb("hn", [P, K, NC, D])
        st, mv, sc = sb("st", [P, K, NC, 6]), sb("mv", [P, K, NC, 2]), sb("sc", [P, K, 5, NC])
        xnT, hnT = sb("xnT", [P, K, S]), sb("hnT", [P, K, S])
        r = sb("r", [P, 2, 4, S])
        qk = sb("qk", [P, K, 4, S])
        sq = sb("sq", [P, 2, 2, S])
        res = sb("res", [P, 2, 4, S])
        parts = sb("parts", [P, K, 4, 3, S], BF16)
        v = sb("v", [P, K, 2, NC, VW])
        rope = sb("rope", [P, 4, S])
        rope_in = ctx.enter_context(nc.semaphore("fr_rope_in"))
        ps = ctx.enter_context(nc.psum_tensor("fr_ps", [P, 8, 512], F32))
        x_in = [sem(f"x_in{n}") for n in range(K // 2)]
        stats, factors, normed, v_step, p_step = (sem(n) for n in "stats factors normed v_step p_step".split())
        turned, turned_cp, pa, qa_cp, ka_cp, va_cp = (sem(n) for n in "turned turned_cp pa qa_cp ka_cp va_cp".split())
        pb, roped_ps, roped, vb_cp, squared, normsq, nmax = (sem(n) for n in "pb roped_ps roped vb_cp squared normsq nmax".split())
        part1, rest1, part2, part3, stored = (sem(n) for n in "part1 rest1 part2 part3 stored".split())

        with nc.Block() as block:

            @block.sync
            def _(sp):
                sp.dma_start(rope[:], c["rope"]).then_inc(rope_in, 16)
                sp.wait_ge(rope_in, 16)

            @block.gpsimd
            def _(pool):
                pool.memset(v[:], 1.0)

        with nc.Fori(0, nb // K) as i:
            clear(nc, sems)
            with nc.Block() as block:

                @block.sync
                def _(sp):
                    for k in range(K):
                        sp.dma_start(x[:, k], c["x"][bass.ds(i * K + k, 1)].rearrange("o (c p) d -> p (o c) d", p=P)).then_inc(x_in[k // 2], 16)
                    n = 0
                    for first in range(0, K, 2):
                        two = (first, first + 1)
                        for k in two:
                            sp.wait_ge(normed, k + 1)
                            sp.dma_start(c["xn_d"][bass.ds(i * K + k, 1)].rearrange("o (c p) d -> p (o c) d", p=P), xn[:, k]).then_inc(stored, 16)
                            n += 1
                        for k in two:
                            for a in range(2):
                                sp.wait_ge((va_cp, vb_cp)[a], k + 1)
                                sp.dma_start(c["v_d"][bass.ds((i * K + k) * 2 + a, 1)].rearrange("o p f -> p (o f)"),
                                             v[:, k, a].rearrange("p c f -> p (c f)")).then_inc(stored, 16)
                                n += 1
                        for k in two:
                            for t in range(4):
                                sp.wait_ge(part3, 4 * k + t + 1)
                                dst = c["parts_d"][bass.ds((i * K + k) * 4 + t, 1)].rearrange("o s p f -> p (o s) f")
                                sp.dma_start(dst[:, 0:3], parts[:, k, t]).then_inc(stored, 16)
                                n += 1
                                if t % 2 == 0:
                                    sp.dma_start(dst[:, 3:5], parts[:, k, t, 0:2]).then_inc(stored, 16)
                                    n += 1
                    sp.wait_ge(stored, 16 * n)

                @block.gpsimd
                def _(pool):
                    step = [0]

                    def link(ins):
                        step[0] += 1
                        ins.then_inc(p_step, 1)
                        pool.wait_ge(p_step, step[0])

                    for n in range(K // 2):
                        two = slice(2 * n, 2 * n + 2)
                        s_, var = (lambda row: sc[:, two, row]), mv[:, two, :, 1]
                        half = W["mhalf"][:, 0:2 * NC].rearrange("p (k c) -> p k c", k=2)
                        pool.wait_ge(stats, n + 1)
                        link(pool.tensor_scalar(s_(0), var, 1e-5, None, ALU.add))
                        link(pool.tensor_tensor(s_(1), s_(0), half, ALU.pow))
                        link(pool.tensor_tensor(s_(2), var, s_(1), ALU.mult))
                        link(pool.tensor_tensor(s_(2), s_(2), s_(1), ALU.mult))
                        link(pool.tensor_scalar(s_(2), s_(2), 1e-6, None, ALU.add))
                        link(pool.tensor_tensor(s_(3), s_(2), half, ALU.pow))
                        pool.tensor_tensor(s_(4), s_(1), s_(3), ALU.mult).then_inc(factors, 1)

                    def rest(k, t):
                        pool.wait_ge(part1, 4 * k + t + 1)
                        if k >= 2:
                            pool.wait_ge(part3, 4 * (k - 2) + t + 1)
                        pool.tensor_tensor(res[:, k % 2, t], qk[:, k, t], parts[:, k, t, 0], ALU.subtract).then_inc(rest1, 1)

                    for k in range(K):
                        pool.wait_ge(qa_cp, k + 1)
                        pool.wait_ge(ka_cp, k + 1)
                        if k >= 2:
                            pool.wait_ge(normsq, k - 1)
                        for t in range(2):
                            ins = pool.tensor_tensor(sq[:, k % 2, t], qk[:, k, t], qk[:, k, t], ALU.mult)
                        ins.then_inc(squared, 1)
                        rest(k, 0)
                        rest(k, 1)
                        for t in range(2):
                            pool.wait_ge(roped_ps, 4 * k + 2 * t + 2)
                            pool.tensor_tensor(qk[:, k, 2 + t], r[:, k % 2, 2 * t], r[:, k % 2, 2 * t + 1], ALU.add).then_inc(roped, 1)
                        rest(k, 2)
                        rest(k, 3)


                @block.tensor
                def _(pe):
                    def turn(k):
                        B = 4 * (k % 2)
                        pe.wait_ge(normed, k + 1)
                        if k >= 2:
                            pe.wait_ge(roped_ps, 4 * (k - 2) + 4)
                            pe.wait_ge(vb_cp, k - 1)
                        for n in range(2):
                            for j in range(NC):
                                ins = pe.transpose(ps[:, B + n, j * P:(j + 1) * P], (xn, hn)[n][:, k, j, :], W["ident"][:])
                            ins.then_inc(turned, 1)

                    def project_a(k):
                        B = 4 * (k % 2)
                        pe.wait_ge(turned_cp, 2 * k + 1)
                        if k >= 2:
                            pe.wait_ge(nmax, k - 1)
                        pe.matmul(ps[:, B + 2, :], W["wqA"][:], xnT[:, k], start=True, stop=True).then_inc(pa, 1)
                        pe.matmul(ps[:, B + 3, :], W["mk"][:], xnT[:, k], start=True, stop=True).then_inc(pa, 1)
                        for j in range(NC):
                            ins = pe.matmul(ps[:, B, j * P:(j + 1) * P], xnT[:, k, j * P:(j + 1) * P], W["mv"][:], start=True, stop=True)
                        ins.then_inc(pa, 1)

                    def project_b(k):
                        B = 4 * (k % 2)
                        waits = ((turned_cp, 2 * k + 2), (qa_cp, k + 1), (ka_cp, k + 1), (va_cp, k + 1))
                        for n, col in enumerate((0, 3, 1, 4)):
                            pe.wait_ge(*waits[n])
                            pe.matmul(ps[:, B + (n + 1) % 4, :], W["wB"][:, col * D:(col + 1) * D], hnT[:, k], start=True, stop=True).then_inc(pb, 1)
                        pe.wait_ge(roped_ps, 4 * k + 1)
                        for j in range(NC):
                            ins = pe.matmul(ps[:, B + 1, j * P:(j + 1) * P], hnT[:, k, j * P:(j + 1) * P], W["wB"][:, 2 * D:3 * D], start=True, stop=True)
                        ins.then_inc(pb, 1)

                    def norms(k):
                        B = 4 * (k % 2)
                        pe.wait_ge(squared, k + 1)
                        pe.wait_ge(roped_ps, 4 * k + 4)
                        pe.matmul(ps[0:H, B + 2, :], W["hsum"][:], sq[:, k % 2, 0], start=True, stop=True)
                        pe.matmul(ps[0:H, B + 3, :], W["hsum"][:], sq[:, k % 2, 1], start=True, stop=True).then_inc(normsq, 1)

                    for first in range(0, K, 2):
                        two = (first, first + 1)
                        if first == 0:
                            for k in two:
                                turn(k)
                        for stage in (project_a, project_b):
                            for k in two:
                                stage(k)
                        for k in two:
                            if k + 2 < K:
                                turn(k + 2)
                        for k in two:
                            norms(k)

                @block.scalar
                def _(act):
                    heads = lambda bank: ps[:, bank, :].rearrange("p (c h d) -> p c h d", c=NC, d=HD)
                    values = lambda k, a: v[:, k, a, :, 0:H * (HD + 1)].rearrange("p c (h e) -> p c h e", e=HD + 1)[:, :, :, 0:HD]

                    def take_rows(k):
                        for n in range(2):
                            act.wait_ge(turned, 2 * k + n + 1)
                            act.copy((xnT, hnT)[n][:, k], ps[:, 4 * (k % 2) + n, :]).then_inc(turned_cp, 1)

                    def take_a(k):
                        B = 4 * (k % 2)
                        act.wait_ge(pa, 3 * k + 1)
                        act.mul(qk[:, k, 0], ps[:, B + 2, :], SCALE_A).then_inc(qa_cp, 1)
                        act.wait_ge(pa, 3 * k + 3)
                        for j in range(NC):
                            ins = act.copy(values(k, 0)[:, j], heads(B)[:, j])
                        ins.then_inc(va_cp, 1)

                    def first_parts(k):
                        act.wait_ge(qa_cp, k + 1)
                        act.copy(parts[:, k, 0, 0], qk[:, k, 0]).then_inc(part1, 1)
                        act.wait_ge(ka_cp, k + 1)
                        act.copy(parts[:, k, 1, 0], qk[:, k, 1]).then_inc(part1, 1)
                        act.wait_ge(pb, 5 * k + 5)
                        for j in range(NC):
                            ins = act.copy(values(k, 1)[:, j], heads(4 * (k % 2) + 1)[:, j])
                        ins.then_inc(vb_cp, 1)
                        for t in range(2):
                            act.wait_ge(roped, 2 * k + t + 1)
                            act.copy(parts[:, k, 2 + t, 0], qk[:, k, 2 + t]).then_inc(part1, 1)

                    for first in range(0, K, 2):
                        two = (first, first + 1)
                        if first == 0:
                            for k in two:
                                take_rows(k)
                        for k in two:
                            take_a(k)
                        for k in two:
                            first_parts(k)
                            if k + 2 < K:
                                take_rows(k + 2)

                @block.vector
                def _(dve):
                    step = [0]

                    def link(ins):
                        step[0] += 1
                        ins.then_inc(v_step, 1)
                        dve.wait_ge(v_step, step[0])

                    def normalize(k):
                        dve.wait_ge(factors, k // 2 + 1)
                        for j in range(NC):
                            dve.tensor_scalar(xn[:, k, j], x[:, k, j], mv[:, k, j, 0:1], sc[:, k, 1, j:j + 1], ALU.subtract, ALU.mult)
                        for j in range(NC):
                            ins = dve.tensor_scalar(hn[:, k, j], x[:, k, j], mv[:, k, j, 0:1], sc[:, k, 4, j:j + 1], ALU.subtract, ALU.mult)
                        ins.then_inc(normed, 1)

                    def rope_parts(k):
                        if k >= 2:
                            dve.wait_ge(roped, 2 * k - 2)
                        for n in range(4):
                            dve.wait_ge(pb, 5 * k + n + 1)
                            dve.tensor_tensor(r[:, k % 2, n], ps[:, 4 * (k % 2) + (n + 1) % 4, :], rope[:, n], ALU.mult).then_inc(roped_ps, 1)

                    def other_parts(k):
                        for t in range(4):
                            dve.wait_ge(rest1, 4 * k + t + 1)
                            dve.tensor_copy(parts[:, k, t, 1], res[:, k % 2, t]).then_inc(part2, 1)
                            dve.wait_ge(part2, 4 * k + t + 1)
                            dve.tensor_tensor(parts[:, k, t, 2], res[:, k % 2, t], parts[:, k, t, 1], ALU.subtract).then_inc(part3, 1)

                    for n in range(K // 2):
                        dve.wait_ge(x_in[n], 32)
                        for k in (2 * n, 2 * n + 1):
                            for j in range(NC):
                                ins = dve.bn_stats(st[:, k, j], x[:, k, j, :])
                        link(ins)
                        for k in (2 * n, 2 * n + 1):
                            for j in range(NC):
                                ins = dve.bn_aggr(mv[:, k, j], st[:, k, j])
                        ins.then_inc(stats, 1)
                    for k in range(2):
                        normalize(k)
                    for first in range(0, K, 2):
                        two = (first, first + 1)
                        for k in two:
                            dve.wait_ge(pa, 3 * k + 2)
                            dve.tensor_copy(qk[:, k, 1], ps[:, 4 * (k % 2) + 3, :]).then_inc(ka_cp, 1)
                        for k in two:
                            if k + 2 < K:
                                normalize(k + 2)
                        for k in two:
                            rope_parts(k)
                        for k in two:
                            other_parts(k)
                        for k in two:
                            dve.wait_ge(normsq, k + 1)
                            for t in range(2):
                                ins = dve.tensor_reduce(W["nmax"][:, bass.ds(i * (2 * K) + 2 * k + t, 1)], ps[0:H, 4 * (k % 2) + 2 + t, :], AX.X, ALU.max)
                            ins.then_inc(nmax, 1)
                    dve.wait_ge(nmax, K)


def attend(nc, c, W, nb):
    with ExitStack() as ctx:
        sb = lambda n, s, d=F32: ctx.enter_context(nc.sbuf_tensor("at_" + n, s, d))
        sems = []

        def sem(n):
            sems.append(ctx.enter_context(nc.semaphore("at_" + n)))
            return sems[-1]

        KB = 2
        aq, ak = sb("aq", [ROWS, 2, 4, S], BF16), sb("ak", [ROWS, 2, 4, S], BF16)
        B_GROUPS = 6
        bq, bk = sb("bq", [ROWS + 3, 4 * B_GROUPS, S], BF16), sb("bk", [ROWS + 3, 4 * B_GROUPS, S], BF16)
        b_slot = lambda bb, h: (4 * bb + h // 4) % B_GROUPS * 4 + h % 4
        v = sb("v", [P, KB, 2, NC, VW])
        RING, B_WIDE = {"A": 8, "T": 6}, S * (NC + 1) // 2
        pT = {"A": sb("pA", [P, RING["A"], NC * S]), "T": sb("pB", [P, RING["T"], B_WIDE])}
        junk = sb("junk", [P, B_WIDE])
        mx = sb("mx", [P, KB, 4 * H])
        neg, res = sb("neg", [16, 2, P]), sb("res", [16, 2, P])
        mrow = sb("mrow", [16, 2, 3, P], BF16)
        oT = sb("oT", [P, 2, S])
        rr = sb("rr", [P, 2, 16])
        on = sb("on", [P, KB, 2, NC, D])
        ps = ctx.enter_context(nc.psum_tensor("at_ps", [P, 8, 512], F32))
        PV, JOB = 6, 7
        a_in = [sem(f"a_in{n}") for n in range(2)]
        b_in = [[sem(f"b_in{bb}{g}") for g in range(4)] for bb in range(KB)]
        v_in, filled, read_v, read_a, exped = (sem(n) for n in "v_in filled read_v read_a exped".split())
        pv, ot_cp, job, job_read, m_ready = (sem(n) for n in "pv ot_cp job job_read m_ready".split())
        m_in = [sem(f"m_in{n}") for n in range(4 * KB)]
        stored, v_step, p_step = (sem(n) for n in "stored v_step p_step".split())

        events = []
        for h in range(H):
            events += [("M", 0, h)] + ([("A", 0, h // 2)] if h % 2 else [])
        for h in range(H):
            events += [("T", 0, h), ("M", 1, h)] + ([("A", 0, H // 2 + h // 2)] if h % 2 else [])
        for h in range(H):
            events += [("T", 1, h), ("A", 1, h)]
        index = {e: n for n, e in enumerate(events)}
        kinds = {k: [e for e in events if e[0] == k] for k in "AMT"}
        seq_of = {e: n for es in kinds.values() for n, e in enumerate(es)}
        tiles_v = lambda n: 2 * sum(e[0] != "T" for e in events[:n])
        tiles_a = lambda n: 2 * sum(e[0] == "T" for e in events[:n])
        tile_ps = lambda t: ps[:, 2 * (t % 3):2 * (t % 3) + 2, :]
        B_AT = {0: 0, 1: 512, 3: 896, 2: 1024}
        DELAY = 2
        plan = {n: [] for n in range(len(events) + 20)}
        groups = [e for e in events if e[0] != "M" and e[2] % 4 == 3]
        gseq = {(e[0], seq_of[e] // 4): G for G, e in enumerate(groups)}
        wishes = [(index[e] + 2, ("MT", e[1], e[2] // 4)) for e in events if e[0] == "M" and e[2] % 4 == 3]
        pv_at = []
        for G, e in enumerate(groups):
            first = max(index[e] + (DELAY + 2 if e[0] == "A" else 2), pv_at[-1] + 2 if G else 0)
            for n, chunks in enumerate(((0,), (1,), (2, 3))):
                plan[first + n].append(("PV", G, e, chunks))
            pv_at.append(first + 2)
            wishes.append((pv_at[G] + 2, ("OT", G, e)))
        jobs, at = [], -3
        for n, what in sorted(wishes, key=lambda w: w[0]):
            at = max(n, at + 4)
            plan[at].append(what)
            jobs.append(what)
        jseq = {j: n for n, j in enumerate(jobs)}
        end = at + 3

        def slot_of(e):
            return pT[e[0]][:, seq_of[e] % RING[e[0]]]

        def free_slot(eng, e):
            if seq_of[e] >= RING[e[0]]:
                G = gseq[e[0], (seq_of[e] - RING[e[0]]) // 4]
                assert pv_at[G] < index[e]
                eng.wait_ge(pv, G + 1)

        LAST = end

        with nc.Block() as block:
            @block.vector
            def _(dve):
                dve.memset(bk[64:ROWS + 3], 1.0)

        with nc.Fori(0, nb // KB) as i:
            clear(nc, sems)
            with nc.Block() as block:

                @block.sync
                def _(sp):
                    def operand(dst, bb, t, rot, h0, nh, sem_):
                        src = c["parts_d"][bass.ds((i * KB + bb) * 4 + t, 1)][:, rot:rot + 3]
                        src = src.rearrange("o s (d h) f -> (o s d) h f", h=H)[:, h0:h0 + nh]
                        sp.dma_start(dst, src).then_inc(sem_, 16)

                    def load_a(n):
                        bb, g = divmod(n, 4)
                        if n >= 2:
                            e = ("A", (n - 2) // 4, 4 * ((n - 2) % 4) + 3)
                            sp.wait_ge(filled, 2 * index[e] + 2)
                        for a in range(3):
                            rows = slice(24 * a, 24 * a + 24)
                            operand(aq[rows, n % 2], bb, 0, a, 4 * g, 4, a_in[n % 2])
                            operand(ak[rows, n % 2], bb, 1, 0, 4 * g, 4, a_in[n % 2])

                    def load_b(n):
                        bb, g = divmod(n, 4)
                        if n >= B_GROUPS:
                            e = ("T", (n - B_GROUPS) // 4, 4 * ((n - B_GROUPS) % 4) + 3)
                            sp.wait_ge(filled, 2 * index[e] + 2)
                        for a in range(3):
                            rows = slice(24 * a, 24 * a + 24)
                            at_ = b_slot(bb, 4 * g)
                            operand(bq[rows, at_:at_ + 4], bb, 2, a, 4 * g, 4, b_in[bb][g])
                            operand(bk[rows, at_:at_ + 4], bb, 3, 0, 4 * g, 4, b_in[bb][g])

                    def load_m(n):
                        bb, g = divmod(n, 4)
                        sp.wait_ge(m_ready, n + 1)
                        for p in range(3):
                            at_ = b_slot(bb, 4 * g)
                            sp.dma_start(bq[ROWS + p:ROWS + p + 1, at_:at_ + 4], mrow[:, n % 2, p, :]).then_inc(m_in[n], 16)

                    load_b(0)
                    load_a(0)
                    for n in range(1, 4):
                        load_b(n)
                    load_a(1)
                    for a in range(2 * KB):
                        sp.dma_start(v[:, a // 2, a % 2].rearrange("p c f -> p (c f)"),
                                     c["v_d"][bass.ds(i * (2 * KB) + a, 1)].rearrange("o p f -> p (o f)")).then_inc(v_in, 16)
                    for n in range(4, B_GROUPS):
                        load_b(n)
                    steps = [(index["M", n // 4, 4 * (n % 4) + 3], load_m, n) for n in range(4 * KB)]
                    steps += [(index["A", (n - 2) // 4, 4 * ((n - 2) % 4) + 3], load_a, n) for n in range(2, 4 * KB)]
                    steps += [(index["T", (n - B_GROUPS) // 4, 4 * ((n - B_GROUPS) % 4) + 3], load_b, n) for n in range(B_GROUPS, 4 * KB)]
                    for _, load, n in sorted(steps, key=lambda w: w[0]):
                        load(n)
                    for bb in range(KB):
                        for a in range(2):
                            last = max(n for n, j in enumerate(jobs) if j[0] == "OT" and j[2][:2] == ("AT"[a], bb))
                            sp.wait_ge(job_read, last + 1)
                            sp.dma_start(c["on_d"][bass.ds((i * KB + bb) * 2 + a, 1)].rearrange("o p f -> p (o f)"),
                                         on[:, bb, a].rearrange("p c f -> p (c f)")).then_inc(stored, 16)
                    sp.wait_ge(stored, 16 * 2 * KB)

                @block.gpsimd
                def _(pool):
                    step = [0]

                    def link(ins):
                        step[0] += 1
                        ins.then_inc(p_step, 1)
                        pool.wait_ge(p_step, step[0])

                    for n in range(4 * KB):
                        b = n % 2
                        pool.wait_ge(job_read, jseq["MT", n // 4, n % 4] + 1)
                        if n >= 2:
                            pool.wait_ge(m_in[n - 2], 48)
                        link(pool.tensor_copy(mrow[:, b, 0], neg[:, b]))
                        link(pool.tensor_tensor(res[:, b], neg[:, b], mrow[:, b, 0], ALU.subtract))
                        link(pool.tensor_copy(mrow[:, b, 1], res[:, b]))
                        pool.tensor_tensor(mrow[:, b, 2], res[:, b], mrow[:, b, 1], ALU.subtract).then_inc(m_ready, 1)

                @block.tensor
                def _(pe):
                    for n in range(LAST):
                        if n < len(events):
                            kind, bb, h = events[n]
                            g = h // 4
                            if kind == "A" and h % 4 == 0:
                                m = 4 * bb + g
                                pe.wait_ge(a_in[m % 2], 96 * (m // 2 + 1))
                            if kind == "M" and h % 4 == 0:
                                pe.wait_ge(b_in[bb][g], 96)
                            if kind == "T" and h % 4 == 0:
                                pe.wait_ge(m_in[4 * bb + g], 48)
                            for half in range(2):
                                t = 2 * n + half
                                if t >= 3:
                                    n3, w3 = divmod(t - 3, 2)
                                    if events[n3][0] == "T":
                                        pe.wait_ge(read_a, tiles_a(n3) + w3 + 1)
                                    else:
                                        pe.wait_ge(read_v, tiles_v(n3) + w3 + 1)
                                dst = tile_ps(t)
                                if kind == "A":
                                    slot = (4 * bb + g) % 2
                                    for w in range(2):
                                        j = 2 * half + w
                                        ins = pe.matmul(dst[:, w], ak[:, slot, h % 4, j * P:(j + 1) * P], aq[:, slot, h % 4], start=True, stop=True)
                                elif kind == "M":
                                    for w in range(2):
                                        j = 2 * half + w
                                        wide = (j + 1) * P
                                        ins = pe.matmul(dst[:, w, 0:wide], bq[0:ROWS, b_slot(bb, h), j * P:(j + 1) * P], bk[0:ROWS, b_slot(bb, h), 0:wide],
                                                        start=True, stop=True)
                                else:
                                    for j in ((0, 1, 3), (2,))[half]:
                                        bank, col = divmod(B_AT[j] - 1024 * half, 512)
                                        pe.matmul(dst[:, bank, col:col + S - j * P], bk[:, b_slot(bb, h), j * P:(j + 1) * P], bq[:, b_slot(bb, h), j * P:S],
                                                  start=True, stop=False)
                                        ins = pe.matmul(dst[:, bank, col:col + P], W["ident_bf"][:], W["cmaskT"][:], start=False, stop=True)
                                ins.then_inc(filled, 1)
                        for what in plan[n]:
                            if what[0] == "PV":
                                _, G, (kind, bb, h), chunks = what
                                a = 0 if kind == "A" else 1
                                if G == 0:
                                    pe.wait_ge(v_in, 16 * 2 * KB)
                                if kind == "A":
                                    pe.wait_ge(exped, seq_of[kind, bb, h] + 1)
                                else:
                                    pe.wait_ge(read_a, tiles_a(index[kind, bb, h] + 1))
                                if G:
                                    pe.wait_ge(ot_cp, G)
                                for j in chunks:
                                    q0 = 0 if a == 0 else j * P
                                    at_ = j * S if a == 0 else B_AT[j]
                                    for s in range(4):
                                        hh = h - 3 + s
                                        probs = slot_of((kind, bb, hh))
                                        ins = pe.matmul(ps[32 * s:32 * s + 32, PV, q0:S], v[:, bb, a, j, hh * (HD + 1):hh * (HD + 1) + 32],
                                                        probs[:, at_:at_ + S - q0], start=(j == 0), stop=(j == NC - 1))
                                if chunks[-1] == NC - 1:
                                    ins.then_inc(pv, 1)
                            else:
                                m = jseq[what]
                                if m:
                                    pe.wait_ge(job_read, m)
                                if what[0] == "OT":
                                    G = what[1]
                                    pe.wait_ge(ot_cp, G + 1)
                                    for j in range(NC):
                                        ins = pe.transpose(ps[:, JOB, j * P:(j + 1) * P], oT[:, G % 2, j * P:(j + 1) * P], W["ident"][:])
                                else:
                                    _, bb, g = what
                                    pe.wait_ge(read_v, tiles_v(index["M", bb, 4 * g + 3] + 1))
                                    ins = pe.transpose(ps[0:16, JOB, 0:P], mx[:, bb, 16 * g:16 * g + 16], W["ident"][:])
                                ins.then_inc(job, 1)

                @block.scalar
                def _(act):
                    for n in range(LAST):
                        if 1 <= n <= len(events) and events[n - 1][0] == "T":
                            e = events[n - 1]
                            slot = slot_of(e)
                            free_slot(act, e)
                            for half in range(2):
                                t = 2 * (n - 1) + half
                                act.wait_ge(filled, t + 1)
                                if half == 0:
                                    act.activation(slot[:, 0:1024], tile_ps(t).rearrange("p b f -> p (b f)"), ACT.Exp).then_inc(read_a, 1)
                                else:
                                    act.activation(slot[:, 1024:1280], tile_ps(t)[:, 0, 0:256], ACT.Exp).then_inc(read_a, 1)
                        if DELAY <= n < len(events) + DELAY and events[n - DELAY][0] == "A":
                            slot = slot_of(events[n - DELAY])
                            act.wait_ge(read_v, tiles_v(n - DELAY + 1))
                            act.activation(slot, slot, ACT.Exp).then_inc(exped, 1)
                        for what in (plan[n - 1] if n else []):
                            if what[0] == "PV" and what[3][-1] == NC - 1:
                                G = what[1]
                                act.wait_ge(pv, G + 1)
                                if G >= 2:
                                    act.wait_ge(job, jseq[next(j for j in jobs if j[0] == "OT" and j[1] == G - 2)] + 1)
                                act.copy(oT[:, G % 2], ps[:, PV, :]).then_inc(ot_cp, 1)

                @block.vector
                def _(dve):
                    step = [0]

                    def link(ins):
                        step[0] += 1
                        ins.then_inc(v_step, 1)
                        dve.wait_ge(v_step, step[0])

                    for n in range(LAST):
                        if n < len(events) and events[n][0] == "A":
                            free_slot(dve, events[n])
                            for half in range(2):
                                t = 2 * n + half
                                dve.wait_ge(filled, t + 1)
                                dve.tensor_tensor(slot_of(events[n])[:, 1024 * half:1024 * half + 1024], tile_ps(t).rearrange("p b f -> p (b f)"),
                                                  W["decay"][:, 2 * half:2 * half + 2].rearrange("p b f -> p (b f)"), ALU.mult).then_inc(read_v, 1)
                        elif n < len(events) and events[n][0] == "M":
                            _, bb, h = events[n]
                            if seq_of[events[n]]:
                                dve.wait_ge(read_v, tiles_v(index[kinds["M"][seq_of[events[n]] - 1]] + 1))
                            for half in range(2):
                                t = 2 * n + half
                                dve.wait_ge(filled, t + 1)
                                for w in range(2):
                                    j = 2 * half + w
                                    wide = (j + 1) * P
                                    ins = dve.tensor_tensor_reduce(junk[:, P * j * (j + 1) // 2:P * (j + 1) * (j + 2) // 2], tile_ps(t)[:, w, 0:wide], W["cmask"][:, S - wide:S], 1.0, -3e38,
                                                                   ALU.add, ALU.max, mx[:, bb, 4 * h + j:4 * h + j + 1])
                                ins.then_inc(read_v, 1)
                        for what in (plan[n - 2] if n >= 2 else []):
                            if what[0] == "PV":
                                continue
                            m = jseq[what]
                            dve.wait_ge(job, m + 1)
                            if what[0] == "MT":
                                q = 4 * what[1] + what[2]
                                if q >= 2:
                                    dve.wait_ge(m_ready, q - 1)
                                dve.tensor_scalar(neg[:, q % 2], ps[0:16, JOB, 0:P], -1.0, None, ALU.mult).then_inc(job_read, 1)
                            else:
                                _, G, (kind, bb, h) = what
                                a, g = (0 if kind == "A" else 1), h // 4
                                src = ps[:, JOB, :].rearrange("p (c s d) -> p c s d", c=NC, s=4)
                                rcp = rr[:, G % 2].rearrange("p (c s) -> p c s", s=4)
                                link(dve.reciprocal(rcp, src[:, :, :, HD]))
                                dst = on[:, bb, a, :, 32 * g:32 * g + 32].rearrange("p c (s d) -> p c s d", d=HD)
                                dve.tensor_tensor(dst, src[:, :, :, 0:HD], bc(rcp, HD), ALU.mult).then_inc(job_read, 1)


def tail(nc, c, W, nb, K=4):
    with ExitStack() as ctx:
        sb = lambda n, s, d=F32: ctx.enter_context(nc.sbuf_tensor("tl_" + n, s, d))
        sems = []

        def sem(n):
            sems.append(ctx.enter_context(nc.semaphore("tl_" + n)))
            return sems[-1]

        x, xn = sb("x", [P, K, NC, D]), sb("xn", [P, K, NC, D])
        on, onT = sb("on", [P, K, 2, NC, D]), sb("onT", [P, K, 2, S])
        hs, x1, xf, xfT = sb("hs", [P, K, NC, D]), sb("x1", [P, K, NC, D]), sb("xf", [P, K, NC, D]), sb("xfT", [P, K, S])
        st, mv, sc = sb("st", [P, K, NC, 6]), sb("mv", [P, K, NC, 2]), sb("sc", [P, K, 5, NC])
        lg, ex, pr = sb("lg", [P, K, NC, E]), sb("ex", [P, K, NC, E]), sb("pr", [P, K, NC, E])
        ps = ctx.enter_context(nc.psum_tensor("tl_ps", [P, 8, 512], F32))
        loaded = [sem(f"loaded{k}") for k in range(K)]
        on_t, on_cp, outp, h_sum, x1d, stats, factors, xfd, xft, xfc = (
            sem(n) for n in "on_t on_cp outp h_sum x1d stats factors xfd xft xfc".split())
        hdone, logit, lsub, lexp, probd, stored, v_step, p_step = (sem(n) for n in "hdone logit lsub lexp probd stored v_step p_step".split())
        flat = lambda ap: ap.rearrange("p c d -> p (c d)")

        with nc.Fori(0, nb // K) as i:
            clear(nc, sems)
            with nc.Block() as block:

                @block.sync
                def _(sp):
                    seq = lambda t, k: t[bass.ds(i * K + k, 1)].rearrange("o (c p) d -> p (o c) d", p=P)
                    for k in range(K):
                        for a in range(2):
                            sp.dma_start(flat(on[:, k, a]), c["on_d"][bass.ds((i * K + k) * 2 + a, 1)].rearrange("o p f -> p (o f)")).then_inc(loaded[k], 16)
                        sp.dma_start(x[:, k], seq(c["x"], k)).then_inc(loaded[k], 16)
                        sp.dma_start(xn[:, k], seq(c["xn_d"], k)).then_inc(loaded[k], 16)
                    for k in range(K):
                        sp.wait_ge(x1d, k + 1)
                        sp.dma_start(seq(c["x1_d"], k), x1[:, k]).then_inc(stored, 16)
                        sp.wait_ge(hdone, k + 1)
                        sp.dma_start(seq(c["h_d"], k), hs[:, k]).then_inc(stored, 16)
                    for k in range(K):
                        sp.wait_ge(xfd, k + 1)
                        sp.dma_start(seq(c["xf_d"], k), xf[:, k]).then_inc(stored, 16)
                    for k in range(K):
                        sp.wait_ge(probd, k + 1)
                        sp.dma_start(c["pr_d"][:, bass.ds(i * K + k, 1)].rearrange("p o c e -> p (o c) e"), pr[:, k]).then_inc(stored, 16)
                    sp.wait_ge(stored, 64 * K)

                @block.gpsimd
                def _(pool):
                    for k in range(K):
                        pool.wait_ge(h_sum, k + 1)
                        pool.wait_ge(x1d, k + 1)
                        pool.tensor_tensor(hs[:, k], hs[:, k], x1[:, k], ALU.add).then_inc(hdone, 1)
                        pool.wait_ge(stats, k + 1)
                        pool.tensor_scalar(sc[:, k, 1], sc[:, k, 0], 1e-6, None, ALU.add).then_inc(p_step, 1)
                        pool.wait_ge(p_step, k + 1)
                        pool.tensor_tensor(sc[:, k, 2], sc[:, k, 1], W["mhalf"][:, 0:NC], ALU.pow).then_inc(factors, 1)

                @block.tensor
                def _(pe):
                    for k in range(K):
                        pe.wait_ge(loaded[k], 64)
                        for a in range(2):
                            for j in range(NC):
                                ins = pe.transpose(ps[:, 2 * k + a, j * P:(j + 1) * P], on[:, k, a, j, :], W["ident"][:])
                            ins.then_inc(on_t, 1)
                    for k in range(K):
                        for a in range(2):
                            pe.wait_ge(on_cp, 2 * k + a + 1)
                            for j in range(NC):
                                ins = pe.matmul(ps[:, 2 * k + a, j * P:(j + 1) * P], onT[:, k, a, j * P:(j + 1) * P], W[("woA", "woB")[a]][:],
                                                start=True, stop=True)
                            ins.then_inc(outp, 1)
                    for k in range(K):
                        pe.wait_ge(xfd, k + 1)
                        for j in range(NC):
                            ins = pe.transpose(ps[:, 2 * k, j * P:(j + 1) * P], xf[:, k, j, :], W["ident"][:])
                        ins.then_inc(xft, 1)
                    for k in range(K):
                        pe.wait_ge(xfc, k + 1)
                        for j in range(NC):
                            ins = pe.matmul(ps[:, 2 * k + 1, j * E:(j + 1) * E], xfT[:, k, j * P:(j + 1) * P], W["wr"][:], start=True, stop=True)
                        ins.then_inc(logit, 1)

                @block.scalar
                def _(act):
                    for k in range(K):
                        for a in range(2):
                            act.wait_ge(on_t, 2 * k + a + 1)
                            act.copy(onT[:, k, a], ps[:, 2 * k + a, :]).then_inc(on_cp, 1)
                    for k in range(K):
                        act.wait_ge(xft, k + 1)
                        act.copy(xfT[:, k], ps[:, 2 * k, :]).then_inc(xfc, 1)
                    for k in range(K):
                        act.wait_ge(lsub, k + 1)
                        act.activation(ex[:, k], lg[:, k], ACT.Exp).then_inc(lexp, 1)

                @block.vector
                def _(dve):
                    step = [0]

                    def link(ins):
                        step[0] += 1
                        ins.then_inc(v_step, 1)
                        dve.wait_ge(v_step, step[0])

                    for k in range(K):
                        dve.wait_ge(outp, 2 * k + 1)
                        dve.tensor_tensor(flat(hs[:, k]), flat(x[:, k]), ps[:, 2 * k, :], ALU.add).then_inc(h_sum, 1)
                        dve.wait_ge(outp, 2 * k + 2)
                        dve.tensor_tensor(flat(x1[:, k]), flat(xn[:, k]), ps[:, 2 * k + 1, :], ALU.add).then_inc(x1d, 1)
                        dve.wait_ge(x1d, k + 1)
                        for j in range(NC):
                            ins = dve.bn_stats(st[:, k, j], x1[:, k, j, :])
                        link(ins)
                        for j in range(NC):
                            ins = dve.bn_aggr(mv[:, k, j], st[:, k, j])
                        link(ins)
                        link(dve.tensor_tensor(sc[:, k, 3], mv[:, k, :, 0], mv[:, k, :, 0], ALU.mult))
                        dve.tensor_tensor(sc[:, k, 0], sc[:, k, 3], mv[:, k, :, 1], ALU.add).then_inc(stats, 1)
                    for k in range(K):
                        dve.wait_ge(factors, k + 1)
                        for j in range(NC):
                            ins = dve.scalar_tensor_tensor(xf[:, k, j], x1[:, k, j], sc[:, k, 2, j:j + 1], W["g2b"][:], ALU.mult, ALU.mult)
                        ins.then_inc(xfd, 1)
                    logits = lambda k: ps[:, 2 * k + 1, 0:NC * E].rearrange("p (c e) -> p c e", e=E)
                    for k in range(K):
                        dve.wait_ge(logit, k + 1)
                        link(dve.tensor_reduce(sc[:, k, 4], logits(k), AX.X, ALU.max))
                        dve.tensor_tensor(lg[:, k], logits(k), bc(sc[:, k, 4], E), ALU.subtract).then_inc(lsub, 1)
                    for k in range(K):
                        dve.wait_ge(lexp, k + 1)
                        link(dve.tensor_reduce(sc[:, k, 3], ex[:, k], AX.X, ALU.add))
                        link(dve.reciprocal(sc[:, k, 4], sc[:, k, 3]))
                        dve.tensor_tensor(pr[:, k], ex[:, k], bc(sc[:, k, 4], E), ALU.mult).then_inc(probd, 1)


def bound_flag(nc, W, nb):
    with ExitStack() as ctx:
        sb = lambda n, s, d=F32: ctx.enter_context(nc.sbuf_tensor("bf_" + n, s, d))
        pb, m, row = sb("pb", [H, nb]), sb("m", [H, 2]), sb("row", [1, 1])
        ps = ctx.enter_context(nc.psum_tensor("bf_ps", [P, 512], F32))
        step, turned = ctx.enter_context(nc.semaphore("bf_step")), ctx.enter_context(nc.semaphore("bf_turned"))
        with nc.Block() as block:

            @block.vector
            def _(dve):
                pairs = W["nmax"][:, 0:2 * nb].rearrange("p (b t) -> p b t", t=2)
                dve.tensor_tensor(pb[:], pairs[:, :, 0], pairs[:, :, 1], ALU.mult).then_inc(step, 1)
                dve.wait_ge(step, 1)
                dve.tensor_reduce(m[:, 0:1], pb[:], AX.X, ALU.max).then_inc(step, 1)
                dve.wait_ge(turned, 1)
                dve.tensor_reduce(row[:], ps[0:1, 0:H], AX.X, ALU.max).then_inc(step, 1)
                dve.wait_ge(step, 3)
                dve.tensor_scalar(row[:], row[:], LIMIT * LIMIT, None, ALU.is_lt).then_inc(step, 1)
                dve.wait_ge(step, 4)
                dve.tensor_scalar(W["flag"][:], row[:], -1.0, 1.0, ALU.mult, ALU.add).then_inc(step, 1)
                dve.wait_ge(step, 5)

            @block.tensor
            def _(pe):
                pe.wait_ge(step, 2)
                pe.transpose(ps[0:1, 0:H], m[:, 0:1], W["ident"][0:H, 0:H]).then_inc(turned, 1)


def attend_any(nc, c, W, nb):
    with ExitStack() as ctx:
        sb = lambda n, s, d=F32: ctx.enter_context(nc.sbuf_tensor("an_" + n, s, d))
        sems = []

        def sem(n):
            sems.append(ctx.enter_context(nc.semaphore("an_" + n)))
            return sems[-1]

        x, xn, x1, hs = sb("x", [P, NC, D]), sb("xn", [P, NC, D]), sb("x1", [P, NC, D]), sb("hs", [P, NC, D])
        xnT = sb("xnT", [P, S])
        q, k, v = sb("q", [P, S]), sb("k", [P, S]), sb("v", [P, NC, H, 32])
        qm = sb("qm", [P, 4, S])
        clip, tt, prob = sb("clip", [P, 2, S]), sb("tt", [P, 2, S]), sb("prob", [P, 3, S])
        pT = sb("pT", [P, 2, 4, NC, S])
        mx, nm, rs = sb("mx", [P, UNITS]), sb("nm", [P, UNITS]), sb("rs", [P, UNITS])
        rr = sb("rr", [P, 16])
        oT = sb("oT", [P, S])
        on, onT = sb("on", [P, NC, D]), sb("onT", [P, S])
        ps = ctx.enter_context(nc.psum_tensor("an_ps", [P, 8, 512], F32))
        x_in, turned, turned_cp, proj, k_cp, qv_cp, masked = (sem(n) for n in "x_in turned turned_cp proj k_cp qv_cp masked".split())
        scored, clipped, reduced, maxed, exped = (sem(n) for n in "scored clipped reduced maxed exped".split())
        transposed, evacuated, pv, ot_cp, ot_t = (sem(n) for n in "transposed evacuated pv ot_cp ot_t".split())
        zeroed, inverted, weighed, on_t, on_cp, projo, based, added, stored = (
            sem(n) for n in "zeroed inverted weighed on_t on_cp projo based added stored".split())
        S0, TP0, OT, OTT, M0, M1 = 0, 2, 4, 5, 6, 7
        LAST = UNITS + 14

        def wait(eng, s, n):
            if n > 0:
                eng.wait_ge(s, n)

        with nc.Fori(0, nb) as i:
            clear(nc, sems)
            with nc.Block() as block:

                @block.sync
                def _(sp):
                    seq = lambda t: t[bass.ds(i, 1)].rearrange("o (c p) d -> p (o c) d", p=P)
                    for dst, src in ((xn, "xn_d"), (x, "x"), (x1, "x1_d")):
                        sp.dma_start(dst[:], seq(c[src])).then_inc(x_in, 16)
                    sp.wait_ge(added, 1)
                    sp.dma_start(seq(c["h_d"]), hs[:]).then_inc(stored, 16)
                    sp.wait_ge(stored, 16)

                @block.gpsimd
                def _(pool):
                    pool.wait_ge(x_in, 48)
                    pool.tensor_tensor(hs[:], x[:], x1[:], ALU.add).then_inc(based, 1)
                    pool.wait_ge(qv_cp, 1)
                    for n in range(H):
                        wait(pool, scored, NC * (n - 3))
                        pool.tensor_scalar(qm[:, n % 4], q[:], W["hsum"][:, n:n + 1], SCALE_A, ALU.mult, ALU.mult).then_inc(masked, 1)

                @block.tensor
                def _(pe):
                    pe.wait_ge(x_in, 48)
                    for j in range(NC):
                        ins = pe.transpose(ps[:, 0, j * P:(j + 1) * P], xn[:, j, :], W["ident"][:])
                    ins.then_inc(turned, 1)
                    pe.wait_ge(turned_cp, 1)
                    pe.matmul(ps[:, 2, :], W["wqA"][:], xnT[:], start=True, stop=True).then_inc(proj, 1)
                    pe.matmul(ps[:, 3, :], W["mk"][:], xnT[:], start=True, stop=True).then_inc(proj, 1)
                    for j in range(NC):
                        ins = pe.matmul(ps[:, 4, j * P:(j + 1) * P], xnT[:, j * P:(j + 1) * P], W["mv"][:], start=True, stop=True)
                    ins.then_inc(proj, 1)
                    pe.wait_ge(k_cp, 1)
                    pe.wait_ge(qv_cp, 2)
                    for t in range(LAST):
                        if t < UNITS:
                            n = t // NC
                            wait(pe, masked, n + 1)
                            wait(pe, clipped, t - 1)
                            pe.matmul(ps[:, S0 + t % 2, :], qm[:, n % 4, (t % NC) * P:(t % NC + 1) * P], k[:], start=True, stop=True).then_inc(scored, 1)
                        u = t - 2
                        if 0 <= u < UNITS:
                            wait(pe, exped, u + 1)
                            wait(pe, evacuated, u - 1)
                            for j in range(NC):
                                ins = pe.transpose(ps[:, TP0 + u % 2, j * P:(j + 1) * P], prob[:, u % 3, j * P:(j + 1) * P], W["ident"][:])
                            ins.then_inc(transposed, 1)
                        g, m = divmod(t - 20, 16)
                        if m == 0 and 0 <= g < NG:
                            wait(pe, evacuated, 16 * g + 16)
                            wait(pe, ot_cp, g)
                            for j in range(NC):
                                for s in range(4):
                                    ins = pe.matmul(ps[32 * s:32 * s + 32, OT, :], v[:, j, 4 * g + s, :], pT[:, g % 2, s, j],
                                                    start=(j == 0), stop=(j == NC - 1))
                            ins.then_inc(pv, 1)
                        g, m = divmod(t - 23, 16)
                        if m == 0 and 0 <= g < NG:
                            wait(pe, ot_cp, g + 1)
                            wait(pe, weighed, g)
                            for j in range(NC):
                                ins = pe.transpose(ps[:, OTT, j * P:(j + 1) * P], oT[:, j * P:(j + 1) * P], W["ident"][:])
                            ins.then_inc(ot_t, 1)
                    wait(pe, weighed, NG)
                    for j in range(NC):
                        ins = pe.transpose(ps[:, M0, j * P:(j + 1) * P], on[:, j, :], W["ident"][:])
                    ins.then_inc(on_t, 1)
                    wait(pe, on_cp, 1)
                    for j in range(NC):
                        ins = pe.matmul(ps[:, M1, j * P:(j + 1) * P], onT[:, j * P:(j + 1) * P], W["woA"][:], start=True, stop=True)
                    ins.then_inc(projo, 1)

                @block.scalar
                def _(act):
                    wait(act, turned, 1)
                    act.copy(xnT[:], ps[:, 0, :]).then_inc(turned_cp, 1)
                    wait(act, proj, 1)
                    act.copy(q[:], ps[:, 2, :]).then_inc(qv_cp, 1)
                    wait(act, proj, 3)
                    wait(act, zeroed, 1)
                    act.copy(v[:, :, :, 0:HD].rearrange("p c h d -> p (c h) d"),
                             ps[:, 4, :].rearrange("p (c h d) -> p (c h) d", c=NC, d=HD)).then_inc(qv_cp, 1)
                    for t in range(LAST):
                        if t < UNITS:
                            wait(act, maxed, t + 1)
                            wait(act, transposed, t - 2)
                            act.activation(prob[:, t % 3], tt[:, t % 2], ACT.Exp, bias=nm[:, t:t + 1], accum_out=rs[:, t:t + 1]).then_inc(exped, 1)
                        u = t - 3
                        if 0 <= u < UNITS:
                            wait(act, transposed, u + 1)
                            wait(act, pv, u // 16 - 1)
                            act.copy(pT[:, (u // 16) % 2, (u // NC) % 4, :, (u % NC) * P:(u % NC + 1) * P],
                                     ps[:, TP0 + u % 2, :].rearrange("p (j r) -> p j r", j=NC)).then_inc(evacuated, 1)
                        g, m = divmod(t - 21, 16)
                        if m == 0 and 0 <= g < NG:
                            wait(act, pv, g + 1)
                            wait(act, ot_t, g)
                            act.copy(oT[:], ps[:, OT, :]).then_inc(ot_cp, 1)
                    wait(act, on_t, 1)
                    act.copy(onT[:], ps[:, M0, :]).then_inc(on_cp, 1)

                @block.vector
                def _(dve):
                    dve.memset(v[:], 0.0).then_inc(zeroed, 1)
                    wait(dve, proj, 2)
                    dve.tensor_copy(k[:], ps[:, 3, :]).then_inc(k_cp, 1)
                    for t in range(UNITS + 14):
                        if t < UNITS:
                            wait(dve, scored, t + 1)
                            wait(dve, exped, t - 1)
                            dve.tensor_scalar(clip[:, t % 2], ps[:, S0 + t % 2, :], CLAMP, -CLAMP, ALU.min, ALU.max).then_inc(clipped, 1)
                            wait(dve, clipped, t + 1)
                            dve.tensor_tensor_reduce(tt[:, t % 2], clip[:, t % 2], W["decay"][:, t % NC], 1.0, -3e38,
                                                     ALU.mult, ALU.max, mx[:, t:t + 1]).then_inc(reduced, 1)
                            wait(dve, reduced, t + 1)
                            dve.tensor_scalar(nm[:, t:t + 1], mx[:, t:t + 1], -1.0, None, ALU.mult).then_inc(maxed, 1)
                        g, m = divmod(t - 25, 16)
                        if m == 0 and 0 <= g < NG:
                            wait(dve, exped, 16 * g + 16)
                            dve.reciprocal(rr[:], rs[:, 16 * g:16 * g + 16]).then_inc(inverted, 1)
                            wait(dve, inverted, g + 1)
                            wait(dve, ot_t, g + 1)
                            for j in range(NC):
                                ins = dve.tensor_tensor(
                                    on[:, j, 32 * g:32 * g + 32].rearrange("p (s d) -> p s d", d=HD),
                                    ps[:, OTT, j * P:(j + 1) * P].rearrange("p (s d) -> p s d", s=4)[:, :, 0:HD],
                                    bc(rr[:].rearrange("p (s c) -> p s c", c=NC)[:, :, j], HD),
                                    ALU.mult)
                            ins.then_inc(weighed, 1)
                    wait(dve, projo, 1)
                    wait(dve, based, 1)
                    flat = lambda t: t[:].rearrange("p c d -> p (c d)")
                    dve.tensor_tensor(flat(hs), flat(hs), ps[:, M1, :], ALU.add).then_inc(added, 1)


def route(nc, c, W, R):
    with ExitStack() as ctx:
        sb = lambda n, s, d=F32: ctx.enter_context(nc.sbuf_tensor("rt_" + n, s, d))
        sem = lambda n: ctx.enter_context(nc.semaphore(n))
        NE = NT * E
        prob = sb("prob", [P, NT, E])
        rank, eqs = sb("rank", [P, NT, E]), sb("eqs", [P, NT, E])
        cmp = sb("cmp", [P, NT, E, E])
        gate = sb("gate", [P, NT, E])
        gt = sb("gt", [P, E, NT])
        hit = sb("hit", [P, 3, E, NT])
        low = sb("low", [P, E, E])
        ones, before = sb("ones", [P, P]), sb("before", [P, P])
        restart = sb("restart", [P, NE])
        cnt, need = sb("cnt", [P, 3, E]), sb("need", [P, E])
        thr, cand, bits, add = sb("thr", [P, E], I32), sb("cand", [P, 3, E], I32), sb("bits", [P, 3, E], I32), sb("add", [P, E], I32)
        enough, taken, unit = sb("enough", [P, 3, E]), sb("taken", [P, E]), sb("unit", [P, E])
        above, equal, keep = sb("above", [P, E, NT]), sb("equal", [P, E, NT]), sb("keep", [P, E, NT])
        incl, pos = sb("incl", [P, NE]), sb("pos", [P, E, NT])
        slots = sb("slots", [P, E, CAP])
        onehot = sb("onehot", [P, 2, 2, E * CAP], BF16)
        ptid = sb("ptid", [P, NT, 2])
        pt = sb("pt", [P, 2, 2, 2], BF16)
        place = sb("place", [2, E * CAP])
        mix = sb("mix", [2, 2])
        ps = ctx.enter_context(nc.psum_tensor("rt_ps", [P, 8, 512], F32))
        s_in, step, counted, scanned = sem("rt_in"), sem("rt_step"), sem("rt_counted"), sem("rt_scanned")
        cnt_ready, bit_step, ranked = sem("rt_cnt_ready"), sem("rt_bit_step"), sem("rt_ranked")
        hot, placed, copied, turned, gated = sem("rt_hot"), sem("rt_placed"), sem("rt_copied"), sem("rt_turned"), sem("rt_gated")
        hot_prep = sem("rt_hot_prep")
        BITS = 30
        block = ctx.enter_context(nc.Block())
        loads = [(prob[:].rearrange("p t e -> p (t e)"), c["pr_d"].rearrange("p b c e -> p (b c e)")),
                 (low[:].rearrange("p a b -> p (a b)"), c["low"]), (before[:], c["before"]), (restart[:], c["restart"]),
                 (slots[:].rearrange("p a b -> p (a b)"), c["slots"]), (ptid[:].rearrange("p a b -> p (a b)"), c["ptid"]),
                 (mix[:], c["mix"])]
        flat = lambda ap: ap.rearrange("p a b -> p (a b)")
        ET = [P, E, NT]

        @block.sync
        def _(sp):
            for dst, src in loads:
                sp.dma_start(dst, src).then_inc(s_in, 16)
            sp.wait_ge(gated, 1)
            sp.dma_start(c["gate_d"].rearrange("(p t) e -> p (t e)", p=P), flat(gate[:])).then_inc(s_in, 16)
            sp.wait_ge(s_in, 16 * (len(loads) + 1))

        @block.vector
        def _(dve):
            n = [0]

            def link(ins):
                n[0] += 1
                ins.then_inc(step, 1)
                dve.wait_ge(step, n[0])

            dve.memset(ones[:], 1.0)
            dve.memset(ps[0:2, 3:6, :], 0.0).then_inc(placed, 2)
            dve.memset(thr[:], 0)
            for k in range(3):
                dve.memset(bits[:, k], (k + 1) << (BITS - 2))
            link(dve.memset(unit[:], float(1 << (BITS - 2))))
            dve.wait_ge(s_in, 16 * len(loads))
            other = prob[:].unsqueeze(2).broadcast_to([P, NT, E, E])
            mine = bc(prob[:], E)
            link(dve.tensor_tensor(cmp[:], other, mine, ALU.is_gt))
            link(dve.tensor_reduce(rank[:], cmp[:], AX.X, ALU.add))
            link(dve.tensor_tensor(cmp[:], other, mine, ALU.is_equal))
            link(dve.tensor_tensor(cmp[:], cmp[:], low[:].unsqueeze(1).broadcast_to([P, NT, E, E]), ALU.mult))
            link(dve.tensor_reduce(eqs[:], cmp[:], AX.X, ALU.add))
            link(dve.tensor_tensor(rank[:], rank[:], eqs[:], ALU.add))
            dve.scalar_tensor_tensor(gate[:], rank[:], float(TOPK), prob[:], ALU.is_lt, ALU.mult).then_inc(gated, 1)
            dve.wait_ge(gated, 1)
            link(dve.tensor_copy(gt[:], gate[:].rearrange("p t e -> p e t")))
            with dve.Fori(0, BITS // 2) as i:
                dve.tensor_tensor(cand[:], thr[:].unsqueeze(1).broadcast_to([P, 3, E]), bits[:], ALU.bitwise_or).then_inc(bit_step, 1)
                dve.wait_ge(bit_step, i * 6 + 1)
                dve.tensor_tensor(hit[:], gt[:].unsqueeze(1).broadcast_to([P, 3, E, NT]), bc(cand[:].bitcast(F32), NT), ALU.is_ge).then_inc(bit_step, 1)
                dve.tensor_scalar(bits[:], bits[:], 2, None, ALU.logical_shift_right)
                dve.wait_ge(bit_step, i * 6 + 2)
                dve.tensor_reduce(cnt[:], hit[:], AX.X, ALU.add).then_inc(cnt_ready, 1)
                dve.wait_ge(counted, i + 1)
                dve.scalar_tensor_tensor(enough[:], ps[:, 0, 0:3 * E].rearrange("p (k e) -> p k e", k=3), float(CAP),
                                         unit[:].unsqueeze(1).broadcast_to([P, 3, E]), ALU.is_ge, ALU.mult).then_inc(bit_step, 1)
                dve.wait_ge(bit_step, i * 6 + 3)
                dve.tensor_reduce(taken[:], enough[:].rearrange("p k e -> p e k"), AX.X, ALU.add).then_inc(bit_step, 1)
                dve.tensor_scalar(unit[:], unit[:], 0.25, None, ALU.mult)
                dve.wait_ge(bit_step, i * 6 + 4)
                dve.tensor_copy(add[:], taken[:]).then_inc(bit_step, 1)
                dve.wait_ge(bit_step, i * 6 + 5)
                dve.tensor_tensor(thr[:], thr[:], add[:], ALU.bitwise_or).then_inc(bit_step, 1)
                dve.wait_ge(bit_step, i * 6 + 6)
            cut = bc(thr[:].bitcast(F32), NT)
            dve.tensor_tensor(above[:], gt[:], cut, ALU.is_gt)
            link(dve.tensor_tensor(equal[:], gt[:], cut, ALU.is_equal))
            dve.tensor_reduce(cnt[:, 0], above[:], AX.X, ALU.add).then_inc(cnt_ready, 1)
            dve.wait_ge(counted, BITS // 2 + 1)
            link(dve.tensor_scalar(need[:], ps[:, 0, 0:E], -1.0, float(CAP), ALU.mult, ALU.add))

            def rank_before(k):
                dve.wait_ge(ranked, k)
                link(dve.tensor_tensor_scan(incl[:], restart[:], ps[:, 2, :], 0.0, ALU.mult, ALU.add))
                link(dve.tensor_tensor(incl[:], incl[:], ps[:, 2, :], ALU.subtract))
                link(dve.tensor_tensor(flat(pos[:]), incl[:], ps[:, 1, :], ALU.add))

            rank_before(1)
            link(dve.tensor_tensor(pos[:], pos[:], bc(need[:], NT), ALU.is_lt))
            link(dve.tensor_tensor(pos[:], pos[:], equal[:], ALU.mult))
            dve.tensor_tensor(keep[:], above[:], pos[:], ALU.add).then_inc(scanned, 1)
            rank_before(2)
            link(dve.scalar_tensor_tensor(pos[:], pos[:], 1.0, keep[:], ALU.add, ALU.mult))
            link(dve.tensor_scalar(pos[:], pos[:], -1.0, None, ALU.add))
            with dve.Fori(0, NT // 4) as i:
                for b in range(2):
                    dve.wait_ge(placed, i * 2 + b + 1)
                    chunks = bass.ds(i * 4 + 2 * b, 2)
                    dve.tensor_copy(pt[:, b], ptid[:, chunks])
                    dve.tensor_tensor(onehot[:, b].rearrange("p c (e s) -> p c e s", e=E), slots[:].unsqueeze(1).broadcast_to([P, 2, E, CAP]),
                                      bc(pos[:, :, chunks].rearrange("p e c -> p c e"), CAP), ALU.is_equal).then_inc(hot, 1)
            dve.wait_ge(placed, NT // 2 + 2)
            for b in range(3):
                w = min(512, E * CAP - 512 * b)
                ins = dve.tensor_copy(place[:, 512 * b:512 * b + w], ps[0:2, 3 + b, 0:w])
            ins.then_inc(copied, 1)
            dve.wait_ge(turned, 1)
            link(dve.tensor_copy(R["rows"][0:HALF], ps[0:HALF, 6, 0:64].rearrange("p (m k) -> p m k", k=2)[:, 0:2 * E, :]))

        @block.tensor
        def _(pe):
            pe.wait_ge(step, 1)
            with pe.Fori(0, BITS // 2 + 1) as i:
                pe.wait_ge(cnt_ready, i + 1)
                pe.matmul(ps[:, 0, 0:3 * E], ones[:], cnt[:].rearrange("p k e -> p (k e)"), start=True, stop=True).then_inc(counted, 1)
            for k, marked in enumerate((equal, keep)):
                pe.wait_ge(*((step, 10) if k == 0 else (scanned, 1)))
                pe.matmul(ps[:, 1, :], before[:], flat(marked[:]), start=True, stop=True)
                pe.matmul(ps[:, 2, :], ones[:], flat(marked[:]), start=True, stop=True).then_inc(ranked, 1)
            with pe.Fori(0, NT // 4) as i:
                for b in range(2):
                    pe.wait_ge(hot, i * 2 + b + 1)
                    for ch in range(2):
                        for m in range(3):
                            w = min(512, E * CAP - 512 * m)
                            ins = pe.matmul(ps[0:2, 3 + m, 0:w], pt[:, b, ch], onehot[:, b, ch, 512 * m:512 * m + w],
                                            start=False, stop=False, skip_group_check=True)
                    ins.then_inc(placed, 1)
            pe.wait_ge(copied, 1)
            for m in range(2 * E):
                ins = pe.matmul(ps[0:HALF, 6, 2 * m:2 * m + 2], place[:, HALF * m:HALF * (m + 1)], mix[:], start=True, stop=True)
            ins.then_inc(turned, 1)


def experts(nc, c, W, R):
    with ExitStack() as ctx:
        sb = lambda n, s, d=F32: ctx.enter_context(nc.sbuf_tensor("ex_" + n, s, d))
        sem = lambda n: ctx.enter_context(nc.semaphore(n))
        w1, w2 = sb("w1", [P, E, FF]), sb("w2", [P, E, 2, D])
        xe, ge = sb("xe", [P, 2 * E, D]), sb("ge", [P, 2 * E, E])
        xeT, hT = sb("xeT", [P, 2, CAP]), sb("hT", [P, 2, 2, CAP])
        ye = sb("ye", [P, 2 * E, D])
        ps = ctx.enter_context(nc.psum_tensor("ex_ps", [P, 8, 512], F32))
        s_in = sem("ex_in")
        fetched = [sem(f"ex_fetched{e}") for e in range(E)]
        turned, turned_cp, hidden, relued, out, scaled, summed = (sem("ex_turned"), sem("ex_turned_cp"), sem("ex_hidden"),
                                                                  sem("ex_relued"), sem("ex_out"), sem("ex_scaled"), sem("ex_summed"))
        rows = R["rows"]
        block = ctx.enter_context(nc.Block())

        @block.sync
        def _(sp):
            sp.dma_start(w1[:], c["w1"].rearrange("e d f -> d e f")).then_inc(s_in, 16)
            sp.dma_start(w2[:].rearrange("p e h d -> p (e h) d"), c["w2"].rearrange("e (h p) d -> p (e h) d", p=P)).then_inc(s_in, 16)

        @block.gpsimd
        def _(pool):
            for m in range(2 * E):
                pool.indirect_dma_start(xe[0:HALF, m, :], None, c["xf_d"].rearrange("b s d -> (b s) d"),
                                        bass.IndirectOffsetOnAxis(rows[0:HALF, m, 0:1], 0)).then_inc(fetched[m // 2], 16)
                pool.indirect_dma_start(ge[0:HALF, m, :], None, c["gate_d"],
                                        bass.IndirectOffsetOnAxis(rows[0:HALF, m, 1:2], 0)).then_inc(fetched[m // 2], 16)
            for m in range(2 * E):
                e = m // 2
                pool.wait_ge(scaled, e + 1)
                pool.wait_ge(summed, 32 * e)
                pool.indirect_dma_start(c["h_d"].rearrange("b s d -> (b s) d"),
                                        bass.IndirectOffsetOnAxis(rows[0:HALF, m, 0:1], 0), ye[0:HALF, m, :], None,
                                        compute_op=ALU.add).then_inc(summed, 16)
            pool.wait_ge(summed, 32 * E)

        @block.tensor
        def _(pe):
            for e in range(E):
                b = e % 2
                pe.wait_ge(fetched[e], 64)
                if e >= 2:
                    pe.wait_ge(turned_cp, e - 1)
                for k in range(2):
                    ins = pe.transpose(ps[:, b, k * HALF:(k + 1) * HALF], xe[0:HALF, 2 * e + k, :], W["ident"][0:HALF, 0:HALF])
                ins.then_inc(turned, 1)
                pe.wait_ge(turned_cp, e + 1)
                pe.wait_ge(s_in, 32)
                if e >= 2:
                    pe.wait_ge(relued, e - 1)
                for f in range(2):
                    ins = pe.matmul(ps[:, 2 + b, f * CAP:(f + 1) * CAP], w1[:, e, f * P:(f + 1) * P], xeT[:, b], start=True, stop=True)
                ins.then_inc(hidden, 1)
                pe.wait_ge(relued, e + 1)
                if e >= 2:
                    pe.wait_ge(scaled, e - 1)
                for k in range(2):
                    for f in range(2):
                        ins = pe.matmul(ps[0:HALF, 4 + b, k * D:(k + 1) * D], hT[:, b, f, k * HALF:(k + 1) * HALF], w2[:, e, f, :],
                                        start=(f == 0), stop=(f == 1))
                ins.then_inc(out, 1)

        @block.scalar
        def _(act):
            for e in range(E):
                b = e % 2
                act.wait_ge(turned, e + 1)
                act.copy(xeT[:, b], ps[:, b, 0:CAP]).then_inc(turned_cp, 1)
                act.wait_ge(hidden, e + 1)
                act.activation(hT[:, b].rearrange("p f s -> p (f s)"), ps[:, 2 + b, 0:2 * CAP], ACT.Relu).then_inc(relued, 1)

        @block.vector
        def _(dve):
            for e in range(E):
                dve.wait_ge(out, e + 1)
                for k in range(2):
                    m = 2 * e + k
                    ins = dve.tensor_scalar(ye[0:HALF, m, :], ps[0:HALF, 4 + e % 2, k * D:(k + 1) * D], ge[0:HALF, m, e:e + 1], None, ALU.mult)
                ins.then_inc(scaled, 1)


B1, SEG, DH = 4, 32, 64
NSEG = S // SEG
PER = 4
BG = NB // B1
PAIRS = H // 2
VE = DH + 1
QMAX = 448.0
Q_ROUND = 1.5 * 2.0 ** 20
Q_LEAST = 2.0 ** -6


def quantize(dve, link, dst, src, scale, tmp, mag):
    link(dve.tensor_scalar(tmp, src, scale, None, ALU.mult))
    link(dve.tensor_scalar(mag.bitcast(I32), tmp.bitcast(I32), 0x7F800000, None, ALU.bitwise_and))
    link(dve.tensor_scalar(mag, mag, Q_LEAST, Q_ROUND, ALU.max, ALU.mult))
    link(dve.tensor_tensor(tmp, tmp, mag, ALU.add))
    return dve.tensor_tensor(dst, tmp, mag, ALU.subtract)


def scale_factors(nc, c, V):
    with ExitStack() as ctx:
        sb = lambda n, s, d=F32: ctx.enter_context(nc.sbuf_tensor("sf_" + n, s, d))
        sem = lambda n: ctx.enter_context(nc.semaphore(n))
        NL = 4
        h = sb("h", [P, 2, NT // NL, D])
        st, mv = sb("st", [P, NT // NL, 6]), sb("mv", [P, NT // NL, 2])
        ve, rstd = sb("ve", [P, NT // NL]), sb("rstd", [P, NT // NL])
        half = sb("half", [P, NT // NL])
        lohi, am = sb("lohi", [P, 2, NT // NL]), sb("am", [P, NL, 2])
        top = sb("top", [P, 2])
        row, mrow, srow = sb("row", [2, P]), sb("mrow", [2, 1]), sb("srow", [2, 1])
        dia = sb("dia", [2, 2])
        ones2 = sb("ones2", [2, P])
        w, wT, tmp, mag = sb("w", [P, D]), sb("wT", [P, D]), sb("tmp", [P, D]), sb("mag", [P, D])
        beta = sb("beta", [P, H])
        ps = ctx.enter_context(nc.psum_tensor("sf_ps", [P, 8, 512], F32))
        s_w, s_h = sem("sf_w"), [sem("sf_h0"), sem("sf_h1")]
        step, stat, fact, used = sem("sf_step"), sem("sf_stat"), sem("sf_fact"), sem("sf_used")
        pe_s, act_s, halves = sem("sf_pe"), sem("sf_act"), sem("sf_halves")
        loads = [(V["wqkv"][:], c["w1qkv"]), (V["wout"][:], c["wout"].rearrange("(j p) d -> p j d", p=P)),
                 (V["g"][:], c["ln_g"]), (V["b"][:], c["ln_b"]), (V["bias"][:], c["bias"]), (beta[:], c["beta"]),
                 (V["ident"][:], c["ident"]), (V["cos"][:], c["cos1"]), (V["sin"][:], c["sin1"]), (V["mask"][:], c["mask1"]),
                 (w[:], c["wffn"])]
        block = ctx.enter_context(nc.Block())
        h_all = c["h_d"].rearrange("b (k p) d -> p (b k) d", p=P)
        K = NT // NL

        @block.sync
        def _(sp):
            for n in range(NL):
                if n >= 2:
                    sp.wait_ge(used, n - 1)
                sp.dma_start(h[:, n % 2], h_all[:, n * K:(n + 1) * K, :]).then_inc(s_h[n % 2], 16)
                if n == 1:
                    for dst, src in loads:
                        sp.dma_start(dst, src).then_inc(s_w, 16)

        @block.gpsimd
        def _(pool):
            pool.memset(half[:], -0.5).then_inc(halves, 1)
            pool.memset(V["mhalf"][:], -0.5)
            pool.memset(V["uu"][:], 1.0)
            pool.memset(V["mem"][:], 0.0).then_inc(halves, 1)
            pool.wait_ge(halves, 2)
            pool.memset(V["mem"][0:DH, :, :, DH:VE], 1e-6).then_inc(halves, 1)
            pool.wait_ge(halves, 3)
            pool.memset(V["mem"][DH:P, :, :, VE + DH:2 * VE], 1e-6).then_inc(halves, 1)
            pool.wait_ge(halves, 4)
            for n in range(NL):
                pool.wait_ge(stat, n + 1)
                pool.tensor_tensor(rstd[:], ve[:], half[:], ALU.pow).then_inc(fact, 1)

        @block.scalar
        def _(act):
            act.wait_ge(s_w, 16 * len(loads))
            act.activation(V["beta"][:], beta[:], ACT.Exp, scale=-1.0).then_inc(act_s, 1)

        @block.tensor
        def _(pe):
            pe.wait_ge(s_w, 16 * len(loads))
            pe.transpose(ps[:, 0, 0:D], w[:], V["ident"][:]).then_inc(pe_s, 1)
            pe.wait_ge(used, NL + 1)
            pe.transpose(ps[0:2, 1, 0:P], top[:], V["ident"][:]).then_inc(pe_s, 1)
            pe.wait_ge(used, NL + 2)
            pe.matmul(ps[:, 2, 0:2], ones2[:], dia[:], start=True, stop=True).then_inc(pe_s, 1)

        @block.vector
        def _(dve):
            n_ = [0]

            def link(ins):
                n_[0] += 1
                ins.then_inc(step, 1)
                dve.wait_ge(step, n_[0])

            for n in range(NL):
                dve.wait_ge(s_h[n % 2], 16 * (n // 2 + 1))
                for j in range(K):
                    ins = dve.bn_stats(st[:, j], h[:, n % 2, j])
                link(ins)
                for j in range(K):
                    ins = dve.bn_aggr(mv[:, j], st[:, j])
                link(ins)
                dve.tensor_scalar(ve[:], mv[:, :, 1], 1e-5, None, ALU.add).then_inc(stat, 1)
                dve.tensor_reduce(lohi[:, 0], h[:, n % 2], AX.X, ALU.min)
                link(dve.tensor_reduce(lohi[:, 1], h[:, n % 2], AX.X, ALU.max))
                link(dve.tensor_tensor(lohi[:], lohi[:], mv[:, :, 0].unsqueeze(1).broadcast_to([P, 2, K]), ALU.subtract))
                dve.wait_ge(fact, n + 1)
                link(dve.tensor_tensor(lohi[:], lohi[:], rstd[:].unsqueeze(1).broadcast_to([P, 2, K]), ALU.mult))
                dve.tensor_reduce(am[:, n, 0:1], lohi[:], AX.XY, ALU.max)
                dve.tensor_reduce(am[:, n, 1:2], lohi[:], AX.XY, ALU.min).then_inc(used, 1)
            dve.wait_ge(used, NL)
            link(dve.tensor_scalar(am[:, :, 1], am[:, :, 1], -1.0, None, ALU.mult))
            dve.tensor_reduce(top[:, 0:1], am[:], AX.XY, ALU.max)
            dve.wait_ge(s_w, 16 * len(loads))
            dve.memset(ones2[:], 1.0)
            dve.tensor_reduce(top[:, 1:2], w[:], AX.X, ALU.max, apply_absolute_value=True).then_inc(used, 1)
            link(dve.tensor_copy(V["ident_bf"][:], V["ident"][:]))
            dve.wait_ge(pe_s, 1)
            link(dve.tensor_copy(wT[:], ps[:, 0, 0:D]))
            dve.wait_ge(act_s, 1)
            link(dve.tensor_scalar(V["beta"][:], V["beta"][:], 1.0, None, ALU.add))
            link(dve.reciprocal(V["beta"][:], V["beta"][:]))
            link(dve.tensor_scalar(V["rest"][:], V["beta"][:], -1.0, 1.0, ALU.mult, ALU.add))
            dve.wait_ge(pe_s, 2)
            link(dve.tensor_reduce(mrow[:], ps[0:2, 1, 0:P], AX.X, ALU.max))
            link(dve.tensor_scalar(mrow[:], mrow[:], 1e-12, None, ALU.max))
            link(dve.reciprocal(srow[:], mrow[:]))
            link(dve.tensor_scalar(srow[:], srow[:], QMAX, None, ALU.mult))
            dve.tensor_scalar(dia[:], V["ident"][0:2, 0:2], srow[:, 0:1], None, ALU.mult).then_inc(used, 1)
            dve.wait_ge(pe_s, 3)
            link(dve.tensor_copy(V["qs"][:, 0:2], ps[:, 2, 0:2]))
            link(dve.reciprocal(V["qs"][:, 2:4], V["qs"][:, 0:2]))
            link(dve.tensor_tensor(V["qs"][:, 4:5], V["qs"][:, 2:3], V["qs"][:, 3:4], ALU.mult))
            link(quantize(dve, link, V["wq"][:], wT[:], V["qs"][:, 1:2], tmp[:], mag[:]))


def scan(nc, c, V, out, nseg):
    with ExitStack() as ctx:
        sb = lambda n, s, d=F32: ctx.enter_context(nc.sbuf_tensor("sc_" + n, s, d))
        sems = []

        def sem(n):
            sems.append(ctx.enter_context(nc.semaphore("sc_" + n)))
            return sems[-1]

        ht, xn, xnn = sb("ht", [P, 2, BG, D]), sb("xn", [P, BG, D]), sb("xnn", [P, BG, D])
        y, hb = sb("y", [P, 2, BG, D]), sb("hb", [P, 2, BG, D])
        st, mv, sc = sb("st", [P, BG, 6]), sb("mv", [P, BG, 2]), sb("sc", [P, 4, BG])
        tq, mq, xq = sb("tq", [P, BG, D]), sb("mq", [P, BG, D]), sb("xq", [P, BG, D], BF16)
        xT, xqT = sb("xT", [P, 2, S]), sb("xqT", [P, 2, S], BF16)
        uu = V["uu"]
        sig = [sb("sq", [P, 4, S]), sb("sk", [P, 4, S])]
        skN = sb("skN", [P, 4, BG, P])
        ol = sb("ol", [P, 4, BG, 2, DH])
        ee, relu = sb("ee", [P, 2, S]), sb("relu", [P, 2, S])
        ra, rb = sb("ra", [P, 2, S]), sb("rb", [P, 2, S])
        rot = [sb("qr", [P, 2, S]), sb("kr", [P, 2, S])]
        GH = 2 * BG
        ss, pT = sb("ss", [P, 2, GH, SEG]), sb("pT", [P, 4, GH, SEG])
        mx, sm = sb("mx", [P, GH]), sb("sm", [P, 4, GH])
        rk, rq = sb("rk", [P, GH]), sb("rq", [P, GH])
        t1, t2 = sb("t1", [P, 2, GH, DH]), sb("t2", [P, 2, GH, DH])
        oT = sb("oT", [P, 2, S])
        ps = ctx.enter_context(nc.psum_tensor("sc_ps", [P, 8, 512], F32))
        names = ("h_in0 h_in1 stat fact xn_d xnn_d xq_d step xt xt_c xqt xqt_c hb_d ffn ffn_c vp v_c pj ex mn rp sn sg add_d sS skt skc "
                 "smask sx se pt pvd old kr_s qr_s kd ud qd od up mu ott otc oproj ydone stored0 stored1").split()
        G = {n: sem(n) for n in names}
        h_seg = c["h_d"].rearrange("(g f) (s i) d -> f s i g d", f=B1, i=SEG)
        o_seg = out.rearrange("(g f) (s i) d -> f s i g d", f=B1, i=SEG)

        def wait(eng, name, n):
            if n > 0:
                eng.wait_ge(G[name], n)

        flat = lambda ap: ap.rearrange("p g d -> p (g d)")
        by_pos = lambda ap: ap.rearrange("p (n i) -> p n i", i=SEG)
        table = lambda name, q: V[name][:, q].unsqueeze(1).broadcast_to([P, S // SEG, SEG])

        def linker(eng):
            count = [0]

            def link(ins):
                count[0] += 1
                ins.then_inc(G["step"], 1)
                eng.wait_ge(G["step"], count[0])
            return link


        def load(sp, seg, j):
            for f in range(B1):
                sp.dma_start(ht[32 * f:32 * f + 32, j % 2], h_seg[f, bass.ds(seg, 1)].rearrange("o i g d -> (o i) g d")).then_inc(G[f"h_in{j % 2}"], 16)

        def wait_h(eng, j):
            wait(eng, f"h_in{j % 2}", 64 * max(1, (j + 1) // 2))

        def moments(dve, link, j, n, k):
            src = (ht[:, j % 2], xn)[k]
            if k == 0:
                wait_h(dve, j)
            else:
                wait(dve, "xn_d", n)
            for g in range(BG):
                ins = dve.bn_stats(st[:, g], src[:, g])
            link(ins)
            for g in range(BG):
                ins = dve.bn_aggr(mv[:, g], st[:, g])
            link(ins)
            dve.tensor_scalar(sc[:, 2 * k], mv[:, :, 1], 1e-5, None, ALU.add).then_inc(G["stat"], 1)

        def root(pool, n, k):
            wait(pool, "stat", 2 * (n - 1) + k + 1)
            pool.tensor_tensor(sc[:, 2 * k + 1], sc[:, 2 * k], V["mhalf"][:, 0:BG], ALU.pow).then_inc(G["fact"], 1)

        def normalize(dve, j, n, k):
            dst, src = (xn, xnn)[k], (ht[:, j % 2], xn)[k]
            wait(dve, "fact", 2 * (n - 1) + k + 1)
            wait(dve, "xt", n - 1)
            for g in range(BG):
                ins = dve.tensor_scalar(dst[:, g], src[:, g], mv[:, g, 0:1], sc[:, 2 * k + 1, g:g + 1], ALU.subtract, ALU.mult)
            ins.then_inc(G[("xn_d", "xnn_d")[k]], 1)

        def add_bias(pool, j):
            wait_h(pool, j)
            pool.tensor_tensor(hb[:, j % 2], ht[:, j % 2], V["bias"][:].unsqueeze(1).broadcast_to([P, BG, D]), ALU.add).then_inc(G["hb_d"], 1)

        def round_fp8(dve, link, n):
            wait(dve, "xqt", n - 1)
            quantize(dve, link, flat(xq[:]), flat(xn[:]), V["qs"][:, 0:1], flat(tq[:]), flat(mq[:])).then_inc(G["xq_d"], 1)

        def turn_x(pe, bank, n):
            wait(pe, "xnn_d", n)
            for g in range(BG):
                ins = pe.transpose(ps[:, bank, g * P:(g + 1) * P], xnn[:, g], V["ident"][:])
            ins.then_inc(G["xt"], 1)

        def turn_xq(pe, bank, n):
            wait(pe, "xq_d", n)
            for g in range(BG):
                ins = pe.transpose(ps[:, bank, 0:256].bitcast(BF16)[:, g * P:(g + 1) * P], xq[:, g], V["ident_bf"][:])
            ins.then_inc(G["xqt"], 1)

        def take_x(act, bank, j, n):
            wait(act, "xt", n)
            act.activation(xT[:, j % 2], ps[:, bank, :], ACT.Identity, bias=V["b"][:, 0:1], scale=V["g"][:, 0:1]).then_inc(G["xt_c"], 1)

        def take_xq(act, bank, j, n):
            wait(act, "xqt", n)
            act.copy(xqT[:, j % 2], ps[:, bank, 0:256].bitcast(BF16)).then_inc(G["xqt_c"], 1)

        def prepare(seg):
            with nc.Block() as block:

                @block.sync
                def _(sp):
                    load(sp, seg, 0)

                @block.vector
                def _(dve):
                    link = linker(dve)
                    for k in range(2):
                        moments(dve, link, 0, 1, k)
                        normalize(dve, 0, 1, k)
                    round_fp8(dve, link, 1)

                @block.gpsimd
                def _(pool):
                    for k in range(2):
                        root(pool, 1, k)
                    add_bias(pool, 0)

                @block.tensor
                def _(pe):
                    turn_x(pe, 0, 1)
                    turn_xq(pe, 1, 1)

                @block.scalar
                def _(act):
                    take_x(act, 0, 0, 1)
                    take_xq(act, 1, 0, 1)

        PT = PER * PAIRS
        STEPS = PT + 4
        inside = lambda p: 0 <= p < PT
        starts = range(0, PT, PAIRS)

        def turn(seg, more):
            readied = {j: PAIRS * (j - 1) for j in range(1, PER + (1 if more else 0))}
            at_step = lambda s, off: [j for j, first in readied.items() if s == first + off]
            users, freed = {}, []

            def user(key, name, count):
                users[key] = len(freed)
                freed.append((name, count))

            for s in range(STEPS):
                if s < PT:
                    user(("q", s), "rp", 2 * s + 1)
                    user(("v", s), "v_c", s + 1)
                    user(("k", s), "rp", 2 * s + 2)
                for j in at_step(s, 5):
                    user(("x", j), "xt_c", j)
                for j in at_step(s, 6):
                    user(("xq", j), "xqt_c", j)
                if s - 7 in starts:
                    user(("ffn", (s - 7) // PAIRS), "ffn_c", (s - 7) // PAIRS + 1)
            bank_of = lambda *key: users[key] % 2

            def free_bank(pe, *key):
                if users[key] >= 2:
                    wait(pe, *freed[users[key] - 2])

            with nc.Block() as block:

                @block.sync
                def _(sp):
                    for j in sorted(readied)[:2]:
                        load(sp, seg + j, j)
                    for j in range(PER):
                        wait(sp, "ydone", j + 1)
                        for f in range(B1):
                            sp.dma_start(o_seg[f, bass.ds(seg + j, 1)].rearrange("o i g d -> (o i) g d"), y[32 * f:32 * f + 32, j % 2]).then_inc(G[f"stored{j % 2}"], 16)
                        if j + 3 in readied:
                            wait(sp, "xn_d", j + 1)
                            wait(sp, "hb_d", j + 1)
                            load(sp, seg + j + 3, j + 3)
                    for k in range(2):
                        wait(sp, f"stored{k}", 64 * (PER // 2))

                @block.gpsimd
                def _(pool):
                    def features(n):
                        p, which = divmod(n, 2)
                        wait(pool, "mn", n + 1)
                        wait(pool, "qr_s", p - 3)
                        wait(pool, "skt", p - 3)
                        pool.tensor_tensor(sig[which][:, p % 4], ee[:, n % 2], relu[:, n % 2], ALU.add).then_inc(G["sg"], 1)
                        wait(pool, "rp", n + 1)
                        pool.tensor_tensor(by_pos(rb[:, n % 2]), by_pos(rb[:, n % 2]), table("sin", which), ALU.mult).then_inc(G["sn"], 1)
                        wait(pool, "sn", n + 1)
                        wait(pool, "sS", p - 1)
                        pool.tensor_tensor(rot[which][:, p % 2], ra[:, n % 2], rb[:, n % 2], ALU.add).then_inc(G["add_d"], 1)

                    for s in range(STEPS):
                        p = s - 2
                        if s < PT:
                            features(2 * s)
                        if inside(p):
                            new = uu[:, p % PAIRS, :, :, 0:DH]
                            wait(pool, "kd", p + 1)
                            wait(pool, "pvd", p + 1)
                            pool.tensor_tensor(new, new, t1[:, p % 2].rearrange("p (g h) d -> p g h d", h=2), ALU.subtract).then_inc(G["ud"], 1)
                        if s < PT:
                            features(2 * s + 1)
                        if inside(p):
                            wait(pool, "qd", p + 1)
                            wait(pool, "old", p + 1)
                            o = ol[:, p % 4].rearrange("p g h d -> p (g h d)")
                            pool.tensor_tensor(o, o, t2[:, p % 2].rearrange("p c d -> p (c d)"), ALU.add).then_inc(G["od"], 1)
                        for j in at_step(s, 1):
                            root(pool, j, 0)
                        for j in at_step(s, 3):
                            root(pool, j, 1)
                            wait(pool, "ffn_c", j - 1)
                            add_bias(pool, j)

                @block.tensor
                def _(pe):
                    def project(n):
                        p, which = divmod(n, 2)
                        free_bank(pe, "qk"[which], p)
                        col = 1024 * which + p % PAIRS * P
                        pe.matmul(ps[:, bank_of("qk"[which], p), :], V["wqkv"][:, col:col + P], xT[:, p // PAIRS % 2], start=True, stop=True).then_inc(G["pj"], 1)

                    def values(p):
                        free_bank(pe, "v", p)
                        col = 2048 + p % PAIRS * P
                        for g in range(BG):
                            ins = pe.matmul(ps[:, bank_of("v", p), g * P:(g + 1) * P], xT[:, p // PAIRS % 2, g * P:(g + 1) * P], V["wqkv"][:, col:col + P],
                                            start=True, stop=True)
                        ins.then_inc(G["vp"], 1)

                    def recall(p, which, done):
                        for g in range(BG):
                            for f in range(B1):
                                at_ = g * P + 32 * f
                                ins = pe.matmul(ps[32 * f:32 * f + 32, 2 + g // 2, (g % 2) * 2 * VE:(g % 2 + 1) * 2 * VE],
                                                sig[which][:, p % 4, at_:at_ + 32], V["mem"][:, p % PAIRS, 4 * g + f, :], start=True, stop=True)
                        ins.then_inc(G[done], 1)

                    def update(p, fs):
                        for f in fs:
                            for g in range(BG):
                                for hh in range(2):
                                    ins = pe.matmul(ps[64 * hh:64 * hh + 64, 4 + f % 2, g * VE:(g + 1) * VE],
                                                    skN[32 * f:32 * f + 32, p % 4, g, 64 * hh:64 * hh + 64],
                                                    uu[32 * f:32 * f + 32, p % PAIRS, g, hh, :], start=True, stop=True)
                        ins.then_inc(G["up"], 1)

                    for s in range(STEPS):
                        if s < PT:
                            if s in starts:
                                wait(pe, "xt_c", s // PAIRS)
                            project(2 * s)
                            values(s)
                        p = s - 2
                        if inside(p):
                            wait(pe, "sg", 2 * p + 2)
                            wait(pe, "v_c", p + 1)
                            wait(pe, "qd", p)
                            wait(pe, "mu", 2 * (p - PAIRS + 1))
                            recall(p, 1, "kr_s")
                            wait(pe, "pt", p + 1)
                            wait(pe, "skc", p + 1)
                            wait(pe, "otc", p - 1)
                            for g in range(BG):
                                for hh in range(2):
                                    for f in range(B1):
                                        ch = 2 * g + hh
                                        ins = pe.matmul(ps[32 * f:32 * f + 32, 6, ch * DH:(ch + 1) * DH], pT[32 * f:32 * f + 32, p % 4, ch, :],
                                                        uu[32 * f:32 * f + 32, p % PAIRS, g, hh, 0:DH], start=True, stop=True)
                            ins.then_inc(G["pvd"], 1)
                        p = s - 1
                        if inside(p):
                            wait(pe, "add_d", 2 * p + 2)
                            wait(pe, "mu", 2 * (s - 3))
                            for hh in range(2):
                                for g in range(BG):
                                    for f in range(B1):
                                        cols = slice(g * P + 32 * f, g * P + 32 * f + 32)
                                        ins = pe.matmul(ps[32 * f:32 * f + 32, 4 + hh, g * SEG:(g + 1) * SEG],
                                                        rot[0][64 * hh:64 * hh + 64, p % 2, cols], rot[1][64 * hh:64 * hh + 64, p % 2, cols],
                                                        start=True, stop=True)
                            ins.then_inc(G["sS"], 1)
                        if s < PT:
                            project(2 * s + 1)
                        p = s - 2
                        if inside(p):
                            wait(pe, "kd", p + 1)
                            recall(p, 0, "qr_s")
                        p = s - 1
                        if inside(p):
                            wait(pe, "sg", 2 * p + 2)
                            wait(pe, "old", p)
                            for g in range(BG):
                                ins = pe.transpose(ps[:, 6, g * P:(g + 1) * P], sig[1][:, p % 4, g * P:(g + 1) * P], V["ident"][:])
                            ins.then_inc(G["skt"], 1)
                        p = s - 3
                        if inside(p):
                            wait(pe, "ud", p + 1)
                            wait(pe, "skc", p + 1)
                            wait(pe, "smask", min(s, PT))
                            wait(pe, "mu", 2 * p)
                            update(p, (0, 1))
                            wait(pe, "od", p + 1)
                            wait(pe, "skc", min(s, PT))
                            wait(pe, "old", min(p + 2, PT))
                            wait(pe, "otc", p)
                            for g in range(BG):
                                ins = pe.transpose(ps[:, 6, g * P:(g + 1) * P], ol[:, p % 4, g].rearrange("p h d -> p (h d)"), V["ident"][:])
                            ins.then_inc(G["ott"], 1)
                        p = s - 4
                        if inside(p):
                            h = p % PAIRS
                            wait(pe, "otc", p + 1)
                            if h == 0:
                                wait(pe, "ydone", p // PAIRS)
                            for g in range(BG):
                                ins = pe.matmul(ps[:, 7, g * P:(g + 1) * P], oT[:, p % 2, g * P:(g + 1) * P], V["wout"][:, h],
                                                start=(h == 0 and g == 0), stop=(h == PAIRS - 1 and g == BG - 1))
                            ins.then_inc(G["oproj"], 1)
                        p = s - 3
                        if inside(p):
                            wait(pe, "mu", 2 * p + 1)
                            update(p, (2, 3))
                        for j in at_step(s, 5):
                            free_bank(pe, "x", j)
                            turn_x(pe, bank_of("x", j), j)
                        for j in at_step(s, 6):
                            free_bank(pe, "xq", j)
                            turn_xq(pe, bank_of("xq", j), j)
                        if s - 7 in starts:
                            j = (s - 7) // PAIRS
                            free_bank(pe, "ffn", j)
                            wait(pe, "xqt_c", j)
                            for g in range(BG):
                                ins = pe.matmul(ps[:, bank_of("ffn", j), g * P:(g + 1) * P], xqT[:, j % 2, g * P:(g + 1) * P], V["wq"][:], start=True, stop=True)
                            ins.then_inc(G["ffn"], 1)

                @block.scalar
                def _(act):
                    def features(n):
                        x = ps[:, bank_of("qk"[n % 2], n // 2), :]
                        wait(act, "pj", n + 1)
                        wait(act, "sg", n - 1)
                        act.activation(ee[:, n % 2], x, ACT.Relu, scale=-1.0)
                        act.activation(relu[:, n % 2], x, ACT.Relu).then_inc(G["ex"], 1)
                        wait(act, "ex", n + 1)
                        act.activation(ee[:, n % 2], ee[:, n % 2], ACT.Exp, scale=-1.0).then_inc(G["mn"], 1)

                    for s in range(STEPS):
                        if s < PT:
                            features(2 * s)
                            wait(act, "vp", s + 1)
                            wait(act, "up", 2 * (s - PAIRS + 1))
                            act.copy(uu[:, s % PAIRS, :, :, 0:DH], ps[:, bank_of("v", s), :].rearrange("p (g h d) -> p g h d", h=2, d=DH)).then_inc(G["v_c"], 1)
                            features(2 * s + 1)
                        p = s - 1
                        if inside(p):
                            wait(act, "sx", p + 1)
                            act.activation(ss[:, p % 2], ss[:, p % 2], ACT.Exp).then_inc(G["se"], 1)
                            wait(act, "skt", p + 1)
                            wait(act, "up", 2 * (p - 3))
                            act.copy(skN[:, p % 4].rearrange("p g r -> p (g r)"), ps[:, 6, :]).then_inc(G["skc"], 1)
                        p = s - 3
                        if inside(p):
                            wait(act, "ott", p + 1)
                            wait(act, "oproj", p - 1)
                            act.copy(oT[:, p % 2], ps[:, 6, :]).then_inc(G["otc"], 1)
                        for j in at_step(s, 5):
                            take_x(act, bank_of("x", j), j, j)
                        for j in at_step(s, 6):
                            take_xq(act, bank_of("xq", j), j, j)

                @block.vector
                def _(dve):
                    link = linker(dve)

                    def rope(n):
                        x = ps[:, bank_of("qk"[n % 2], n // 2), :]
                        wait(dve, "ex", n + 1)
                        wait(dve, "add_d", n - 1)
                        dve.stream_shuffle(rb[:, n % 2], x, [lane ^ 1 for lane in range(32)])
                        dve.tensor_tensor(by_pos(ra[:, n % 2]), by_pos(x), table("cos", n % 2), ALU.mult).then_inc(G["rp"], 1)

                    recalled = ps[:, 2:4, 0:4 * VE].rearrange("p b (c v) -> p b c v", v=VE)
                    by_bank = lambda ap: ap.rearrange("p (b c) d -> p b c d", b=2)

                    def update(p, k):
                        wait(dve, "up", 2 * p + k + 1)
                        for hh in range(2):
                            rows = slice(64 * hh, 64 * hh + 64)
                            m = V["mem"][rows, p % PAIRS].rearrange("p (g f) v -> p f g v", f=B1)[:, 2 * k:2 * k + 2, :, hh * VE:(hh + 1) * VE]
                            ins = dve.tensor_tensor(m, m, ps[rows, 4:6, 0:BG * VE].rearrange("p b (g v) -> p b g v", g=BG), ALU.add)
                        ins.then_inc(G["mu"], 1)

                    def share(name, p):
                        h = p % PAIRS
                        return V[name][:, 2 * h:2 * h + 2].unsqueeze(1).broadcast_to([P, BG, 2])

                    for s in range(STEPS):
                        if s < PT:
                            rope(2 * s)
                        p = s - 2
                        if inside(p):
                            wait(dve, "kr_s", p + 1)
                            link(dve.reciprocal(rk[:].rearrange("p (b c) -> p b c", b=2), recalled[:, :, :, DH]))
                            wait(dve, "ud", p - 1)
                            dve.tensor_tensor(by_bank(t1[:, p % 2]), recalled[:, :, :, 0:DH],
                                              bc(rk[:].rearrange("p (b c) -> p b c", b=2), DH), ALU.mult).then_inc(G["kd"], 1)
                            wait(dve, "pvd", p + 1)
                            wait(dve, "pt", p + 1)
                            wait(dve, "ott", p - 3)
                            dve.tensor_tensor(ol[:, p % 4].rearrange("p g h d -> p (g h) d"), ps[:, 6, :].rearrange("p (c d) -> p c d", d=DH),
                                              bc(sm[:, p % 4], DH), ALU.mult).then_inc(G["old"], 1)
                        p = s - 1
                        if inside(p):
                            wait(dve, "sS", p + 1)
                            by_head = ss[:, p % 2].rearrange("p (g h) j -> p h g j", h=2)
                            dve.tensor_tensor(by_head, ps[:, 4:6, 0:P].rearrange("p b (g j) -> p b g j", j=SEG),
                                              V["mask"][:].unsqueeze(1).unsqueeze(1).broadcast_to([P, 2, BG, SEG]), ALU.add).then_inc(G["smask"], 1)
                            wait(dve, "smask", p + 1)
                            link(dve.tensor_reduce(mx[:], ss[:, p % 2], AX.X, ALU.max))
                            dve.tensor_tensor(ss[:, p % 2], ss[:, p % 2], bc(mx[:], SEG), ALU.subtract).then_inc(G["sx"], 1)
                        if s < PT:
                            rope(2 * s + 1)
                        p = s - 2
                        if inside(p):
                            wait(dve, "qr_s", p + 1)
                            r = rq[:].rearrange("p (b c) -> p b c", b=2)
                            link(dve.tensor_scalar(r, recalled[:, :, :, DH], 1e-6, None, ALU.add))
                            link(dve.reciprocal(rq[:], rq[:]))
                            pairs = rq[:].rearrange("p (g h) -> p g h", h=2)
                            link(dve.tensor_tensor(pairs, pairs, share("beta", p), ALU.mult))
                            wait(dve, "od", p - 1)
                            dve.tensor_tensor(by_bank(t2[:, p % 2]), recalled[:, :, :, 0:DH], bc(r, DH), ALU.mult).then_inc(G["qd"], 1)
                        p = s - 3
                        if inside(p):
                            update(p, 0)
                        p = s - 1
                        if inside(p):
                            wait(dve, "se", p + 1)
                            dve.transpose(pT[:, p % 4].rearrange("p c j -> p (c j)"), ss[:, p % 2].rearrange("p c j -> p (c j)"))
                            s_ = sm[:, p % 4]
                            link(dve.tensor_reduce(s_, ss[:, p % 2], AX.X, ALU.add))
                            link(dve.reciprocal(s_, s_))
                            pairs = s_.rearrange("p (g h) -> p g h", h=2)
                            dve.tensor_tensor(pairs, pairs, share("rest", p), ALU.mult).then_inc(G["pt"], 1)
                        p = s - 3
                        if inside(p):
                            update(p, 1)
                        for k in range(2):
                            for j in at_step(s, 2 * k + 1):
                                moments(dve, link, j, j, k)
                            for j in at_step(s, 2 * k + 2):
                                normalize(dve, j, j, k)
                        for j in at_step(s, 5):
                            round_fp8(dve, link, j)
                        if s - 7 in starts:
                            j = (s - 7) // PAIRS
                            wait(dve, "ffn", j + 1)
                            wait(dve, "hb_d", j)
                            wait(dve, f"stored{j % 2}", 64 * (j // 2))
                            dve.scalar_tensor_tensor(flat(y[:, j % 2]), ps[:, bank_of("ffn", j), :], V["qs"][:, 4:5], flat(hb[:, j % 2]),
                                                     ALU.mult, ALU.add).then_inc(G["ffn_c"], 1)
                        p = s - 4
                        if inside(p) and p % PAIRS == PAIRS - 1:
                            j = p // PAIRS
                            wait(dve, "oproj", p + 1)
                            wait(dve, "ffn_c", j + 1)
                            dve.tensor_tensor(flat(y[:, j % 2]), flat(y[:, j % 2]), ps[:, 7, :], ALU.add).then_inc(G["ydone"], 1)

        clear(nc, sems)
        prepare(0)
        if nseg > PER:
            with nc.Fori(0, nseg // PER - 1) as i:
                clear(nc, sems)
                turn(i * PER, True)
        clear(nc, sems)
        turn(nseg - PER, False)


def block1_tensors(nc, ctx):
    sb = lambda n, s, d=F32: ctx.enter_context(nc.sbuf_tensor("v_" + n, s, d))
    shapes = dict(wqkv=[P, 3072], wout=[P, PAIRS, D], g=[P, 1], b=[P, 1], bias=[P, D], beta=[P, H], rest=[P, H],
                  ident=[P, P], cos=[P, 2, SEG], sin=[P, 2, SEG], mask=[P, SEG], qs=[P, 5], mem=[P, PAIRS, NB, 2 * VE],
                  uu=[P, PAIRS, BG, 2, VE], mhalf=[P, BG])
    V = {n: sb(n, s) for n, s in shapes.items()}
    V["wq"], V["ident_bf"] = sb("wq", [P, D], BF16), sb("ident_bf", [P, P], BF16)
    return V


def weights(nc, ctx):
    sb = lambda n, s, d=F32: ctx.enter_context(nc.sbuf_tensor("w_" + n, s, d))
    shapes = dict(wqA=[P, D], mk=[P, D], mv=[P, D], woA=[P, D], woB=[P, D], wB=[P, 5 * D], ident=[P, P],
                  decay=[P, NC, S], cmask=[P, S], hsum=[P, H], g2b=[P, D], wr=[P, E], mhalf=[P, 2 * NC],
                  nmax=[H, 2 * NB])
    W = {n: sb(n, s) for n, s in shapes.items()}
    W["ident_bf"], W["cmaskT"], W["flag"] = sb("ident_bf", [P, P], BF16), sb("cmaskT", [P, P], BF16), sb("flag", [1, 1], I32)
    return W


def shape_constants():
    f32 = np.float32
    pos = np.arange(S, dtype=f32)
    d = np.exp(f32(-0.01 * 0.01) * np.abs(pos[:, None] - pos[None, :])).astype(f32)
    decay = d.reshape(NC, P, S).transpose(1, 0, 2).copy()
    cmask = np.zeros((P, S), f32)
    cmask[:, S - P:] = np.where(np.arange(P)[None, :] <= np.arange(P)[:, None], 0.0, MASKED)
    hsum = (np.arange(P)[:, None] % H == np.arange(H)[None, :]).astype(f32)
    cmaskT = np.where(np.arange(P)[:, None] <= np.arange(P)[None, :], 0.0, MASKED).astype(f32)
    theta = (f32(10000.0) ** (f32(-2.0) * (np.arange(HD // 2, dtype=f32) / HD))).astype(f32)
    ang = (pos[:, None] * theta[None, :]).astype(f32)
    feature = np.arange(P) // H
    sign = np.where(feature % 2 == 0, -1.0, 1.0).astype(f32)
    cos, sin = np.cos(ang)[:, feature // 2].T, np.sin(ang)[:, feature // 2].T * sign[:, None]
    rope = np.stack([cos * f32(SCALE_B), sin * f32(SCALE_B), cos, sin], 1).astype(f32)
    seq = np.arange(P)
    low = np.broadcast_to((np.arange(E)[None, :] < np.arange(E)[:, None]).reshape(1, E * E), (P, E * E)).astype(f32)
    restart = np.broadcast_to((np.arange(E * NT) % NT != 0).astype(f32)[None], (P, E * NT)).copy()
    slots = np.broadcast_to((np.arange(E * CAP) % CAP).astype(f32)[None], (P, E * CAP)).copy()
    ptid = np.stack([np.broadcast_to(seq[:, None], (P, NT)), np.broadcast_to(np.arange(NT)[None], (P, NT))], 2)
    route = dict(low=low, before=(seq[:, None] < seq[None, :]).astype(f32), restart=restart, slots=slots,
                 ptid=ptid.reshape(P, 2 * NT).astype(f32), mix=np.array([[1, NT], [P, 1]], f32))
    freqs = f32(10000.0) ** (-np.arange(0, DH, 2, dtype=f32) / f32(DH))
    ang1 = (np.arange(SEG, dtype=f32)[:, None] * freqs[None, :]).astype(f32)
    row1, sign1 = (seq % DH) // 2, np.where(seq % 2 == 0, -1.0, 1.0).astype(f32)
    cos1 = np.cos(ang1)[:, row1].T.astype(f32)
    sin1 = (np.sin(ang1)[:, row1].T * sign1[:, None]).astype(f32)
    per_side = lambda t: np.stack([t * f32(DH ** -0.5), t], 1).copy()
    i, j = np.arange(P)[:, None] % SEG, np.arange(SEG)[None, :]
    scan = dict(cos1=per_side(cos1), sin1=per_side(sin1), mask1=np.where(j <= i, 0.0, MASKED).astype(f32))
    return dict(**route, **scan, ident=np.eye(P, dtype=f32), decay=decay, cmask=cmask,
                hsum=hsum, cmaskT=cmaskT, rope=rope)


def inputs_of(a):
    c = dict(
        x=a["L0_attn_x"], Wq=a["L0_attn_Wq"], Wk=a["L0_attn_Wk"], Wv=a["L0_attn_Wv"], WoA=a["L0_attn_Wo"],
        Wdown=a["L0_attn_W_down_kv"], Wuk=a["L0_attn_W_up_k"], Wuv=a["L0_attn_W_up_v"],
        g1=a["L0_ffn_g1"].reshape(P, 1), Wqkv=a["L0_ffn_w_qkv"], WoB=a["L0_ffn_w_o"],
        g2b=np.broadcast_to(a["L0_ffn_g2"].reshape(1, D), (P, D)), Wr=a["L0_ffn_w_router"], w1=a["L0_ffn_w1"], w2=a["L0_ffn_w2"],
        w1qkv=a["L1_attn_w_qkv"], wout=a["L1_attn_w_out"], ln_g=a["L1_attn_ln_g"].reshape(P, 1), ln_b=a["L1_attn_ln_b"].reshape(P, 1),
        beta=np.broadcast_to(a["L1_attn_mem_beta"].reshape(1, H), (P, H)), wffn=a["L1_ffn_weight"],
        bias=np.broadcast_to(a["L1_ffn_bias"].reshape(1, D), (P, D)))
    c.update(shape_constants())
    return c


def scratch(nc):
    shapes = dict(xn=((NB, S, D), F32), v=((NB * 2, P, NC * VW), F32), parts=((NB * 4, 5, P, S), BF16),
                  on=((NB * 2, P, NC * D), F32), x1=((NB, S, D), F32), h=((NB, S, D), F32), xf=((NB, S, D), F32),
                  pr=((P, NB, NC, E), F32), gate=((NT * P, E), F32))
    return {n + "_d": nc.dram_tensor(n + "_scratch", shape, dt, kind="Internal").ap() for n, (shape, dt) in shapes.items()}


def program(nc, c):
    c.update(scratch(nc))
    with ExitStack() as ctx:
        W = weights(nc, ctx)
        R = {"rows": ctx.enter_context(nc.sbuf_tensor("rows", [P, 2 * E, 2], U32))}
        fold_weights(nc, c, W)
        front(nc, c, W, NB)
        attend(nc, c, W, NB)
        tail(nc, c, W, NB)
        bound_flag(nc, W, NB)
        flag = nc.values_load(W["flag"][0:1, 0:1], min_val=0, max_val=1)
        with nc.If(flag > 0):
            attend_any(nc, c, W, NB)
        route(nc, c, W, R)
        experts(nc, c, W, R)
    with ExitStack() as ctx:
        V = block1_tensors(nc, ctx)
        scale_factors(nc, c, V)
        scan(nc, c, V, c["out"], NSEG)


def kernel(**inputs):
    import concourse.bacc as _bacc
    from concourse.bass_utils import run_bass_kernel_spmd as _run

    nc = _bacc.Bacc("TRN2", target_bir_lowering=False, num_devices=1)
    arrays, c = {}, {}
    for name, a in inputs_of({k: np.asarray(v) for k, v in inputs.items()}).items():
        a = np.ascontiguousarray(a)
        arrays["in_" + name] = a
        c[name] = nc.dram_tensor("in_" + name, a.shape, mybir.dt.from_np(a.dtype), kind="ExternalInput").ap()
    c["out"] = nc.dram_tensor("out_dram", (NB, S, D), F32, kind="ExternalOutput").ap()
    program(nc, c)
    return _run(nc, [arrays], core_ids=[0]).results[0]["out_dram"]
```
